# Optimizing a Trainium2 kernel written in Bass

```python
import numpy as np
import jax
import jax.numpy as jnp

def _softmax(x, axis=-1):
    return jax.nn.softmax(x, axis=axis)

def _gelu(x):
    return jax.nn.gelu(x, approximate=True)

def _silu(x):
    return jax.nn.silu(x)

def _sigmoid(x):
    return jax.nn.sigmoid(x)

def _layernorm(x, axis=-1, eps=1e-05):
    m = jnp.mean(x, axis=axis, keepdims=True)
    v = jnp.var(x, axis=axis, keepdims=True)
    return (x - m) / jnp.sqrt(v + eps)

def _scatter_add(tgt, idx, src, axis=0):
    return tgt.at[idx].add(src)

def _segment_sum(src, seg, n):
    return jax.ops.segment_sum(src, seg, n)
kernel_name = 'mk_gnn_ffn_d1_gnn_r8_21ac81'

def setup_inputs(seed: int=0):
    np.random.seed(seed)
    _w = jnp.asarray

    def _rec_inputs():
        import jax
        import jax.numpy as jnp
        _gk = jax.random.key(seed)
        x = -0.0003713 + 1 * jax.random.normal(jax.random.fold_in(_gk, 1), (6250, 256), jnp.float32)
        _s = jax.random.randint(jax.random.fold_in(_gk, 2), (100000,), 0, 6250, jnp.int32)
        _d = jax.random.randint(jax.random.fold_in(_gk, 3), (100000,), 0, 6250, jnp.int32)
        _loop = jnp.arange(6250, dtype=jnp.int32)
        src = jnp.concatenate([_s, _d, _loop])
        dst = jnp.concatenate([_d, _s, _loop])
        _o = jnp.argsort(dst, stable=True)
        src = src[_o]
        dst = dst[_o]
        return (x, src, dst)
    x, src, dst = _rec_inputs()

    def _L0_gnn_setup():
        import jax, jax.numpy as jnp
        import numpy as np
        N_NODES = 6250

        def _gcn_conv(x, W, b, src, dst, n):
            h = x @ W
            loop = jnp.arange(n, dtype=src.dtype)
            src_sl = jnp.concatenate([src, loop])
            dst_sl = jnp.concatenate([dst, loop])
            deg = jax.ops.segment_sum(jnp.ones_like(dst_sl, dtype=h.dtype), dst_sl, num_segments=n)
            dinv = jnp.where(deg > 0, jax.lax.rsqrt(deg), 0.0)
            norm = dinv[src_sl] * dinv[dst_sl]
            msgs = h[src_sl] * norm[:, None]
            out = jax.ops.segment_sum(msgs, dst_sl, num_segments=n)
            return out + b
        key = jax.random.key(seed)
        k0, k1, k2, k3 = jax.random.split(key, 4)
        d = 256
        E = 50000
        scale = 1.0 / np.sqrt(d)
        x = jax.random.normal(k0, (N_NODES, d), dtype=jnp.float32)
        edge_index = jax.random.randint(k1, (2, E), 0, N_NODES, dtype=jnp.int64)
        W1 = jax.random.normal(k2, (d, d), dtype=jnp.float32) * scale
        b1 = jnp.zeros((d,), dtype=jnp.float32)
        W2 = jax.random.normal(k3, (d, d), dtype=jnp.float32) * scale
        b2 = jnp.zeros((d,), dtype=jnp.float32)
        return {'x': x, 'edge_index': edge_index, 'W1': W1, 'b1': b1, 'W2': W2, 'b2': b2}
    _L0_gnn_all = _L0_gnn_setup()
    _L0_gnn_in = {k: v for k, v in _L0_gnn_all.items() if k in ('W1', 'b1', 'W2', 'b2')}
    del _L0_gnn_all

    def _L0_ffn_setup():
        import jax, jax.numpy as jnp
        import numpy as np
        TOP_K = 2
        LN_EPS = 1e-05
        key = jax.random.key(seed)
        ks = jax.random.split(key, 8)
        B, S, D, E, H = (16, 1024, 256, 8, 1024)
        x = jax.random.normal(ks[0], (B, S, D), dtype=jnp.float32)
        Wr = jax.random.normal(ks[1], (D, E), dtype=jnp.float32) * 0.1
        br = jnp.zeros((E,), dtype=jnp.float32)
        ln_g = jnp.ones((E, D), dtype=jnp.float32)
        ln_b = jnp.zeros((E, D), dtype=jnp.float32)
        W1 = jax.random.normal(ks[2], (E, D, H), dtype=jnp.float32) * (1.0 / np.sqrt(D))
        b1 = jnp.zeros((E, H), dtype=jnp.float32)
        W2 = jax.random.normal(ks[3], (E, H, D), dtype=jnp.float32) * (1.0 / np.sqrt(H))
        b2 = jnp.zeros((E, D), dtype=jnp.float32)
        return {'x': x, 'Wr': Wr, 'br': br, 'ln_g': ln_g, 'ln_b': ln_b, 'W1': W1, 'b1': b1, 'W2': W2, 'b2': b2}
    _L0_ffn_all = _L0_ffn_setup()
    _L0_ffn_in = {k: v for k, v in _L0_ffn_all.items() if k in ('Wr', 'br', 'ln_g', 'ln_b', 'W1', 'b1', 'W2', 'b2')}
    del _L0_ffn_all
    return {'x': x, 'src': src, 'dst': dst, 'L0_gnn_W1': _L0_gnn_in['W1'], 'L0_gnn_b1': _L0_gnn_in['b1'], 'L0_gnn_W2': _L0_gnn_in['W2'], 'L0_gnn_b2': _L0_gnn_in['b2'], 'L0_ffn_Wr': _L0_ffn_in['Wr'], 'L0_ffn_br': _L0_ffn_in['br'], 'L0_ffn_ln_g': _L0_ffn_in['ln_g'], 'L0_ffn_ln_b': _L0_ffn_in['ln_b'], 'L0_ffn_W1': _L0_ffn_in['W1'], 'L0_ffn_b1': _L0_ffn_in['b1'], 'L0_ffn_W2': _L0_ffn_in['W2'], 'L0_ffn_b2': _L0_ffn_in['b2']}

def reference(x, src, dst, L0_gnn_W1, L0_gnn_b1, L0_gnn_W2, L0_gnn_b2, L0_ffn_Wr, L0_ffn_br, L0_ffn_ln_g, L0_ffn_ln_b, L0_ffn_W1, L0_ffn_b1, L0_ffn_W2, L0_ffn_b2):
    import jax
    import jax.numpy as jnp

    def _L0_gnn_ref(x, edge_index, W1, b1, W2, b2):
        import jax, jax.numpy as jnp
        import numpy as np
        N_NODES = 6250

        def _gcn_conv(x, W, b, src, dst, n):
            h = x @ W
            loop = jnp.arange(n, dtype=src.dtype)
            src_sl = jnp.concatenate([src, loop])
            dst_sl = jnp.concatenate([dst, loop])
            deg = jax.ops.segment_sum(jnp.ones_like(dst_sl, dtype=h.dtype), dst_sl, num_segments=n)
            dinv = jnp.where(deg > 0, jax.lax.rsqrt(deg), 0.0)
            norm = dinv[src_sl] * dinv[dst_sl]
            msgs = h[src_sl] * norm[:, None]
            out = jax.ops.segment_sum(msgs, dst_sl, num_segments=n)
            return out + b
        src, dst = (edge_index[0], edge_index[1])
        h = _gcn_conv(x, W1, b1, src, dst, N_NODES)
        h = jax.nn.relu(h)
        h = _gcn_conv(h, W2, b2, src, dst, N_NODES)
        h = jax.nn.relu(h)
        return h

    def _L0_ffn_ref(x, Wr, br, ln_g, ln_b, W1, b1, W2, b2):
        import jax, jax.numpy as jnp
        import numpy as np
        TOP_K = 2
        LN_EPS = 1e-05
        B, S, D = x.shape
        N = B * S
        xt = x.reshape(N, D)
        logits = xt @ Wr + br
        probs = jax.nn.softmax(logits, axis=-1)
        top_p, top_idx = jax.lax.top_k(probs, TOP_K)
        weights = top_p / top_p.sum(axis=-1, keepdims=True)
        mu = xt.mean(axis=-1, keepdims=True)
        var = ((xt - mu) ** 2).mean(axis=-1, keepdims=True)
        xn = (xt - mu) * jax.lax.rsqrt(var + LN_EPS)
        xe = xn[None, :, :] * ln_g[:, None, :] + ln_b[:, None, :]
        h = jax.nn.gelu(jnp.einsum('end,edh->enh', xe, W1) + b1[:, None, :], approximate=False)
        y = jnp.einsum('enh,ehd->end', h, W2) + b2[:, None, :]
        y_tok = jnp.transpose(y, (1, 0, 2))
        sel = jnp.take_along_axis(y_tok, top_idx[:, :, None], axis=1)
        out = (weights[:, :, None] * sel).sum(axis=1)
        return out.reshape(B, S, D)
    edge_index = jnp.stack([src, dst])
    x = x + _L0_gnn_ref(_layernorm(x, axis=-1), edge_index, L0_gnn_W1, L0_gnn_b1, L0_gnn_W2, L0_gnn_b2)
    x = x + _L0_ffn_ref(_layernorm(x, axis=-1)[None], L0_ffn_Wr, L0_ffn_br, L0_ffn_ln_g, L0_ffn_ln_b, L0_ffn_W1, L0_ffn_b1, L0_ffn_W2, L0_ffn_b2)[0]
    return x

_drawn_inputs = setup_inputs


def setup_inputs(seed=0):
    import zlib

    import numpy as np

    out = dict(_drawn_inputs(seed))
    spreads = {'L0_gnn_b1': (0.0, 0.1),
     'L0_gnn_b2': (0.0, 0.1),
     'L0_ffn_br': (0.0, 0.1),
     'L0_ffn_ln_g': (1.0, 0.2),
     'L0_ffn_ln_b': (0.0, 0.1),
     'L0_ffn_b1': (0.0, 0.1),
     'L0_ffn_b2': (0.0, 0.1)}
    factors = {}
    for name, (base, spread) in spreads.items():
        noise = np.random.default_rng([zlib.crc32(name.encode()), seed]).standard_normal(out[name].shape)
        drawn = base * np.exp(spread * noise) if base else spread * noise
        out[name] = jnp.asarray(drawn.astype(out[name].dtype))
    for name, factor in factors.items():
        out[name] = (out[name] * factor).astype(out[name].dtype)
    return out
```

```python
from contextlib import ExitStack

import concourse.bass as bass
from concourse import mybir

P = 128
D = 256
KF = D // P
NODES = 6250
BLOCKS = -(-NODES // P)
PAD_NODES = BLOCKS * P
EDGES = 206250
EDGE_TILES = -(-EDGES // P)
ITEMS = EDGES // P + BLOCKS
ITEM_COLS = -(-ITEMS // P)
EXPERTS = 8
HIDDEN = 1024
HB = HIDDEN // P
TOKEN_TILES = (2 * PAD_NODES + EXPERTS * (P - 1)) // P
SLOTS = TOKEN_TILES * P
EPS = 1e-5
SCALE = 64.0

fp32 = mybir.dt.float32
fp16 = mybir.dt.float16
bf16 = mybir.dt.bfloat16
i32 = mybir.dt.int32
u32 = mybir.dt.uint32
ALU = mybir.AluOpType
ACT = mybir.ActivationFunctionType
AX = mybir.AxisListType

GRP = 13
GROUPS = EDGE_TILES // GRP
HRING = 4
HTURNS = GROUPS // HRING
BANK = 512
RING = 4
U = 7
TURNS = BLOCKS // U
R = 20
AGG_TURNS = ITEMS // R
HALF = R // 2
SUMS = 4
M = 5
TILE_TURNS = TOKEN_TILES // M
LN_STEPS = 2 * U + 1
assert GROUPS * GRP == EDGE_TILES and HTURNS * HRING == GROUPS and TURNS * U == BLOCKS
assert AGG_TURNS * R == ITEMS and TILE_TURNS * M == TOKEN_TILES


class Kernel:

    def __init__(self, nc, ctx, dram):
        self.nc, self.ctx, self.io = nc, ctx, dram

    def sb(self, name, shape, dt):
        return self.ctx.enter_context(self.nc.sbuf_tensor(name, shape, dt))

    def dr(self, name, shape, dt):
        return self.nc.dram_tensor(name, shape, dt, kind="Internal").ap()


def local(nc, st):
    def banks(name, shape, dt):
        n = -(-shape[1] // BANK) * BANK
        return st.enter_context(nc.psum_tensor(name, [P, n], dt))[0:shape[0], 0:shape[1]]

    sems = []

    def sem(name):
        sems.append(nc.alloc_semaphore(name))
        return sems[-1]

    def give_back():
        nc.clear_and_free_semaphores(sems)
        nc.all_engine_barrier()

    st.callback(give_back)
    return lambda name, shape, dt: st.enter_context(nc.sbuf_tensor(name, shape, dt)), banks, sem


def hold_waits(k, eng):
    if eng is k.nc.gpsimd:
        eng.tensor_tensor(k.held_pool[:, 0:1], k.held_pool[:, 1:2], k.held_pool[:, 1:2], ALU.add)
    else:
        eng.memset(k.held_dve[:], 0.0)


def since(u):
    return RING if u >= RING else U - max(v for v in range(U) if v % RING == u)


def bc(ap, shape):
    return ap.to_broadcast(shape)


def build_constants(k, ast):
    nc = k.nc
    k.ident = k.sb("ident", [P, P], fp32)
    k.ones = k.sb("ones", [P, P], fp32)
    k.held_pool = k.sb("held_pool", [1, 2], fp32)
    k.held_dve = k.sb("held_dve", [1, 1], fp32)
    k.eps = k.sb("eps", [P, 1], fp32)
    k.tri = k.sb("tri", [P, P], fp32)
    k.lane_h = k.sb("lane_h", [P, P], fp16)
    k.lane_b = k.sb("lane_b", [P, P], bf16)
    k.lane_f = k.sb("lane_f", [P, P], fp32)
    k.item_id = k.sb("item_id", [P, ITEM_COLS], fp32)
    k.token_id = k.sb("token_id", [P, BLOCKS], i32)
    k.dinv_in = k.sb("dinv_in", [P, BLOCKS], fp32)
    k.dinv_out = k.sb("dinv_out", [P, BLOCKS], fp32)
    k.logits = k.sb("logits", [P, BLOCKS, EXPERTS], fp32)
    k.gate = k.sb("gate", [P, 2, BLOCKS], fp32)
    k.slot = k.sb("slot", [P, 2, BLOCKS], i32)
    k.slot_token = k.sb("slot_token", [P, TOKEN_TILES], i32)
    k.tile_expert = k.sb("tile_expert", [1, TOKEN_TILES], i32)
    k.x2_rows = k.dr("x2_rows", [PAD_NODES, D], fp32)
    k.acc = ast.enter_context(nc.sbuf_tensor("acc", [P, BLOCKS, D], fp32))
    k.h_rows = k.dr("h_rows", [PAD_NODES, 2 * D], fp16)
    with ExitStack() as st:
        sb, pb, sem = local(nc, st)
        ints = sb("c_ints", [P, P], i32)
        item_i = sb("c_item_i", [P, ITEM_COLS], i32)
        io_done, ones_done, x_in = sem("c_iota"), sem("c_ones"), sem("c_x_in")
        block = st.enter_context(nc.Block())

        @block.sync
        def _(sp):
            sp.dma_start(k.acc[:], k.io["x"].rearrange("(b p) d -> p b d", p=P)).then_inc(x_in, 16)
            sp.wait_ge(x_in, 16)

        @block.gpsimd
        def _(pool):
            nc.gpsimd.iota(ints[:], pattern=[[1, P]], base=0, channel_multiplier=0).then_inc(io_done, 1)
            nc.gpsimd.iota(item_i[:], pattern=[[P, ITEM_COLS]], base=0, channel_multiplier=1).then_inc(io_done, 1)
            nc.gpsimd.iota(k.token_id[:], pattern=[[P, BLOCKS]], base=0, channel_multiplier=1).then_inc(io_done, 1)
            pool.wait_ge(ones_done, 1)
            nc.gpsimd.affine_select(out=k.ident[:], in_=k.ones[:], compare_op=ALU.is_equal, fill=0.0, base=0,
                                    pattern=[[-1, P]], channel_multiplier=1)
            nc.gpsimd.affine_select(out=k.tri[:], in_=k.ones[:], compare_op=ALU.is_gt, fill=0.0, base=0,
                                    pattern=[[1, P]], channel_multiplier=-1)

        @block.vector
        def _(dve):
            nc.vector.memset(k.ones[:], 1.0).then_inc(ones_done, 1)
            nc.vector.memset(k.eps[:], EPS)
            nc.vector.memset(k.held_pool[:], 0.0)
            dve.wait_ge(io_done, 3)
            nc.vector.tensor_copy(k.lane_h[:], ints[:])
            nc.vector.tensor_copy(k.lane_b[:], ints[:])
            nc.vector.tensor_copy(k.lane_f[:], ints[:])
            nc.vector.tensor_copy(k.item_id[:], item_i[:])


def build_edge_tables(k, gst):
    nc = k.nc
    own = lambda name, shape, dt: gst.enter_context(nc.sbuf_tensor(name, shape, dt))
    k.edge_src = own("edge_src", [P, ITEM_COLS * P], i32)
    k.edge_dst = own("edge_dst", [P, ITEM_COLS * P], fp32)
    k.item_block = own("item_block", [1, ITEM_COLS * P], i32)
    block_row = k.dr("block_row", [ITEM_COLS, P], i32)
    with ExitStack() as st:
        sb, pb, sem = local(nc, st)
        dst = sb("t_dst", [P, EDGE_TILES], i32)
        part = sb("t_part", [P, EDGE_TILES], i32)
        hi = sb("t_hi", [P, EDGE_TILES], bf16)
        lo = sb("t_lo", [P, EDGE_TILES], bf16)
        oh_lo = sb("t_oh_lo", [P, HRING, GRP, P], bf16)
        oh_hi = sb("t_oh_hi", [P, HRING, GRP, BLOCKS], bf16)
        deg = sb("t_deg", [P, BLOCKS], fp32)
        tmp = sb("t_tmp", [P, BLOCKS], fp32)
        tot = sb("t_tot", [P, BLOCKS], fp32)
        cum = sb("t_cum", [P, BLOCKS], fp32)
        first_i = sb("t_first_i", [P, BLOCKS], i32)
        first = sb("t_first", [P, BLOCKS], fp32)
        le = sb("t_le", [P, ITEM_COLS, BLOCKS - 1], fp32)
        blk = sb("t_blk", [P, ITEM_COLS], fp32)
        blk_off = sb("t_blk_off", [P, ITEM_COLS], fp32)
        tile_f = sb("t_tile_f", [P, ITEM_COLS], fp32)
        tile_i = sb("t_tile_i", [P, ITEM_COLS], i32)
        blk_t = sb("t_blk_t", [ITEM_COLS, P], i32)
        rows_s = sb("t_rows_s", [P, ITEM_COLS, P], i32)
        rows_d = sb("t_rows_d", [P, ITEM_COLS, P], i32)
        rows_sf = sb("t_rows_sf", [P, ITEM_COLS, P], fp32)
        rows_df = sb("t_rows_df", [P, ITEM_COLS, P], fp32)
        ps_deg = pb("tp_deg", [P, BLOCKS], fp32)
        ps_tot = pb("tp_tot", [P, BLOCKS], fp32)
        ps_blk = pb("tp_blk", [ITEM_COLS, P], fp32)
        ps_t = [pb(f"tp_t{i}", [P, P], fp32) for i in range(4)]
        dst_in, lo_done, hi_done, groups_done = (
            sem("t_dst_in"), sem("t_lo_done"), sem("t_hi_done"), sem("t_groups_done"))
        step = sem("t_step")
        deg_ready, tot_done, root_done, blk_ready, blk_t_done, blk_row_ready = (
            sem("t_deg_ready"), sem("t_tot_done"), sem("t_root"), sem("t_blk_ready"), sem("t_blk_t"), sem("t_blk_row"))
        row_out, row_in, tile_ready, got_rows, rows_ready, t_done, t_copied = (
            sem("t_row_out"), sem("t_row_in"), sem("t_tile_ready"), sem("t_got_rows"), sem("t_rows_ready"),
            sem("t_t_done"), sem("t_t_copied"))
        block = st.enter_context(nc.Block())

        @block.sync
        def _(sp):
            sp.dma_start(dst[:], k.io["dst"].rearrange("(p c) -> p c", p=P)).then_inc(dst_in, 16)
            sp.wait_ge(blk_row_ready, 1)
            sp.dma_start(block_row, blk_t[:]).then_inc(row_out, 16)
            sp.wait_ge(row_out, 16)
            sp.dma_start(k.item_block[:], block_row.rearrange("c p -> (c p)")[None, :]).then_inc(row_in, 16)
            sp.wait_ge(row_in, 16)

        @block.vector
        def _(dve):
            dve.wait_ge(dst_in, 16)
            nc.vector.tensor_single_scalar(part[:], dst[:], 7, ALU.arith_shift_right).then_inc(step, 1)
            dve.wait_ge(step, 1)
            nc.vector.tensor_copy(hi[:], part[:]).then_inc(step, 1)
            dve.wait_ge(step, 2)
            nc.vector.tensor_single_scalar(part[:], dst[:], P - 1, ALU.bitwise_and).then_inc(step, 1)
            dve.wait_ge(step, 3)
            nc.vector.tensor_copy(lo[:], part[:]).then_inc(step, 1)
            dve.wait_ge(step, 4)

            def one_hots(n):
                for r in range(HRING):
                    if not (isinstance(n, int) and n == 0):
                        dve.wait_ge(groups_done, n * HRING + (r + 1 - HRING))
                    nc.vector.tensor_tensor(
                        oh_lo[:, r], bc(k.lane_b[:, None, :], [P, GRP, P]),
                        bc(lo[:, bass.ds(n * (HRING * GRP) + r * GRP, GRP)][:, :, None], [P, GRP, P]),
                        ALU.is_equal).then_inc(lo_done, 1)
                    nc.vector.tensor_tensor(
                        oh_hi[:, r], bc(k.lane_b[:, None, 0:BLOCKS], [P, GRP, BLOCKS]),
                        bc(hi[:, bass.ds(n * (HRING * GRP) + r * GRP, GRP)][:, :, None], [P, GRP, BLOCKS]),
                        ALU.is_equal).then_inc(hi_done, 1)
            one_hots(0)
            with nc.vector.Fori(1, HTURNS) as n:
                one_hots(n)
            dve.wait_ge(groups_done, GROUPS)
            nc.vector.tensor_copy(deg[:], ps_deg[:]).then_inc(deg_ready, 1)
            dve.wait_ge(deg_ready, 1)
            nc.vector.tensor_scalar(tmp[:], deg[:], 1.0, None, ALU.add).then_inc(deg_ready, 1)
            dve.wait_ge(root_done, 1)
            nc.vector.reciprocal(cum[:], tot[:]).then_inc(step, 1)
            dve.wait_ge(step, 5)
            nc.vector.tensor_scalar(k.dinv_in[:], cum[:], SCALE, None, ALU.mult)
            nc.vector.tensor_scalar(k.dinv_out[:], cum[:], 1.0 / SCALE, None, ALU.mult).then_inc(step, 1)
            dve.wait_ge(tot_done, 1)
            dve.wait_ge(step, 6)
            nc.vector.tensor_copy(tot[:], ps_tot[:]).then_inc(step, 1)
            nc.vector.memset(tmp[:], 1.0).then_inc(step, 1)
            dve.wait_ge(step, 8)
            nc.vector.tensor_tensor_scan(cum[:], tmp[:], tot[:], 0.0, ALU.mult, ALU.add).then_inc(step, 1)
            dve.wait_ge(step, 9)
            nc.vector.tensor_copy(first_i[:], cum[:]).then_inc(step, 1)
            dve.wait_ge(step, 10)
            nc.vector.tensor_single_scalar(first_i[:], first_i[:], 7, ALU.arith_shift_right).then_inc(step, 1)
            dve.wait_ge(step, 11)
            nc.vector.tensor_copy(first[:], first_i[:]).then_inc(step, 1)
            dve.wait_ge(step, 12)
            nc.vector.tensor_tensor(first[:], first[:], k.lane_f[:, 1:BLOCKS + 1], ALU.add).then_inc(step, 1)
            dve.wait_ge(step, 13)
            nc.vector.tensor_tensor(le[:], bc(first[:, None, 0:BLOCKS - 1], [P, ITEM_COLS, BLOCKS - 1]),
                                    bc(k.item_id[:, :, None], [P, ITEM_COLS, BLOCKS - 1]), ALU.is_le).then_inc(step, 1)
            dve.wait_ge(step, 14)
            nc.vector.tensor_reduce(blk[:], le[:], AX.X, ALU.add).then_inc(step, 1)
            dve.wait_ge(step, 15)
            nc.vector.tensor_scalar(blk_off[:], blk[:], float(P), None, ALU.mult).then_inc(blk_ready, 1)
            nc.vector.tensor_tensor(tile_f[:], k.item_id[:], blk[:], ALU.subtract).then_inc(step, 1)
            dve.wait_ge(step, 16)
            nc.vector.tensor_scalar(tile_f[:], tile_f[:], float(EDGE_TILES - 1), None, ALU.min).then_inc(step, 1)
            dve.wait_ge(step, 17)
            nc.vector.tensor_copy(tile_i[:], tile_f[:]).then_inc(tile_ready, 1)
            dve.wait_ge(blk_t_done, 1)
            nc.vector.tensor_copy(blk_t[:], ps_blk[:]).then_inc(blk_row_ready, 1)
            dve.wait_ge(blk_ready, 1)
            for c in range(ITEM_COLS):
                dve.wait_ge(got_rows, 32 * ITEM_COLS)
                nc.vector.tensor_copy(rows_sf[:, c, :], rows_s[:, c, :]).then_inc(rows_ready, 1)
                nc.vector.tensor_scalar(rows_df[:, c, :], rows_d[:, c, :], blk_off[:, c:c + 1], None,
                                        ALU.subtract).then_inc(rows_ready, 1)
            for c in range(2 * ITEM_COLS):
                dve.wait_ge(t_done, c + 1)
                out = k.edge_src if c % 2 == 0 else k.edge_dst
                nc.vector.tensor_copy(out[:, (c // 2) * P:(c // 2 + 1) * P], ps_t[c % 4][:]).then_inc(t_copied, 1)

        @block.scalar
        def _(act):
            act.wait_ge(deg_ready, 2)
            nc.scalar.activation(tot[:], tmp[:], ACT.Sqrt).then_inc(root_done, 1)

        @block.gpsimd
        def _(pool):
            pool.wait_ge(tile_ready, 1)
            for c in range(ITEM_COLS):
                for rows, name in ((rows_s, "src"), (rows_d, "dst")):
                    pool.indirect_dma_start(
                        out=rows[:, c, :], out_offset=None, in_=k.io[name].rearrange("(t e) -> t e", e=P),
                        in_offset=bass.IndirectOffsetOnAxis(ap=tile_i[:, c:c + 1], axis=0)).then_inc(got_rows, 16)
            pool.wait_ge(got_rows, 32 * ITEM_COLS)

        @block.tensor
        def _(pe):
            def group(n, first=False, last=False):
                for r in range(HRING):
                    pe.wait_ge(lo_done, n * HRING + r + 1)
                    pe.wait_ge(hi_done, n * HRING + r + 1)
                    for g in range(GRP):
                        mm = nc.tensor.matmul(ps_deg[:], oh_lo[:, r, g, :], oh_hi[:, r, g, :],
                                              start=first and r == 0 and g == 0,
                                              stop=last and r == HRING - 1 and g == GRP - 1)
                    mm.then_inc(groups_done, 1)
            group(0, first=True)
            with nc.tensor.Fori(1, HTURNS - 1) as n:
                group(n)
            group(HTURNS - 1, last=True)
            pe.wait_ge(deg_ready, 1)
            nc.tensor.matmul(ps_tot[:], k.ones[:], deg[:], start=True, stop=True).then_inc(tot_done, 1)
            pe.wait_ge(blk_ready, 1)
            nc.tensor.transpose(ps_blk[:], blk[:], k.ident[:]).then_inc(blk_t_done, 1)
            for c in range(2 * ITEM_COLS):
                pe.wait_ge(rows_ready, c + 1)
                if c >= 4:
                    pe.wait_ge(t_copied, c - 3)
                rows = rows_sf if c % 2 == 0 else rows_df
                nc.tensor.transpose(ps_t[c % 4][:], rows[:, c // 2, :], k.ident[:]).then_inc(t_done, 1)


def build_project(k, name, weight, bias):
    nc = k.nc
    with ExitStack() as st:
        sb, pb, sem = local(nc, st)
        w = sb(f"{name}_w", [P, KF, D], fp32)
        brow = sb(f"{name}_b", [P, D], fp32)
        pre = sb(f"{name}_pre", [P, U, D], fp32)
        z = sb(f"{name}_z", [P, U, D], fp32)
        zt = sb(f"{name}_zt", [P, U, D], fp32)
        halves = sb(f"{name}_halves", [P, U, 2 * D], fp16)
        stats = sb(f"{name}_stats", [P, U, 6], fp32)
        mv = sb(f"{name}_mv", [P, U, 2], fp32)
        ps_t = [pb(f"{name}_pt{i}", [P, D], fp32) for i in range(RING)]
        ps_h = [pb(f"{name}_ph{i}", [P, D], fp32) for i in range(RING)]
        w_in, root = sem(f"{name}_w_in"), sem(f"{name}_root")
        ln, z_ready, t_done, t_copied, h_done, acc_done, hi_done, lo_done, pre_done = (
            sem(f"{name}_{x}") for x in ("ln", "z_ready", "t_done", "t_copied", "h_done", "acc_done", "hi_done",
                                         "lo_done", "pre_done"))
        stored = [sem(f"{name}_stored{u}") for u in range(U)]
        block = st.enter_context(nc.Block())

        @block.sync
        def _(sp):
            sp.dma_start(w[:], k.io[weight].rearrange("(c p) n -> p c n", p=P)).then_inc(w_in, 16)
            if bias:
                sp.dma_start(brow[:], k.io[bias][None, :].to_broadcast([P, D])).then_inc(w_in, 16)

            def turn(n):
                for u in range(U):
                    sp.wait_ge(hi_done, n * U + u + 1)
                    sp.wait_ge(lo_done, n * U + u + 1)
                    sp.dma_start(k.h_rows[bass.ds((n * U + u) * P, P), :], halves[:, u, :]).then_inc(stored[u], 16)
            with nc.sync.Fori(0, TURNS) as n:
                turn(n)
            for u in range(U):
                sp.wait_ge(stored[u], 16 * TURNS)

        @block.vector
        def _(dve):
            if bias:
                dve.wait_ge(w_in, 32)

            def turn(n, first=False):
                blk = lambda u: k.acc[:, bass.ds(n * U + u, 1), :][:, 0, :]
                if not first:
                    dve.wait_ge(t_done, n * U)
                if bias:
                    if not first:
                        dve.wait_ge(pre_done, n * U)
                    for u in range(U):
                        nc.vector.scalar_tensor_tensor(pre[:, u, :], blk(u), k.dinv_out[:, bass.ds(n * U + u, 1)],
                                                       brow[:], ALU.mult, ALU.add).then_inc(ln, 1)
                else:
                    hold_waits(k, nc.vector)
                    for u in range(U):
                        nc.vector.bn_stats(stats[:, u, :], blk(u)).then_inc(ln, 1)
                    dve.wait_ge(ln, n * LN_STEPS + U)
                    hold_waits(k, nc.vector)
                    for u in range(U):
                        nc.vector.bn_aggr(mv[:, u, :], stats[:, u, :]).then_inc(ln, 1)
                    dve.wait_ge(root, n + 1)
                    nc.vector.reciprocal(mv[:, :, 1], mv[:, :, 1]).then_inc(ln, 1)
                    dve.wait_ge(ln, n * LN_STEPS + LN_STEPS)
                    for u in range(U):
                        nc.vector.tensor_scalar(z[:, u, :], blk(u), mv[:, u, 0:1], mv[:, u, 1:2],
                                                ALU.subtract, ALU.mult).then_inc(z_ready, 1)
                    dve.wait_ge(z_ready, n * U + U)
                if not first:
                    for u in range(U):
                        dve.wait_ge(stored[u], n * 16)
                for u in range(U):
                    dve.wait_ge(h_done, n * U + u + 1)
                    nc.vector.tensor_scalar(blk(u), ps_h[u % RING], k.dinv_in[:, bass.ds(n * U + u, 1)], None,
                                            ALU.mult).then_inc(acc_done, 1)
                for u in range(U):
                    dve.wait_ge(acc_done, n * U + u + 1)
                    dve.wait_ge(hi_done, n * U + u + 1)
                    nc.vector.tensor_tensor(halves[:, u, D:2 * D], blk(u), halves[:, u, 0:D],
                                            ALU.subtract).then_inc(lo_done, 1)
            turn(0, first=True)
            with nc.vector.Fori(1, TURNS) as n:
                turn(n)

        @block.scalar
        def _(act):
            def turn(n, first=False):
                if not bias:
                    act.wait_ge(ln, n * LN_STEPS + 2 * U)
                    nc.scalar.activation(mv[:, :, 1], mv[:, :, 1], ACT.Sqrt, bias=k.eps[:]).then_inc(root, 1)
                if bias:
                    if not first:
                        act.wait_ge(t_done, n * U)
                    for u in range(U):
                        act.wait_ge(ln, n * U + u + 1)
                        nc.scalar.activation(z[:, u, :], pre[:, u, :], ACT.Relu).then_inc(pre_done, 1)
                for u in range(U):
                    act.wait_ge(t_done, n * U + u + 1)
                    if not first:
                        act.wait_ge(h_done, n * U + (u + 1 - U))
                    nc.scalar.activation(zt[:, u, :], ps_t[u % RING], ACT.Copy).then_inc(t_copied, 1)
                for u in range(U):
                    act.wait_ge(acc_done, n * U + u + 1)
                    if not first:
                        act.wait_ge(stored[u], n * 16)
                    nc.scalar.activation(halves[:, u, 0:D], k.acc[:, bass.ds(n * U + u, 1), :][:, 0, :],
                                         ACT.Copy).then_inc(hi_done, 1)
            turn(0, first=True)
            with nc.scalar.Fori(1, TURNS) as n:
                turn(n)

        @block.tensor
        def _(pe):
            pe.wait_ge(w_in, 32 if bias else 16)

            def turn(n, first=False):
                for u in range(U):
                    pe.wait_ge(pre_done if bias else z_ready, n * U + u + 1)
                    if not (first and u < RING):
                        pe.wait_ge(t_copied, n * U + (u + 1 - since(u)))
                    for c in range(KF):
                        mm = nc.tensor.transpose(ps_t[u % RING][:, c * P:(c + 1) * P], z[:, u, c * P:(c + 1) * P], k.ident[:])
                    mm.then_inc(t_done, 1)
                for u in range(U):
                    pe.wait_ge(t_copied, n * U + u + 1)
                    if not (first and u < RING):
                        pe.wait_ge(acc_done, n * U + (u + 1 - since(u)))
                    for c in range(KF):
                        mm = nc.tensor.matmul(ps_h[u % RING], zt[:, u, c * P:(c + 1) * P], w[:, c, :],
                                              start=c == 0, stop=c == KF - 1)
                    mm.then_inc(h_done, 1)
            turn(0, first=True)
            with nc.tensor.Fori(1, TURNS) as n:
                turn(n)


def build_aggregate(k, name):
    nc = k.nc
    with ExitStack() as st:
        sb, pb, sem = local(nc, st)
        rows = sb(f"{name}_rows", [P, R, 2 * D], fp16)
        stage = sb(f"{name}_stage", [P, 2, HALF], i32)
        sel = sb(f"{name}_sel", [P, R, P], fp16)
        ps = [pb(f"{name}_ps{i}", [P, D], fp32) for i in range(SUMS)]
        got = [sem(f"{name}_got{r}") for r in range(R)]
        staged, sel_ready, sum_done, added = (sem(f"{name}_{x}") for x in ("staged", "sel", "sum", "added"))
        block = st.enter_context(nc.Block())

        @block.gpsimd
        def _(pool):
            def turn(n, first=False):
                for h in range(2):
                    if not first:
                        for r in range(h * HALF, (h + 1) * HALF):
                            pool.wait_ge(got[r], 16 * n)
                        pool.wait_ge(sum_done, n * R + ((h + 1) * HALF - R))
                    nc.gpsimd.tensor_copy(stage[:, h, :], k.edge_src[:, bass.ds(n * R + h * HALF, HALF)]).then_inc(staged, 1)
                    pool.wait_ge(staged, n * 2 + h + 1)
                    hold_waits(k, nc.gpsimd)
                    for r in range(HALF):
                        s = h * HALF + r
                        pool.indirect_dma_start(
                            out=rows[:, s, :], out_offset=None, in_=k.h_rows,
                            in_offset=bass.IndirectOffsetOnAxis(ap=stage[:, h, r:r + 1], axis=0)).then_inc(got[s], 16)
            turn(0, first=True)
            with nc.gpsimd.Fori(1, AGG_TURNS) as n:
                turn(n)

        @block.vector
        def _(dve):
            regs = [nc.vector.alloc_register(f"{name}_blk{r}") for r in range(R)]

            def select(n, s, first):
                if not first:
                    dve.wait_ge(sum_done, n * R + (s + 1 - R))
                nc.vector.tensor_scalar(sel[:, s, :], k.lane_h[:], k.edge_dst[:, bass.ds(n * R + s, 1)], None,
                                        ALU.is_equal).then_inc(sel_ready, 1)

            def turn(n, first=False):
                nc.vector.load(regs, k.item_block[0:1, bass.ds(n * R, R)])
                blocks = [nc.vector.snap(r, min_val=0, max_val=BLOCKS - 1) for r in regs]
                for s in range(R):
                    select(n, s, first)
                for s in range(R):
                    dve.wait_ge(sum_done, n * R + s + 1)
                    if not (first and s == 0):
                        dve.wait_ge(added, n * R + s)
                    a = k.acc[:, bass.ds(blocks[s], 1), :][:, 0, :]
                    nc.vector.tensor_tensor(a, a, ps[s % SUMS][:], ALU.add).then_inc(added, 1)
            turn(0, first=True)
            with nc.vector.Fori(1, AGG_TURNS) as n:
                turn(n)

        @block.tensor
        def _(pe):
            def turn(n, first=False):
                for s in range(R):
                    pe.wait_ge(sel_ready, n * R + s + 1)
                    pe.wait_ge(got[s], 16 * (n + 1))
                    if not (first and s < SUMS):
                        pe.wait_ge(added, n * R + (s + 1 - SUMS))
                    nc.tensor.matmul(ps[s % SUMS][:], sel[:, s, :], rows[:, s, 0:D], start=True, stop=False)
                    nc.tensor.matmul(ps[s % SUMS][:], sel[:, s, :], rows[:, s, D:2 * D], start=False,
                                     stop=True).then_inc(sum_done, 1)
            turn(0, first=True)
            with nc.tensor.Fori(1, AGG_TURNS) as n:
                turn(n)


def build_tokens(k):
    nc = k.nc
    k.xn_rows = k.dr("xn_rows", [PAD_NODES, D], fp32)
    with ExitStack() as st:
        sb, pb, sem = local(nc, st)
        wr = sb("r_wr", [P, KF, EXPERTS], fp32)
        br = sb("r_br", [P, EXPERTS], fp32)
        b2 = sb("r_b2", [P, D], fp32)
        x = sb("r_x", [P, U, D], fp32)
        z = sb("r_z", [P, U, D], fp32)
        xn = sb("r_xn", [P, U, D], fp32)
        zt = sb("r_zt", [P, U, D], fp32)
        stats = sb("r_stats", [P, U, 6], fp32)
        mv = sb("r_mv", [P, U, 2], fp32)
        ps_t = [pb(f"rp_t{i}", [P, D], fp32) for i in range(RING)]
        ps_l = pb("rp_l", [P, U * EXPERTS], fp32)
        w_in, step, xt_ready, t_done, t_copied, l_done, xn_ready, logit_ready = (
            sem("r_" + s) for s in ("w_in", "step", "xt_ready", "t_done", "t_copied", "l_done", "xn_ready", "logit"))
        x_in = [sem(f"r_x_in{u}") for u in range(U)]
        stored = [sem(f"r_stored{u}") for u in range(U)]
        x_free, kept, root = sem("r_x_free"), sem("r_kept"), sem("r_root")
        block = st.enter_context(nc.Block())
        STEPS = U + 2 * LN_STEPS + 1

        @block.sync
        def _(sp):
            sp.dma_start(wr[:], k.io["L0_ffn_Wr"].rearrange("(c p) n -> p c n", p=P)).then_inc(w_in, 16)
            sp.dma_start(br[:], k.io["L0_ffn_br"][None, :].to_broadcast([P, EXPERTS])).then_inc(w_in, 16)
            sp.dma_start(b2[:], k.io["L0_gnn_b2"][None, :].to_broadcast([P, D])).then_inc(w_in, 16)

            def turn(n, first=False):
                for u in range(U):
                    if not first:
                        sp.wait_ge(x_free, n * U + (u + 1 - U))
                    sp.dma_start(x[:, u, :], k.io["x"][bass.ds((n * U + u) * P, P), :]).then_inc(x_in[u], 16)
            turn(0, first=True)
            with nc.sync.Fori(1, TURNS) as n:
                turn(n)

        @block.scalar
        def _(act):
            def turn(n, first=False):
                for t in range(2):
                    act.wait_ge(step, n * STEPS + U + t * LN_STEPS + 2 * U)
                    nc.scalar.activation(mv[:, :, 1], mv[:, :, 1], ACT.Sqrt, bias=k.eps[:]).then_inc(root, 1)
                for u in range(U):
                    act.wait_ge(t_done, n * U + u + 1)
                    if not first:
                        act.wait_ge(l_done, n * U + (u + 1 - U))
                    nc.scalar.activation(zt[:, u, :], ps_t[u % RING], ACT.Copy).then_inc(t_copied, 1)
                for u in range(U):
                    act.wait_ge(xn_ready, n * U + u + 1)
                    act.dma_start(k.xn_rows[bass.ds((n * U + u) * P, P), :], xn[:, u, :]).then_inc(stored[u], 16)
                    act.dma_start(k.x2_rows[bass.ds((n * U + u) * P, P), :],
                                  k.acc[:, bass.ds(n * U + u, 1), :][:, 0, :]).then_inc(kept, 16)
            turn(0, first=True)
            with nc.scalar.Fori(1, TURNS) as n:
                turn(n)
            for u in range(U):
                act.wait_ge(stored[u], 16 * TURNS)
            act.wait_ge(kept, 16 * BLOCKS)

        @block.vector
        def _(dve):
            dve.wait_ge(w_in, 48)

            def turn(n, first=False):
                blk = lambda u: k.acc[:, bass.ds(n * U + u, 1), :][:, 0, :]
                if not first:
                    dve.wait_ge(t_done, n * U)
                    for u in range(U):
                        dve.wait_ge(stored[u], n * 16)
                for u in range(U):
                    nc.vector.scalar_tensor_tensor(z[:, u, :], blk(u), k.dinv_out[:, bass.ds(n * U + u, 1)],
                                                   b2[:], ALU.mult, ALU.add).then_inc(step, 1)
                dve.wait_ge(step, n * STEPS + U)
                for u in range(U):
                    dve.wait_ge(x_in[u], n * 16 + 16)
                    nc.vector.scalar_tensor_tensor(blk(u), z[:, u, :], 0.0, x[:, u, :], ALU.max,
                                                   ALU.add).then_inc(x_free, 1)
                dve.wait_ge(x_free, n * U + U)
                for t, (src, out, done) in enumerate(((blk, z, xt_ready), (lambda u: z[:, u, :], xn, xn_ready))):
                    s0 = n * STEPS + U + t * LN_STEPS
                    hold_waits(k, nc.vector)
                    for u in range(U):
                        nc.vector.bn_stats(stats[:, u, :], src(u)).then_inc(step, 1)
                    dve.wait_ge(step, s0 + U)
                    hold_waits(k, nc.vector)
                    for u in range(U):
                        nc.vector.bn_aggr(mv[:, u, :], stats[:, u, :]).then_inc(step, 1)
                    dve.wait_ge(root, n * 2 + t + 1)
                    nc.vector.reciprocal(mv[:, :, 1], mv[:, :, 1]).then_inc(step, 1)
                    dve.wait_ge(step, s0 + LN_STEPS)
                    for u in range(U):
                        nc.vector.tensor_scalar(out[:, u, :], src(u), mv[:, u, 0:1], mv[:, u, 1:2],
                                                ALU.subtract, ALU.mult).then_inc(done, 1)
                    dve.wait_ge(done, n * U + U)
                dve.wait_ge(l_done, n * U + U)
                nc.vector.tensor_tensor(k.logits[:, bass.ds(n * U, U), :], ps_l.rearrange("p (u e) -> p u e", u=U),
                                        bc(br[:, None, :], [P, U, EXPERTS]), ALU.add).then_inc(step, 1)
            turn(0, first=True)
            with nc.vector.Fori(1, TURNS) as n:
                turn(n)

        @block.tensor
        def _(pe):
            pe.wait_ge(w_in, 48)

            def turn(n, first=False):
                for u in range(U):
                    pe.wait_ge(xt_ready, n * U + u + 1)
                    if not (first and u < RING):
                        pe.wait_ge(t_copied, n * U + (u + 1 - since(u)))
                    for c in range(KF):
                        mm = nc.tensor.transpose(ps_t[u % RING][:, c * P:(c + 1) * P], z[:, u, c * P:(c + 1) * P], k.ident[:])
                    mm.then_inc(t_done, 1)
                for u in range(U):
                    pe.wait_ge(t_copied, n * U + u + 1)
                    if not first:
                        pe.wait_ge(step, n * STEPS)
                    for c in range(KF):
                        mm = nc.tensor.matmul(ps_l[:, u * EXPERTS:(u + 1) * EXPERTS], zt[:, u, c * P:(c + 1) * P], wr[:, c, :],
                                              start=c == 0, stop=c == KF - 1)
                    mm.then_inc(l_done, 1)
            turn(0, first=True)
            with nc.tensor.Fori(1, TURNS) as n:
                turn(n)


def build_routing(k):
    nc = k.nc
    slot_list = k.dr("slot_list", [SLOTS, 1], i32)
    NE = BLOCKS * EXPERTS
    with ExitStack() as st:
        sb, pb, sem = local(nc, st)
        back = sb("o_back", [P, EXPERTS], fp32)
        best = sb("o_best", [P, 2, BLOCKS], fp32)
        rest = sb("o_rest", [P, BLOCKS, EXPERTS], fp32)
        pick = sb("o_pick", [P, BLOCKS], fp32)
        hot = sb("o_hot", [P, 2, BLOCKS, EXPERTS], fp32)
        both = sb("o_both", [P, BLOCKS, EXPERTS], fp32)
        inner = sb("o_inner", [P, BLOCKS, EXPERTS], fp32)
        tot = sb("o_tot", [P, EXPERTS, BLOCKS], fp32)
        cum = sb("o_cum", [P, EXPERTS, BLOCKS], fp32)
        ones = sb("o_ones", [P, BLOCKS], fp32)
        cnt = sb("o_cnt", [P, EXPERTS], fp32)
        cnt_i = sb("o_cnt_i", [P, EXPERTS], i32)
        tiles = sb("o_tiles", [P, EXPERTS], fp32)
        ends = sb("o_ends", [P, EXPERTS], fp32)
        begin = sb("o_begin", [P, EXPERTS], fp32)
        slot_f = sb("o_slot_f", [P, 2, BLOCKS], fp32)
        gap = sb("o_gap", [P, BLOCKS], fp32)
        ex = sb("o_ex", [P, BLOCKS], fp32)
        le = sb("o_le", [1, TOKEN_TILES, EXPERTS - 1], fp32)
        te = sb("o_te", [1, TOKEN_TILES], fp32)
        zero = sb("o_zero", [TOKEN_TILES, P], i32)
        lst = sb("o_lst", [TOKEN_TILES, P], i32)
        lst_f = sb("o_lst_f", [TOKEN_TILES, P], fp32)
        stage = sb("o_stage", [P, 2, U], i32)
        stage_id = sb("o_stage_id", [P, U], i32)
        ps_in = pb("op_in", [P, NE], fp32)
        ps_tot = pb("op_tot", [P, NE], fp32)
        ps_l = pb("op_l", [P, TOKEN_TILES], fp32)
        s, hot_ready, pre_done, gap_ready, exp_done, slots_ready = (
            sem("o_" + x) for x in ("s", "hot", "pre", "gap", "exp", "slots"))
        zeroed, staged, list_in, lst_ready, lst_t = (
            sem("o_" + x) for x in ("zeroed", "staged", "list_in", "lst_ready", "lst_t"))
        put = [sem(f"o_put{i}") for i in range(2 * U)]
        zero_set = sem("o_zero_set")
        block = st.enter_context(nc.Block())

        @block.vector
        def _(dve):
            count = [0]

            def link(ins):
                count[0] += 1
                ins.then_inc(s, 1)
                dve.wait_ge(s, count[0])

            nc.vector.memset(zero[:], 0).then_inc(zero_set, 1)
            link(nc.vector.memset(ones[:], 1.0))

            link(nc.vector.tensor_scalar(back[:], k.lane_f[:, 0:EXPERTS], float(-EXPERTS), None, ALU.add))
            full = [P, BLOCKS, EXPERTS]
            for c in range(2):
                src = k.logits if c == 0 else rest
                link(nc.vector.tensor_reduce(best[:, c, :], src[:], AX.X, ALU.max))
                link(nc.vector.tensor_tensor(inner[:], src[:], bc(best[:, c, :, None], full), ALU.is_equal))
                link(nc.vector.tensor_tensor(inner[:], inner[:], bc(back[:, None, :], full), ALU.mult))
                link(nc.vector.tensor_reduce(pick[:], inner[:], AX.X, ALU.min))
                link(nc.vector.tensor_tensor(hot[:, c], bc(back[:, None, :], full), bc(pick[:, :, None], full),
                                             ALU.is_equal))
                if c == 0:
                    link(nc.vector.scalar_tensor_tensor(rest[:], hot[:, 0], -3e38, k.logits[:], ALU.mult, ALU.add))
            link(nc.vector.tensor_tensor(gap[:], best[:, 1, :], best[:, 0, :], ALU.subtract))
            nc.vector.tensor_tensor(both[:], hot[:, 0], hot[:, 1], ALU.add).then_inc(hot_ready, 1)
            dve.wait_ge(exp_done, 1)
            link(nc.vector.tensor_scalar(gap[:], ex[:], 1.0, None, ALU.add))
            link(nc.vector.reciprocal(k.gate[:, 0, :], gap[:]))
            link(nc.vector.tensor_tensor(k.gate[:, 1, :], ex[:], k.gate[:, 0, :], ALU.mult))
            dve.wait_ge(pre_done, 1)
            link(nc.vector.tensor_copy(inner[:], ps_in[:].rearrange("p (b e) -> p b e", e=EXPERTS)))
            link(nc.vector.tensor_copy(tot[:], ps_tot[:].rearrange("p (b e) -> p e b", e=EXPERTS)))
            for e in range(EXPERTS):
                link(nc.vector.tensor_tensor_scan(cum[:, e, :], ones[:], tot[:, e, :], 0.0, ALU.mult, ALU.add))
            link(nc.vector.tensor_scalar(cnt[:], cum[:, :, BLOCKS - 1], float(P - 1), None, ALU.add))
            link(nc.vector.tensor_copy(cnt_i[:], cnt[:]))
            link(nc.vector.tensor_single_scalar(cnt_i[:], cnt_i[:], 7, ALU.arith_shift_right))
            link(nc.vector.tensor_copy(tiles[:], cnt_i[:]))
            link(nc.vector.tensor_tensor_scan(ends[:], ones[:, 0:EXPERTS], tiles[:], 0.0, ALU.mult, ALU.add))
            link(nc.vector.tensor_tensor(begin[:], ends[:], tiles[:], ALU.subtract))
            link(nc.vector.tensor_scalar(begin[:], begin[:], float(P), None, ALU.mult))
            link(nc.vector.tensor_tensor(cum[:], cum[:], tot[:], ALU.subtract))
            link(nc.vector.tensor_tensor(inner[:], inner[:], cum[:].rearrange("p e b -> p b e"), ALU.add))
            link(nc.vector.tensor_tensor(inner[:], inner[:], bc(begin[:, None, :], [P, BLOCKS, EXPERTS]), ALU.add))
            for c in range(2):
                link(nc.vector.tensor_tensor(hot[:, c], hot[:, c], inner[:], ALU.mult))
                link(nc.vector.tensor_reduce(slot_f[:, c, :], hot[:, c], AX.X, ALU.add))
            nc.vector.tensor_copy(k.slot[:], slot_f[:]).then_inc(slots_ready, 1)
            link(nc.vector.tensor_tensor(le[:], bc(ends[0:1, None, 0:EXPERTS - 1], [1, TOKEN_TILES, EXPERTS - 1]),
                                         bc(k.lane_f[0:1, 0:TOKEN_TILES, None], [1, TOKEN_TILES, EXPERTS - 1]), ALU.is_le))
            link(nc.vector.tensor_reduce(te[:], le[:], AX.X, ALU.add))
            nc.vector.tensor_copy(k.tile_expert[:], te[:])
            dve.wait_ge(list_in, 16)
            nc.vector.tensor_copy(lst_f[:], lst[:]).then_inc(lst_ready, 1)
            dve.wait_ge(lst_t, 1)
            nc.vector.tensor_copy(k.slot_token[:], ps_l[:])

        @block.scalar
        def _(act):
            act.wait_ge(hot_ready, 1)
            nc.scalar.activation(ex[:], gap[:], ACT.Exp).then_inc(exp_done, 1)

        @block.tensor
        def _(pe):
            pe.wait_ge(hot_ready, 1)
            flat = both[:].rearrange("p b e -> p (b e)")
            nc.tensor.matmul(ps_in[:], k.tri[:], flat, start=True, stop=True)
            nc.tensor.matmul(ps_tot[:], k.ones[:], flat, start=True, stop=True).then_inc(pre_done, 1)
            pe.wait_ge(lst_ready, 1)
            nc.tensor.transpose(ps_l[:], lst_f[:], k.ident[0:TOKEN_TILES, 0:TOKEN_TILES]).then_inc(lst_t, 1)

        @block.sync
        def _(sp):
            sp.wait_ge(zero_set, 1)
            sp.dma_start(slot_list.rearrange("(t p) o -> t (p o)", p=P), zero[:]).then_inc(zeroed, 16)
            sp.wait_ge(zeroed, 16)
            for i in range(2 * U):
                sp.wait_ge(put[i], 16 * TURNS)
            sp.dma_start(lst[:], slot_list.rearrange("(t p) o -> t (p o)", p=P)).then_inc(list_in, 16)
            sp.wait_ge(list_in, 16)

        @block.gpsimd
        def _(pool):
            pool.wait_ge(zeroed, 16)
            pool.wait_ge(slots_ready, 1)

            def turn(n, first=False):
                if not first:
                    for i in range(2 * U):
                        pool.wait_ge(put[i], 16 * n)
                nc.gpsimd.tensor_copy(stage[:], k.slot[:, :, bass.ds(n * U, U)]).then_inc(staged, 1)
                nc.gpsimd.tensor_copy(stage_id[:], k.token_id[:, bass.ds(n * U, U)]).then_inc(staged, 1)
                pool.wait_ge(staged, n * 2 + 2)
                hold_waits(k, nc.gpsimd)
                for c in range(2):
                    for u in range(U):
                        pool.indirect_dma_start(
                            out=slot_list, out_offset=bass.IndirectOffsetOnAxis(ap=stage[:, c, u:u + 1], axis=0),
                            in_=stage_id[:, u:u + 1], in_offset=None).then_inc(put[c * U + u], 16)
            turn(0, first=True)
            with nc.gpsimd.Fori(1, TURNS) as n:
                turn(n)
            for i in range(2 * U):
                pool.wait_ge(put[i], 16 * TURNS)


def build_expert_weights(k, kst):
    nc = k.nc
    own = lambda name, shape, dt: kst.enter_context(nc.sbuf_tensor(name, shape, dt))
    k.w1 = own("w1", [P, EXPERTS, 2, KF, HIDDEN], fp16)
    k.w2 = own("w2", [P, EXPERTS, 2, HB, D], fp16)
    k.b1 = own("b1", [P, EXPERTS * HB], fp32)
    k.b2 = own("b2", [P, EXPERTS, D], fp32)
    W = KF * HIDDEN
    assert W == HB * D
    with ExitStack() as st:
        sb, pb, sem = local(nc, st)
        raw = sb("w_raw", [P, W], fp32)
        scaled = sb("w_scaled", [P, W], fp32)
        g = sb("w_g", [P, EXPERTS, KF], fp32)
        beta = sb("w_beta", [P, EXPERTS, KF], fp32)
        b1_raw = sb("w_b1", [P, EXPERTS * HB], fp32)
        ps_b = pb("wp_b", [P, EXPERTS * HB], fp32)
        small_in, g_ready, raw_in, raw_used, s, hi, lo = (
            sem("w_" + x) for x in ("small_in", "g_ready", "raw_in", "raw_used", "s", "hi", "lo"))
        block = st.enter_context(nc.Block())

        @block.sync
        def _(sp):
            with nc.allow_non_contiguous_dma(reason="small per-feature vectors"):
                for e in range(EXPERTS):
                    sp.dma_start(g[:, e, :], k.io["L0_ffn_ln_g"][e].rearrange("(c p) -> p c", p=P)).then_inc(small_in, 16)
                    sp.dma_start(beta[:, e, :], k.io["L0_ffn_ln_b"][e].rearrange("(c p) -> p c", p=P)).then_inc(small_in, 16)
                    sp.dma_start(b1_raw[:, e * HB:(e + 1) * HB],
                                 k.io["L0_ffn_b1"][e].rearrange("(c p) -> p c", p=P)).then_inc(small_in, 16)
                sp.dma_start(k.b2[:], k.io["L0_ffn_b2"][None, :, :].to_broadcast([P, EXPERTS, D])).then_inc(small_in, 16)
            for i in range(2 * EXPERTS):
                e = i // 2
                if i:
                    sp.wait_ge(raw_used, i)
                src = (k.io["L0_ffn_W1"][e].rearrange("(c p) n -> p c n", p=P) if i % 2 == 0 else
                       k.io["L0_ffn_W2"][e].rearrange("(c p) n -> p c n", p=P))
                sp.dma_start(raw[:].rearrange("p (c n) -> p c n", n=HIDDEN if i % 2 == 0 else D), src).then_inc(raw_in, 16)
            sp.wait_ge(small_in, 16 * (3 * EXPERTS + 1))
            sp.wait_ge(raw_in, 32 * EXPERTS)

        @block.vector
        def _(dve):
            dve.wait_ge(small_in, 16 * (3 * EXPERTS + 1))
            nc.vector.tensor_scalar(g[:], g[:], SCALE, None, ALU.mult).then_inc(g_ready, 1)
            dve.wait_ge(g_ready, 1)
            for i in range(2 * EXPERTS):
                e = i // 2
                dve.wait_ge(raw_in, 16 * (i + 1))
                if i:
                    dve.wait_ge(lo, i)
                    dve.wait_ge(hi, i)
                if i % 2 == 0:
                    for c in range(KF):
                        mm = nc.vector.tensor_scalar(scaled[:, c * HIDDEN:(c + 1) * HIDDEN], raw[:, c * HIDDEN:(c + 1) * HIDDEN],
                                                     g[:, e, c:c + 1], None, ALU.mult)
                else:
                    mm = nc.vector.tensor_scalar(scaled[:], raw[:], SCALE, None, ALU.mult)
                mm.then_inc(s, 1)
                dve.wait_ge(hi, i + 1)
                w = k.w1 if i % 2 == 0 else k.w2
                nc.vector.tensor_tensor(w[:, e, 1].rearrange("p c n -> p (c n)"), scaled[:],
                                        w[:, e, 0].rearrange("p c n -> p (c n)"), ALU.subtract).then_inc(lo, 1)
            dve.wait_ge(raw_used, 2 * EXPERTS - 1)
            nc.vector.tensor_tensor(k.b1[:], ps_b[:], b1_raw[:], ALU.add)

        @block.scalar
        def _(act):
            for i in range(2 * EXPERTS):
                e = i // 2
                act.wait_ge(s, i + 1)
                w = k.w1 if i % 2 == 0 else k.w2
                nc.scalar.activation(w[:, e, 0].rearrange("p c n -> p (c n)"), scaled[:], ACT.Copy).then_inc(hi, 1)

        @block.tensor
        def _(pe):
            pe.wait_ge(small_in, 16 * (3 * EXPERTS + 1))
            for i in range(2 * EXPERTS):
                e = i // 2
                pe.wait_ge(raw_in, 16 * (i + 1))
                pe.wait_ge(s, i + 1)
                if i % 2:
                    nc.tensor.nop().then_inc(raw_used, 1)
                    continue
                for h in range(HB):
                    for c in range(KF):
                        mm = nc.tensor.matmul(ps_b[:, e * HB + h:e * HB + h + 1],
                                              raw[:, c * HIDDEN + h * P:c * HIDDEN + (h + 1) * P], beta[:, e, c:c + 1],
                                              start=c == 0, stop=c == KF - 1)
                mm.then_inc(raw_used, 1)


def build_experts(k):
    nc = k.nc
    k.y_rows = k.dr("y_rows", [SLOTS, D], fp32)
    PAIRS = ((0, 0), (0, 1), (1, 0))
    with ExitStack() as st:
        sb, pb, sem = local(nc, st)
        stage = sb("f_stage", [P, M], i32)
        xg = sb("f_xg", [P, M, D], fp32)
        xt = sb("f_xt", [P, 2, 2, D], fp16)
        h32 = sb("f_h32", [P, 2, HIDDEN], fp32)
        hh = sb("f_hh", [P, 2, 2, HIDDEN], fp16)
        y = sb("f_y", [P, M, D], fp32)
        ps_x = [pb(f"fp_x{i}", [P, D], fp32) for i in range(2)]
        ps_h = [pb(f"fp_h{i}", [P, HIDDEN], fp32) for i in range(2)]
        ps_y = [pb(f"fp_y{i}", [P, D], fp32) for i in range(2)]
        got = [sem(f"f_got{i}") for i in range(M)]
        stored = [sem(f"f_stored{i}") for i in range(M)]
        staged, x_t, x_hi, x_lo, up, act_done, h_hi, h_lo, down, y_ready = (
            sem("f_" + x) for x in ("staged", "x_t", "x_hi", "x_lo", "up", "act", "h_hi", "h_lo", "down", "y_ready"))
        block = st.enter_context(nc.Block())
        PT = TILE_TURNS // 2

        def experts(eng, regs, n):
            eng.load(regs, k.tile_expert[0:1, bass.ds(n * M, M)])
            return [eng.snap(r, min_val=0, max_val=EXPERTS - 1) for r in regs]

        def every(eng, turn):
            turn(0, 0, True)
            with eng.Fori(0, PT) as n:
                turn(2 * n + 1, M % 2, False)
                turn(2 * n + 2, 0, False)

        assert TILE_TURNS % 2 == 1 and M % 2 == 1

        @block.gpsimd
        def _(pool):
            def turn(n, par, first):
                if not first:
                    for m in range(M):
                        pool.wait_ge(got[m], 16 * n)
                    pool.wait_ge(x_t, n * M)
                nc.gpsimd.tensor_copy(stage[:], k.slot_token[:, bass.ds(n * M, M)]).then_inc(staged, 1)
                pool.wait_ge(staged, n + 1)
                hold_waits(k, nc.gpsimd)
                for m in range(M):
                    pool.indirect_dma_start(
                        out=xg[:, m, :], out_offset=None, in_=k.xn_rows,
                        in_offset=bass.IndirectOffsetOnAxis(ap=stage[:, m:m + 1], axis=0)).then_inc(got[m], 16)
            every(nc.gpsimd, turn)

        @block.tensor
        def _(pe):
            regs = [nc.tensor.alloc_register(f"f_pe{m}") for m in range(M)]

            def transposes(n, m, par, first):
                q = (par + m) % 2
                pe.wait_ge(got[m], 16 * (n + 1))
                if not (first and m < 2):
                    pe.wait_ge(x_hi, n * M + (m - 1))
                    pe.wait_ge(x_lo, n * M + (m - 1))
                for c in range(KF):
                    mm = nc.tensor.transpose(ps_x[q][:, c * P:(c + 1) * P], xg[:, m, c * P:(c + 1) * P], k.ident[:])
                mm.then_inc(x_t, 1)

            def turn(n, par, first):
                ex = experts(nc.tensor, regs, n)
                for m in range(M):
                    q = (par + m) % 2
                    transposes(n, m, par, first)
                    pe.wait_ge(x_hi, n * M + m + 1)
                    pe.wait_ge(x_lo, n * M + m + 1)
                    if not (first and m < 2):
                        pe.wait_ge(act_done, n * M + (m - 1))
                    for h in range(HB):
                        i = 0
                        for wh, xh in PAIRS:
                            for c in range(KF):
                                w = k.w1[:, bass.ds(ex[m], 1), wh, c, h * P:(h + 1) * P][:, 0, :]
                                mm = nc.tensor.matmul(ps_h[q][:, h * P:(h + 1) * P], w,
                                                      xt[:, q, xh, c * P:(c + 1) * P], start=i == 0, stop=i == 5)
                                i += 1
                    mm.then_inc(up, 1)
                    if not (first and m < 2):
                        pe.wait_ge(y_ready, n * M + (m - 1))
                    pe.wait_ge(h_hi, n * M + m + 1)
                    pe.wait_ge(h_lo, n * M + m + 1)
                    i = 0
                    for h in range(HB):
                        for wh, xh in PAIRS:
                            w = k.w2[:, bass.ds(ex[m], 1), wh, h, :][:, 0, :]
                            mm = nc.tensor.matmul(ps_y[q][:], hh[:, q, xh, h * P:(h + 1) * P], w,
                                                  start=i == 0, stop=i == 3 * HB - 1)
                            i += 1
                    mm.then_inc(down, 1)
            every(nc.tensor, turn)

        @block.scalar
        def _(act):
            regs = [nc.scalar.alloc_register(f"f_act{m}") for m in range(M)]

            def turn(n, par, first):
                ex = experts(nc.scalar, regs, n)
                for m in range(M):
                    q = (par + m) % 2
                    act.wait_ge(x_t, n * M + m + 1)
                    if not (first and m < 2):
                        act.wait_ge(up, n * M + (m - 1))
                    nc.scalar.activation(xt[:, q, 0, :], ps_x[q][:], ACT.Copy).then_inc(x_hi, 1)
                    act.wait_ge(up, n * M + m + 1)
                    if not (first and m < 2):
                        act.wait_ge(h_lo, n * M + (m - 1))
                        act.wait_ge(h_hi, n * M + (m - 1))
                    for h in range(HB):
                        a = nc.scalar.activation(h32[:, q, h * P:(h + 1) * P], ps_h[q][:, h * P:(h + 1) * P], ACT.Gelu,
                                                 bias=k.b1[:, bass.ds(ex[m] * HB + h, 1)], scale=1.0 / SCALE)
                    a.then_inc(act_done, 1)
            every(nc.scalar, turn)

        @block.vector
        def _(dve):
            regs = [nc.vector.alloc_register(f"f_dve{m}") for m in range(M)]

            def turn(n, par, first):
                ex = experts(nc.vector, regs, n)
                for m in range(M):
                    q = (par + m) % 2
                    dve.wait_ge(x_hi, n * M + m + 1)
                    nc.vector.tensor_tensor(xt[:, q, 1, :], ps_x[q][:], xt[:, q, 0, :], ALU.subtract).then_inc(x_lo, 1)
                    dve.wait_ge(act_done, n * M + m + 1)
                    if not (first and m < 2):
                        dve.wait_ge(down, n * M + (m - 1))
                    nc.vector.tensor_copy(hh[:, q, 0, :], h32[:, q, :]).then_inc(h_hi, 1)
                    dve.wait_ge(h_hi, n * M + m + 1)
                    nc.vector.tensor_tensor(hh[:, q, 1, :], h32[:, q, :], hh[:, q, 0, :], ALU.subtract).then_inc(h_lo, 1)
                    dve.wait_ge(down, n * M + m + 1)
                    if not first:
                        dve.wait_ge(stored[m], n * 16)
                    nc.vector.scalar_tensor_tensor(y[:, m, :], ps_y[q][:], 1.0 / SCALE,
                                                   k.b2[:, bass.ds(ex[m], 1), :][:, 0, :], ALU.mult,
                                                   ALU.add).then_inc(y_ready, 1)
            every(nc.vector, turn)

        @block.sync
        def _(sp):
            def turn(n, par, first):
                for m in range(M):
                    sp.wait_ge(y_ready, n * M + m + 1)
                    sp.dma_start(k.y_rows[bass.ds((n * M + m) * P, P), :], y[:, m, :]).then_inc(stored[m], 16)
            every(nc.sync, turn)
            for m in range(M):
                sp.wait_ge(stored[m], 16 * TILE_TURNS)


def build_combine(k):
    nc = k.nc
    with ExitStack() as st:
        sb, pb, sem = local(nc, st)
        stage = sb("z_stage", [P, 2, U], i32)
        rows = sb("z_rows", [P, 2, U, D], fp32)
        got = [sem(f"z_got{i}") for i in range(2 * U)]
        x2 = sb("z_x2", [P, U, D], fp32)
        x2_in = [sem(f"z_x2_in{u}") for u in range(U)]
        staged, first_done, ready = sem("z_staged"), sem("z_first"), sem("z_ready")
        stored = [sem(f"z_stored{u}") for u in range(U)]
        block = st.enter_context(nc.Block())

        @block.scalar
        def _(act):
            def turn(n, first=False):
                for u in range(U):
                    if not first:
                        act.wait_ge(stored[u], 16 * n)
                    act.dma_start(x2[:, u, :], k.x2_rows[bass.ds((n * U + u) * P, P), :]).then_inc(x2_in[u], 16)
            turn(0, first=True)
            with nc.scalar.Fori(1, TURNS) as n:
                turn(n)

        @block.gpsimd
        def _(pool):
            def turn(n, first=False):
                if not first:
                    for i in range(2 * U):
                        pool.wait_ge(got[i], 16 * n)
                    pool.wait_ge(ready, n * U)
                nc.gpsimd.tensor_copy(stage[:], k.slot[:, :, bass.ds(n * U, U)]).then_inc(staged, 1)
                pool.wait_ge(staged, n + 1)
                hold_waits(k, nc.gpsimd)
                for u in range(U):
                    for c in range(2):
                        pool.indirect_dma_start(
                            out=rows[:, c, u, :], out_offset=None, in_=k.y_rows,
                            in_offset=bass.IndirectOffsetOnAxis(ap=stage[:, c, u:u + 1], axis=0)).then_inc(got[c * U + u], 16)
            turn(0, first=True)
            with nc.gpsimd.Fori(1, TURNS) as n:
                turn(n)

        @block.vector
        def _(dve):
            def turn(n):
                for c, done in ((0, first_done), (1, ready)):
                    for u in range(U):
                        a = x2[:, u, :]
                        dve.wait_ge(got[c * U + u], 16 * (n + 1))
                        dve.wait_ge(x2_in[u], 16 * (n + 1))
                        if c:
                            dve.wait_ge(first_done, n * U + u + 1)
                        nc.vector.scalar_tensor_tensor(a, rows[:, c, u, :], k.gate[:, c, bass.ds(n * U + u, 1)], a,
                                                       ALU.mult, ALU.add).then_inc(done, 1)
            with nc.vector.Fori(0, TURNS) as n:
                turn(n)

        @block.sync
        def _(sp):
            def turn(n):
                for u in range(U):
                    sp.wait_ge(ready, n * U + u + 1)
                    sp.dma_start(k.io["out"][bass.ds((n * U + u) * P, P), :], x2[:, u, :]).then_inc(stored[u], 16)
            with nc.sync.Fori(0, TURNS) as n:
                turn(n)
            for u in range(U):
                sp.wait_ge(stored[u], 16 * TURNS)


def build(nc, io):
    with ExitStack() as ctx:
        k = Kernel(nc, ctx, io)
        with ExitStack() as ast:
            build_constants(k, ast)
            with ExitStack() as gst:
                build_edge_tables(k, gst)
                build_project(k, "p1", "L0_gnn_W1", None)
                build_aggregate(k, "a1")
                build_project(k, "p2", "L0_gnn_W2", "L0_gnn_b1")
                build_aggregate(k, "a2")
            build_tokens(k)
        build_routing(k)
        with ExitStack() as kst:
            build_expert_weights(k, kst)
            build_experts(k)
        build_combine(k)


_INS = ["x", "src", "dst", "L0_gnn_W1", "L0_gnn_b1", "L0_gnn_W2", "L0_gnn_b2", "L0_ffn_Wr", "L0_ffn_br",
        "L0_ffn_ln_g", "L0_ffn_ln_b", "L0_ffn_W1", "L0_ffn_b1", "L0_ffn_W2", "L0_ffn_b2"]


def kernel(**inputs):
    import numpy as _np
    import concourse.bacc as _bacc
    from concourse import mybir as _mybir
    from concourse.bass_utils import run_bass_kernel_spmd as _run

    arrays = {n: _np.ascontiguousarray(inputs[n]) for n in _INS}
    arrays["x"] = _np.concatenate([arrays["x"], _np.zeros((PAD_NODES - NODES, D), arrays["x"].dtype)])
    pad = EDGE_TILES * P - EDGES
    arrays["src"] = _np.concatenate([arrays["src"], _np.zeros(pad, arrays["src"].dtype)])
    arrays["dst"] = _np.concatenate([arrays["dst"], _np.full(pad, PAD_NODES, arrays["dst"].dtype)])
    nc = _bacc.Bacc("TRN2", target_bir_lowering=False, num_devices=1)
    io, ins = {}, {}
    for n, a in arrays.items():
        ins[f"in_{n}_dram"] = a
        io[n] = nc.dram_tensor(f"in_{n}_dram", a.shape, _mybir.dt.from_np(a.dtype), kind="ExternalInput").ap()
    io["out"] = nc.dram_tensor("out_0_dram", (PAD_NODES, D), _mybir.dt.float32, kind="ExternalOutput").ap()
    build(nc, io)
    r = _run(nc, [ins], core_ids=[0])
    return r.results[0]["out_0_dram"][:NODES]
```

```python
from contextlib import ExitStack

import concourse.bass as bass
from concourse import mybir

P = 128
D = 256
KF = D // P
NODES = 6250
BLOCKS = -(-NODES // P)
PAD_NODES = BLOCKS * P
ROWS = PAD_NODES + P
EDGES = 206250
EDGE_TILES = -(-EDGES // P)
WIN = 8
WINS = PAD_NODES // WIN
BLOCK_WINS = P // WIN
CELLS = WIN * BLOCKS
ITEMS = EDGES // P + WINS
ITEM_COLS = -(-ITEMS // P)
EXPERTS = 8
HIDDEN = 1024
HB = HIDDEN // P
TOKEN_TILES = (2 * PAD_NODES + EXPERTS * (P - 1)) // P
SLOTS = TOKEN_TILES * P
EPS = 1e-5
SCALE = 64.0

fp32 = mybir.dt.float32
fp16 = mybir.dt.float16
bf16 = mybir.dt.bfloat16
i32 = mybir.dt.int32
u16 = mybir.dt.uint16
ALU = mybir.AluOpType
ACT = mybir.ActivationFunctionType
AX = mybir.AxisListType

GRP = 13
GROUPS = EDGE_TILES // GRP
HRING = 4
HTURNS = GROUPS // HRING
BANK = 512
RING = 4
U = 7
TURNS = BLOCKS // U
R = 20
G = 5
GS = R // G
ADJ_TURNS = -(-ITEMS // R)
ADJ_ITEMS = ADJ_TURNS * R
PLAN = R + GS
BANKS = 8
COUNT_SCALE = 0.25
M = 5
TILE_TURNS = TOKEN_TILES // M
LN_STEPS = 2 * U + 1
assert GROUPS * GRP == EDGE_TILES and HTURNS * HRING == GROUPS and TURNS * U == BLOCKS
assert GS * G == R and G < BANKS and ADJ_ITEMS <= ITEM_COLS * P and TILE_TURNS * M == TOKEN_TILES


class Kernel:

    def __init__(self, nc, ctx, dram):
        self.nc, self.ctx, self.io = nc, ctx, dram

    def sb(self, name, shape, dt):
        return self.ctx.enter_context(self.nc.sbuf_tensor(name, shape, dt))

    def dr(self, name, shape, dt):
        return self.nc.dram_tensor(name, shape, dt, kind="Internal").ap()


def local(nc, st):
    def banks(name, shape, dt):
        n = -(-shape[1] // BANK) * BANK
        return st.enter_context(nc.psum_tensor(name, [P, n], dt))[0:shape[0], 0:shape[1]]

    sems = []

    def sem(name):
        sems.append(nc.alloc_semaphore(name))
        return sems[-1]

    def give_back():
        nc.clear_and_free_semaphores(sems)
        nc.all_engine_barrier()

    st.callback(give_back)
    return lambda name, shape, dt: st.enter_context(nc.sbuf_tensor(name, shape, dt)), banks, sem


def hold_waits(k, eng, place=0):
    if eng is k.nc.gpsimd:
        last = k.held_pool[:, M + 2:M + 3]
        eng.tensor_tensor(k.held_pool[:, place:place + 1], last, last, ALU.add)
    else:
        eng.memset(k.held_dve[:], 0.0)


def since(u):
    return RING if u >= RING else U - max(v for v in range(U) if v % RING == u)


def bc(ap, shape):
    return ap.to_broadcast(shape)


def build_constants(k):
    nc = k.nc
    k.ident = k.sb("ident", [P, P], fp32)
    k.ones = k.sb("ones", [P, P], fp32)
    k.held_pool = k.sb("held_pool", [1, M + 3], fp32)
    k.held_act = k.sb("held_act", [P, 1], fp32)
    k.self_loop = k.sb("self_loop", [P, P], fp16)
    k.held_dve = k.sb("held_dve", [1, 1], fp32)
    k.eps = k.sb("eps", [P, 1], fp32)
    k.tri = k.sb("tri", [P, P], fp32)
    k.lane_h = k.sb("lane_h", [P, P], fp16)
    k.lane_b = k.sb("lane_b", [P, P], bf16)
    k.lane_f = k.sb("lane_f", [P, P], fp32)
    k.item_id = k.sb("item_id", [P, ITEM_COLS], fp32)
    k.token_id = k.sb("token_id", [P, BLOCKS], i32)
    k.dinv_in = k.sb("dinv_in", [P, BLOCKS], fp32)
    k.dinv_out = k.sb("dinv_out", [P, BLOCKS], fp32)
    k.logits = k.sb("logits", [P, BLOCKS, EXPERTS], fp32)
    k.gate = k.sb("gate", [P, 2, BLOCKS], fp32)
    k.slot_gate = k.sb("slot_gate", [P, TOKEN_TILES], fp32)
    k.slot = k.sb("slot", [P, 2, BLOCKS], i32)
    k.slot_token = k.sb("slot_token", [P, TOKEN_TILES], i32)
    k.tile_expert = k.sb("tile_expert", [1, 1 + TOKEN_TILES], i32)
    k.adj = k.dr("adj", [BLOCKS, P, BLOCKS * P], fp16)
    with ExitStack() as st:
        sb, pb, sem = local(nc, st)
        ints = sb("c_ints", [P, P], i32)
        item_i = sb("c_item_i", [P, ITEM_COLS], i32)
        io_done, ones_done = sem("c_iota"), sem("c_ones")
        block = st.enter_context(nc.Block())

        @block.gpsimd
        def _(pool):
            nc.gpsimd.iota(ints[:], pattern=[[1, P]], base=0, channel_multiplier=0).then_inc(io_done, 1)
            nc.gpsimd.iota(item_i[:], pattern=[[P, ITEM_COLS]], base=0, channel_multiplier=1).then_inc(io_done, 1)
            nc.gpsimd.iota(k.token_id[:], pattern=[[P, BLOCKS]], base=0, channel_multiplier=1).then_inc(io_done, 1)
            pool.wait_ge(ones_done, 1)
            nc.gpsimd.affine_select(out=k.ident[:], in_=k.ones[:], compare_op=ALU.is_equal, fill=0.0, base=0,
                                    pattern=[[-1, P]], channel_multiplier=1).then_inc(io_done, 1)
            nc.gpsimd.affine_select(out=k.tri[:], in_=k.ones[:], compare_op=ALU.is_gt, fill=0.0, base=0,
                                    pattern=[[1, P]], channel_multiplier=-1)

        @block.vector
        def _(dve):
            nc.vector.memset(k.ones[:], 1.0).then_inc(ones_done, 1)
            nc.vector.memset(k.eps[:], EPS)
            nc.vector.memset(k.held_pool[:], 0.0)
            dve.wait_ge(io_done, 4)
            nc.vector.tensor_scalar(k.self_loop[:], k.ident[:], COUNT_SCALE, None, ALU.mult)
            nc.vector.tensor_copy(k.lane_h[:], ints[:])
            nc.vector.tensor_copy(k.lane_b[:], ints[:])
            nc.vector.tensor_copy(k.lane_f[:], ints[:])
            nc.vector.tensor_copy(k.item_id[:], item_i[:])


def in_pairs(eng, total, turn):
    peeled = 2 + total % 2
    for i in range(peeled):
        turn(i, i % 2, i // 2 + 1, i < 2)
    with eng.Fori(0, (total - peeled) // 2) as n:
        if peeled == 3:
            turn(2 * n + 3, 1, n + 2, False)
            turn(2 * n + 4, 0, n + 3, False)
        else:
            turn(2 * n + 2, 0, n + 2, False)
            turn(2 * n + 3, 1, n + 2, False)


def build_edge_tables(k, gst):
    nc = k.nc
    own = lambda name, shape, dt: gst.enter_context(nc.sbuf_tensor(name, shape, dt))
    k.edge_cell = own("edge_cell", [P, ITEM_COLS * P], fp32)
    k.edge_lane = own("edge_lane", [P, ITEM_COLS * P], bf16)
    k.plan = own("plan", [1, ADJ_TURNS * PLAN], u16)
    k.win_end = own("win_end", [1, WINS], u16)
    win_first = k.dr("win_first", [1, WINS], i32)
    win_row_d = k.dr("win_row_d", [ITEM_COLS, P], i32)
    with ExitStack() as st:
        sb, pb, sem = local(nc, st)
        dst = sb("t_dst", [P, EDGE_TILES], i32)
        part = sb("t_part", [P, EDGE_TILES], i32)
        hi = sb("t_hi", [P, EDGE_TILES], bf16)
        lo = sb("t_lo", [P, EDGE_TILES], bf16)
        oh_lo = sb("t_oh_lo", [P, HRING, GRP, P], bf16)
        oh_hi = sb("t_oh_hi", [P, HRING, GRP, BLOCKS], bf16)
        deg = sb("t_deg", [P, BLOCKS], fp32)
        tmp = sb("t_tmp", [P, BLOCKS], fp32)
        tot = sb("t_tot", [P, BLOCKS], fp32)
        cum = sb("t_cum", [P, BLOCKS], fp32)
        below = sb("t_below", [P, BLOCK_WINS], fp32)
        win_id = sb("t_win_id", [BLOCK_WINS, BLOCKS], i32)
        win_idf = sb("t_win_idf", [BLOCK_WINS, BLOCKS], fp32)
        first = sb("t_first", [BLOCK_WINS, BLOCKS], fp32)
        first_i = sb("t_first_i", [BLOCK_WINS, BLOCKS], i32)
        all_i = sb("t_all_i", [P, WINS], i32)
        all_f = sb("t_all_f", [P, WINS], fp32)
        le = sb("t_le", [P, WINS], fp32)
        win = sb("t_win", [P, ITEM_COLS], fp32)
        win8 = sb("t_win8", [P, ITEM_COLS], fp32)
        tile_f = sb("t_tile_f", [P, ITEM_COLS], fp32)
        tile_i = sb("t_tile_i", [P, ITEM_COLS], i32)
        win_t = sb("t_win_t", [ITEM_COLS, P], i32)
        win_row = sb("t_win_row", [1, ITEM_COLS * P], i32)
        bank_row = sb("t_bank_row", [1, ITEM_COLS * P], i32)
        rows_s = sb("t_rows_s", [P, 4, P], i32)
        rows_d = sb("t_rows_d", [P, 4, P], i32)
        rows_p = sb("t_rows_p", [P, 2, P], i32)
        rows_l = sb("t_rows_l", [P, 4, P], fp32)
        rows_h = sb("t_rows_h", [P, 4, P], fp32)
        rows_c = sb("t_rows_c", [P, 4, P], fp32)
        ps_deg = pb("tp_deg", [P, BLOCKS], fp32)
        ps_tot = pb("tp_tot", [P, BLOCKS], fp32)
        ps_win = pb("tp_win", [ITEM_COLS, P], fp32)
        ps_t = [pb(f"tp_t{i}", [P, P], fp32) for i in range(4)]
        ps_in = pb("tp_in", [BLOCK_WINS, BLOCKS], fp32)
        (dst_in, lo_done, hi_done, groups_done, step, consts, deg_ready, tot_done, root_done, first_ready, first_out,
         all_in, tile_ready, win_ready, win_t_done, win_t_ready, row_out, row_in, lane_ready, cell_ready,
         t_done, t_copied) = (sem("t_" + x) for x in (
             "dst_in", "lo", "hi", "groups", "step", "consts", "deg", "tot", "root", "first", "first_out", "all_in",
             "tile", "win", "win_t", "win_tr", "row_out", "row_in", "lane", "cell", "t_done", "t_copied"))
        got = [sem(f"t_got{i}") for i in range(4)]
        block = st.enter_context(nc.Block())

        @block.sync
        def _(sp):
            sp.dma_start(dst[:], k.io["dst"].rearrange("(p c) -> p c", p=P)).then_inc(dst_in, 16)
            sp.wait_ge(first_ready, 1)
            with nc.allow_non_contiguous_dma(reason="one number per window"):
                sp.dma_start(win_first[0].rearrange("(b m) -> m b", m=BLOCK_WINS), first_i[:]).then_inc(first_out, 16)
            sp.wait_ge(first_out, 16)
            sp.dma_start(all_i[:], win_first.to_broadcast([P, WINS])).then_inc(all_in, 16)
            sp.wait_ge(win_t_ready, 1)
            sp.dma_start(win_row_d, win_t[:]).then_inc(row_out, 16)
            sp.wait_ge(row_out, 16)
            sp.dma_start(win_row[:], win_row_d.rearrange("c p -> (c p)")[None, :]).then_inc(row_in, 16)
            sp.wait_ge(row_in, 16)

        @block.vector
        def _(dve):
            count = [0]

            def link(ins):
                count[0] += 1
                ins.then_inc(step, 1)
                dve.wait_ge(step, count[0])

            dve.wait_ge(dst_in, 16)
            link(nc.vector.tensor_single_scalar(part[:], dst[:], 7, ALU.arith_shift_right))
            link(nc.vector.tensor_copy(hi[:], part[:]))
            link(nc.vector.tensor_single_scalar(part[:], dst[:], P - 1, ALU.bitwise_and))
            link(nc.vector.tensor_copy(lo[:], part[:]))

            def one_hots(n):
                for r in range(HRING):
                    if not (isinstance(n, int) and n == 0):
                        dve.wait_ge(groups_done, n * HRING + (r + 1 - HRING))
                    nc.vector.tensor_tensor(
                        oh_lo[:, r], bc(k.lane_b[:, None, :], [P, GRP, P]),
                        bc(lo[:, bass.ds(n * (HRING * GRP) + r * GRP, GRP)][:, :, None], [P, GRP, P]),
                        ALU.is_equal).then_inc(lo_done, 1)
                    nc.vector.tensor_tensor(
                        oh_hi[:, r], bc(k.lane_b[:, None, 0:BLOCKS], [P, GRP, BLOCKS]),
                        bc(hi[:, bass.ds(n * (HRING * GRP) + r * GRP, GRP)][:, :, None], [P, GRP, BLOCKS]),
                        ALU.is_equal).then_inc(hi_done, 1)
            one_hots(0)
            with nc.vector.Fori(1, HTURNS) as n:
                one_hots(n)
            dve.wait_ge(groups_done, GROUPS)
            nc.vector.tensor_copy(deg[:], ps_deg[:]).then_inc(deg_ready, 1)
            dve.wait_ge(deg_ready, 1)
            nc.vector.tensor_scalar(tmp[:], deg[:], 1.0, None, ALU.add).then_inc(deg_ready, 1)
            dve.wait_ge(root_done, 1)
            link(nc.vector.reciprocal(cum[:], tot[:]))
            nc.vector.tensor_scalar(k.dinv_in[:], cum[:], SCALE, None, ALU.mult)
            link(nc.vector.tensor_scalar(k.dinv_out[:], cum[:], 1.0 / (SCALE * COUNT_SCALE), None, ALU.mult))
            dve.wait_ge(tot_done, 1)
            link(nc.vector.tensor_copy(tot[:], ps_tot[:]))
            link(nc.vector.memset(tmp[:], 1.0))
            link(nc.vector.tensor_tensor_scan(cum[:], tmp[:], tot[:], 0.0, ALU.mult, ALU.add))
            link(nc.vector.tensor_tensor(cum[:], cum[:], tot[:], ALU.subtract))
            link(nc.vector.tensor_tensor(first[:], cum[0:BLOCK_WINS, :], ps_in[:], ALU.add))
            link(nc.vector.tensor_copy(first_i[:], first[:]))
            link(nc.vector.tensor_single_scalar(first_i[:], first_i[:], 7, ALU.arith_shift_right))
            link(nc.vector.tensor_copy(first[:], first_i[:]))
            dve.wait_ge(consts, 3)
            link(nc.vector.tensor_copy(win_idf[:], win_id[:]))
            link(nc.vector.tensor_tensor(first[:], first[:], win_idf[:], ALU.add))
            nc.vector.tensor_copy(first_i[:], first[:]).then_inc(first_ready, 1)
            dve.wait_ge(all_in, 16)
            link(nc.vector.tensor_copy(all_f[:], all_i[:]))
            for c in range(ITEM_COLS):
                link(nc.vector.tensor_scalar(le[:], all_f[:], k.item_id[:, c:c + 1], None, ALU.is_le))
                link(nc.vector.tensor_reduce(win[:, c:c + 1], le[:], AX.X, ALU.add))
            link(nc.vector.tensor_scalar(win[:], win[:], -1.0, None, ALU.add))
            nc.vector.tensor_scalar(win8[:], win[:], float(WIN), None, ALU.mult).then_inc(win_ready, 1)
            link(nc.vector.tensor_tensor(tile_f[:], k.item_id[:], win[:], ALU.subtract))
            link(nc.vector.tensor_scalar(tile_f[:], tile_f[:], float(EDGE_TILES - 1), None, ALU.min))
            nc.vector.tensor_copy(tile_i[:], tile_f[:]).then_inc(tile_ready, 1)
            dve.wait_ge(win_t_done, 1)
            nc.vector.tensor_copy(win_t[:], ps_win[:]).then_inc(win_t_ready, 1)
            dve.wait_ge(win_ready, 1)
            for c in range(ITEM_COLS):
                s = c % 4
                dve.wait_ge(got[s], 32 * (c // 4 + 1))
                if c >= 4:
                    dve.wait_ge(t_done, 2 * (c - 3))
                link(nc.vector.tensor_single_scalar(rows_p[:, 0], rows_s[:, s], P - 1, ALU.bitwise_and))
                nc.vector.tensor_copy(rows_l[:, s], rows_p[:, 0]).then_inc(lane_ready, 1)
                link(nc.vector.tensor_single_scalar(rows_p[:, 1], rows_s[:, s], 7, ALU.arith_shift_right))
                link(nc.vector.tensor_copy(rows_h[:, s], rows_p[:, 1]))
                link(nc.vector.tensor_scalar(rows_c[:, s], rows_d[:, s], win8[:, c:c + 1], float(BLOCKS),
                                             ALU.subtract, ALU.mult))
                dve.wait_ge(lane_ready, c + 1)
                nc.vector.tensor_tensor(rows_c[:, s], rows_c[:, s], rows_h[:, s], ALU.add).then_inc(cell_ready, 1)
                dve.wait_ge(t_done, 2 * c + 2)
                dve.wait_ge(cell_ready, c + 1)
                nc.vector.tensor_copy(k.edge_lane[:, c * P:(c + 1) * P], ps_t[(2 * c) % 4][:]).then_inc(t_copied, 1)
                nc.vector.tensor_copy(k.edge_cell[:, c * P:(c + 1) * P], ps_t[(2 * c + 1) % 4][:]).then_inc(t_copied, 1)
            dve.wait_ge(row_in, 16)
            plan = k.plan[:].rearrange("o (n w) -> o n w", w=PLAN)
            items = lambda t: t[:, 0:ADJ_ITEMS].rearrange("o (n r) -> o n r", r=R)
            for g in range(GS):
                nc.vector.tensor_scalar(plan[:, :, R + g], items(win_row)[:, :, (g + 1) * G - 1], 1.0, None, ALU.add)
            link(nc.vector.tensor_scalar(bank_row[:], win_row[:], BANKS - 1, 9, ALU.bitwise_and, ALU.logical_shift_left))
            nc.vector.tensor_copy(plan[:, :, 0:R], items(bank_row))
            nc.vector.tensor_copy(k.win_end[:, 0:WINS - 1], all_i[0:1, 1:WINS])
            nc.vector.memset(k.win_end[:, WINS - 1:WINS], ADJ_ITEMS)
            dve.wait_ge(t_copied, 2 * ITEM_COLS)
            nc.vector.memset(k.edge_cell[:, ITEMS:], -1.0)

        @block.scalar
        def _(act):
            act.wait_ge(deg_ready, 2)
            nc.scalar.activation(tot[:], tmp[:], ACT.Sqrt).then_inc(root_done, 1)

        @block.gpsimd
        def _(pool):
            nc.gpsimd.memset(below[:], 1.0).then_inc(consts, 1)
            pool.wait_ge(consts, 1)
            nc.gpsimd.affine_select(out=below[:], in_=below[:], compare_op=ALU.is_gt, fill=0.0, base=0,
                                    pattern=[[WIN, BLOCK_WINS]], channel_multiplier=-1).then_inc(consts, 1)
            nc.gpsimd.iota(win_id[:], pattern=[[BLOCK_WINS, BLOCKS]], base=0, channel_multiplier=1).then_inc(consts, 1)
            pool.wait_ge(tile_ready, 1)
            for c in range(ITEM_COLS):
                if c >= 4:
                    pool.wait_ge(cell_ready, c - 3)
                for rows, name in ((rows_s, "src"), (rows_d, "dst")):
                    pool.indirect_dma_start(
                        out=rows[:, c % 4, :], out_offset=None, in_=k.io[name].rearrange("(t e) -> t e", e=P),
                        in_offset=bass.IndirectOffsetOnAxis(ap=tile_i[:, c:c + 1], axis=0)).then_inc(got[c % 4], 16)

        @block.tensor
        def _(pe):
            def group(n, first=False, last=False):
                for r in range(HRING):
                    pe.wait_ge(lo_done, n * HRING + r + 1)
                    pe.wait_ge(hi_done, n * HRING + r + 1)
                    for g in range(GRP):
                        mm = nc.tensor.matmul(ps_deg[:], oh_lo[:, r, g, :], oh_hi[:, r, g, :],
                                              start=first and r == 0 and g == 0,
                                              stop=last and r == HRING - 1 and g == GRP - 1)
                    mm.then_inc(groups_done, 1)
            group(0, first=True)
            with nc.tensor.Fori(1, HTURNS - 1) as n:
                group(n)
            group(HTURNS - 1, last=True)
            pe.wait_ge(deg_ready, 1)
            pe.wait_ge(consts, 2)
            nc.tensor.matmul(ps_in[:], below[:], deg[:], start=True, stop=True)
            nc.tensor.matmul(ps_tot[:], k.ones[:], deg[:], start=True, stop=True).then_inc(tot_done, 1)
            pe.wait_ge(win_ready, 1)
            nc.tensor.transpose(ps_win[:], win[:], k.ident[:]).then_inc(win_t_done, 1)
            for c in range(ITEM_COLS):
                for j, rows, ready in ((0, rows_l, lane_ready), (1, rows_c, cell_ready)):
                    pe.wait_ge(ready, c + 1)
                    if c >= 2:
                        pe.wait_ge(t_copied, 2 * c + j - 3)
                    nc.tensor.transpose(ps_t[(2 * c + j) % 4][:], rows[:, c % 4, :], k.ident[:]).then_inc(t_done, 1)


def build_input_rows(k):
    nc = k.nc
    with ExitStack() as st:
        sb, pb, sem = local(nc, st)
        w = sb("p_w", [P, KF, D], fp32)
        x = sb("p_x", [P, U, D], fp32)
        z = sb("p_z", [P, U, D], fp32)
        zt = sb("p_zt", [P, U, D], fp32)
        h = sb("p_h", [P, U, D], fp32)
        stats = sb("p_stats", [P, U, 6], fp32)
        mv = sb("p_mv", [P, U, 2], fp32)
        ps_t = [pb(f"pp_t{i}", [P, D], fp32) for i in range(RING)]
        ps_h = [pb(f"pp_h{i}", [P, D], fp32) for i in range(RING)]
        w_in, root, ln, z_ready, t_done, t_copied, h_done, scaled, hi_done, lo_done = (
            sem("p_" + s) for s in ("w_in", "root", "ln", "z_ready", "t_done", "t_copied", "h_done", "scaled",
                                    "hi_done", "lo_done"))
        x_in = [sem(f"p_x_in{u}") for u in range(U)]
        block = st.enter_context(nc.Block())

        @block.sync
        def _(sp):
            sp.dma_start(w[:], k.io["L0_gnn_W1"].rearrange("(c p) n -> p c n", p=P)).then_inc(w_in, 16)

            def turn(n, first=False):
                if not first:
                    sp.wait_ge(z_ready, n * U)
                for u in range(U):
                    sp.dma_start(x[:, u, :], k.io["x"][bass.ds((n * U + u) * P, P), :]).then_inc(x_in[u], 16)
            turn(0, first=True)
            with nc.sync.Fori(1, TURNS) as n:
                turn(n)

        @block.vector
        def _(dve):
            def turn(n, first=False):
                if not first:
                    dve.wait_ge(t_done, n * U)
                for u in range(U):
                    dve.wait_ge(x_in[u], n * 16 + 16)
                hold_waits(k, nc.vector)
                for u in range(U):
                    nc.vector.bn_stats(stats[:, u, :], x[:, u, :]).then_inc(ln, 1)
                dve.wait_ge(ln, n * LN_STEPS + U)
                hold_waits(k, nc.vector)
                for u in range(U):
                    nc.vector.bn_aggr(mv[:, u, :], stats[:, u, :]).then_inc(ln, 1)
                dve.wait_ge(root, n + 1)
                nc.vector.reciprocal(mv[:, :, 1], mv[:, :, 1]).then_inc(ln, 1)
                dve.wait_ge(ln, n * LN_STEPS + LN_STEPS)
                for u in range(U):
                    nc.vector.tensor_scalar(z[:, u, :], x[:, u, :], mv[:, u, 0:1], mv[:, u, 1:2],
                                            ALU.subtract, ALU.mult).then_inc(z_ready, 1)
                for u in range(U):
                    dve.wait_ge(h_done, n * U + u + 1)
                    if not first:
                        dve.wait_ge(hi_done, n * U + (u + 1 - U))
                        dve.wait_ge(lo_done, n * U + (u + 1 - U))
                    nc.vector.tensor_scalar(h[:, u, :], ps_h[u % RING], k.dinv_in[:, bass.ds(n * U + u, 1)], None,
                                            ALU.mult).then_inc(scaled, 1)
                for u in range(U):
                    dve.wait_ge(scaled, n * U + u + 1)
                    dve.wait_ge(hi_done, n * U + u + 1)
                    rows = k.rows[0][:, bass.ds(n * U + u, 1), :][:, 0, :]
                    nc.vector.tensor_tensor(rows[:, D:2 * D], h[:, u, :], rows[:, 0:D], ALU.subtract).then_inc(lo_done, 1)
            turn(0, first=True)
            with nc.vector.Fori(1, TURNS) as n:
                turn(n)

        @block.scalar
        def _(act):
            def turn(n, first=False):
                act.wait_ge(ln, n * LN_STEPS + 2 * U)
                nc.scalar.activation(mv[:, :, 1], mv[:, :, 1], ACT.Sqrt, bias=k.eps[:]).then_inc(root, 1)
                for u in range(U):
                    act.wait_ge(t_done, n * U + u + 1)
                    if not first:
                        act.wait_ge(h_done, n * U + (u + 1 - U))
                    nc.scalar.activation(zt[:, u, :], ps_t[u % RING], ACT.Copy).then_inc(t_copied, 1)
                for u in range(U):
                    act.wait_ge(scaled, n * U + u + 1)
                    nc.scalar.activation(k.rows[0][:, bass.ds(n * U + u, 1), 0:D][:, 0, :], h[:, u, :],
                                         ACT.Copy).then_inc(hi_done, 1)
            turn(0, first=True)
            with nc.scalar.Fori(1, TURNS) as n:
                turn(n)

        @block.tensor
        def _(pe):
            pe.wait_ge(w_in, 16)

            def turn(n, first=False):
                for u in range(U):
                    pe.wait_ge(z_ready, n * U + u + 1)
                    if not (first and u < RING):
                        pe.wait_ge(t_copied, n * U + (u + 1 - since(u)))
                    for c in range(KF):
                        mm = nc.tensor.transpose(ps_t[u % RING][:, c * P:(c + 1) * P], z[:, u, c * P:(c + 1) * P], k.ident[:])
                    mm.then_inc(t_done, 1)
                for u in range(U):
                    pe.wait_ge(t_copied, n * U + u + 1)
                    if not (first and u < RING):
                        pe.wait_ge(scaled, n * U + (u + 1 - since(u)))
                    for c in range(KF):
                        mm = nc.tensor.matmul(ps_h[u % RING], zt[:, u, c * P:(c + 1) * P], w[:, c, :],
                                              start=c == 0, stop=c == KF - 1)
                    mm.then_inc(h_done, 1)
            turn(0, first=True)
            with nc.tensor.Fori(1, TURNS) as n:
                turn(n)


def build_adjacency(k):
    nc = k.nc
    with ExitStack() as st:
        sb, pb, sem = local(nc, st)
        cells = sb("j_cells", [P, CELLS], fp16)
        cells_i = sb("j_cells_i", [P, CELLS], i32)
        oh_lane = sb("j_oh_lane", [P, 2, R, P], fp16)
        oh_cell = sb("j_oh_cell", [P, 2, R, CELLS], fp16)
        zeros = sb("j_zeros", [P, CELLS], fp16)
        counts = sb("j_counts", [P, 2, BLOCKS, P], fp16)
        ps = st.enter_context(nc.psum_tensor("jp", [P, BANKS * BANK], fp32))
        iota_done, cells_ready, lane_ready, cell_ready, item_done, emptied, zeroed, block_ready, zeros_set = (
            sem("j_" + x) for x in ("iota", "cells", "lane", "cell", "item", "emptied", "zeroed", "block", "zeros"))
        stored = [sem(f"j_stored{q}") for q in range(2)]
        block = st.enter_context(nc.Block())

        def bank(j):
            return ps[:, (j % BANKS) * BANK:(j % BANKS) * BANK + CELLS]

        @block.gpsimd
        def _(pool):
            nc.gpsimd.iota(cells_i[:], pattern=[[1, CELLS]], base=0, channel_multiplier=0).then_inc(iota_done, 1)
            nc.gpsimd.memset(zeros[:], 0.0).then_inc(zeros_set, 1)

        @block.vector
        def _(dve):
            dve.wait_ge(iota_done, 1)
            nc.vector.tensor_copy(cells[:], cells_i[:]).then_inc(cells_ready, 1)
            dve.wait_ge(cells_ready, 1)

            def turn(i, q, uses, first):
                for r in range(R):
                    if r % G == 0:
                        if not first:
                            dve.wait_ge(item_done, i * R + (r + G - 2 * R))
                        nc.vector.tensor_tensor(oh_lane[:, q, r:r + G], bc(k.lane_b[:, None, :], [P, G, P]),
                                                bc(k.edge_lane[:, bass.ds(i * R + r, G)][:, :, None], [P, G, P]),
                                                ALU.is_equal).then_inc(lane_ready, 1)
                    nc.vector.tensor_scalar(oh_cell[:, q, r, :], cells[:], k.edge_cell[:, bass.ds(i * R + r, 1)], None,
                                            ALU.is_equal).then_inc(cell_ready, 1)
            in_pairs(nc.vector, ADJ_TURNS, turn)

        @block.tensor
        def _(pe):
            regs = [nc.tensor.alloc_register(f"j_plan{m}") for m in range(PLAN)]

            def turn(i, q, uses, first):
                nc.tensor.load(regs, k.plan[0:1, bass.ds(i * PLAN, PLAN)])
                banks = [nc.tensor.snap(r, min_val=0, max_val=(BANKS - 1) * BANK) for r in regs[0:R]]
                begun = [nc.tensor.snap(r, min_val=1, max_val=WINS) for r in regs[R:]]
                for r in range(R):
                    if r % G == 0:
                        pe.wait_ge(lane_ready, i * GS + (r // G + 1))
                        pe.wait_ge(zeroed, begun[r // G])
                    pe.wait_ge(cell_ready, i * R + r + 1)
                    nc.tensor.matmul(ps[:, bass.ds(banks[r], CELLS)], oh_lane[:, q, r, :], oh_cell[:, q, r, :],
                                     start=False, stop=True, skip_group_check=True).then_inc(item_done, 1)
            in_pairs(nc.tensor, ADJ_TURNS, turn)

        @block.scalar
        def _(act):
            regs = [nc.scalar.alloc_register(f"j_end{m}") for m in range(BLOCK_WINS)]
            act.wait_ge(zeros_set, 1)
            for j in range(BANKS):
                nc.scalar.activation(bank(j), zeros[:], ACT.Copy).then_inc(zeroed, 1)

            def turn(i, q, uses, first):
                nc.scalar.load(regs, k.win_end[0:1, bass.ds(i * BLOCK_WINS, BLOCK_WINS)])
                ends = [nc.scalar.snap(r, min_val=1, max_val=ADJ_ITEMS) for r in regs]
                if not first:
                    act.wait_ge(stored[q], 16 * (uses - 1))
                for j in range(BLOCK_WINS):
                    act.wait_ge(item_done, ends[j])
                    nc.scalar.activation(
                        counts[:, q, :, j * WIN:(j + 1) * WIN].rearrange("p h d -> p d h"),
                        bank(j).rearrange("p (d h) -> p d h", h=BLOCKS), ACT.Copy, scale=COUNT_SCALE).then_inc(emptied, 1)
                    act.wait_ge(emptied, i * BLOCK_WINS + (j + 1))
                    nc.scalar.activation(bank(j), zeros[:], ACT.Copy).then_inc(zeroed, 1)
                nc.scalar.activation(k.held_act[:], k.ones[:, 0:1], ACT.Copy).then_inc(block_ready, 1)
            in_pairs(nc.scalar, BLOCKS, turn)

        @block.sync
        def _(sp):
            def turn(i, q, uses, first):
                sp.wait_ge(block_ready, i + 1)
                sp.dma_start(k.adj[bass.ds(i, 1)][0], counts[:, q].rearrange("p h d -> p (h d)")).then_inc(stored[q], 16)
            in_pairs(nc.sync, BLOCKS, turn)
            for q in range(2):
                sp.wait_ge(stored[q], 16 * ((BLOCKS + 1 - q) // 2))


AHEAD = BLOCKS // 2


def aggregate(k, pe, i, q, uses, adj, adj_in, rows, ps, part):
    nc = k.nc
    if part == 0:
        pe.wait_ge(adj_in[q], 16 * uses)
        nc.tensor.matmul(ps, k.self_loop[:], rows[:, bass.ds(i, 1), :][:, 0, :], start=True, stop=False)
    for s in (range(0, AHEAD) if part == 0 else range(AHEAD, BLOCKS)):
        mm = nc.tensor.matmul(ps, adj[:, q, s * P:(s + 1) * P], rows[:, s, :], start=False, stop=s == BLOCKS - 1)
    return mm


def load_adjacency(k, sp, adj, adj_in, summed, more=None):
    def turn(i, q, uses, first):
        if not first:
            sp.wait_ge(summed, i - 1)
        sp.dma_start(adj[:, q, :], k.adj[bass.ds(i, 1)][0]).then_inc(adj_in[q], 16)
        if more:
            more(i, q, uses, first)
    in_pairs(k.nc.sync, BLOCKS, turn)


def build_layer_one(k):
    nc = k.nc
    with ExitStack() as st:
        sb, pb, sem = local(nc, st)
        w = sb("l_w", [P, KF, D], fp32)
        brow = sb("l_b", [P, D], fp32)
        adj = sb("l_adj", [P, 2, BLOCKS * P], fp16)
        pre = sb("l_pre", [P, 2, D], fp32)
        z = sb("l_z", [P, 2, D], fp32)
        zt = sb("l_zt", [P, 2, D], fp32)
        h = sb("l_h", [P, 2, D], fp32)
        ps_o = [pb(f"lp_o{i}", [P, 2 * D], fp32) for i in range(2)]
        ps_t = [pb(f"lp_t{i}", [P, D], fp32) for i in range(2)]
        ps_h = [pb(f"lp_h{i}", [P, D], fp32) for i in range(2)]
        w_in, summed, half, out_ready, z_ready, t_done, t_copied, h_done, scaled, hi_done, lo_done = (
            sem("l_" + s) for s in ("w_in", "summed", "half", "out", "z", "t_done", "t_copied", "h_done", "scaled",
                                    "hi_done", "lo_done"))
        adj_in = [sem(f"l_adj_in{q}") for q in range(2)]
        block = st.enter_context(nc.Block())

        @block.sync
        def _(sp):
            sp.dma_start(w[:], k.io["L0_gnn_W2"].rearrange("(c p) n -> p c n", p=P)).then_inc(w_in, 16)
            sp.dma_start(brow[:], k.io["L0_gnn_b1"][None, :].to_broadcast([P, D])).then_inc(w_in, 16)
            load_adjacency(k, sp, adj, adj_in, summed)

        @block.tensor
        def _(pe):
            pe.wait_ge(w_in, 32)

            def transposes(i, q, first):
                pe.wait_ge(z_ready, i + 1)
                if not first:
                    pe.wait_ge(t_copied, i - 1)
                for c in range(KF):
                    mm = nc.tensor.transpose(ps_t[q][:, c * P:(c + 1) * P], z[:, q, c * P:(c + 1) * P], k.ident[:])
                mm.then_inc(t_done, 1)

            def products(i, q, first):
                pe.wait_ge(t_copied, i + 1)
                if not first:
                    pe.wait_ge(scaled, i - 1)
                for c in range(KF):
                    mm = nc.tensor.matmul(ps_h[q], zt[:, q, c * P:(c + 1) * P], w[:, c, :], start=c == 0, stop=c == KF - 1)
                mm.then_inc(h_done, 1)

            def turn(i, q, uses, first):
                if not first:
                    pe.wait_ge(out_ready, i - 1)
                aggregate(k, pe, i, q, uses, adj, adj_in, k.rows[0], ps_o[q], 0)
                if not (isinstance(i, int) and i == 0):
                    transposes(i - 1, 1 - q, isinstance(i, int) and i < 3)
                aggregate(k, pe, i, q, uses, adj, adj_in, k.rows[0], ps_o[q], 1).then_inc(summed, 1)
                if not (isinstance(i, int) and i == 0):
                    products(i - 1, 1 - q, isinstance(i, int) and i < 3)
            in_pairs(nc.tensor, BLOCKS, turn)
            transposes(BLOCKS - 1, 0, False)
            products(BLOCKS - 1, 0, False)

        @block.vector
        def _(dve):
            dve.wait_ge(w_in, 32)

            def finish(i, q, first):
                dve.wait_ge(h_done, i + 1)
                if not first:
                    dve.wait_ge(hi_done, i - 1)
                    dve.wait_ge(lo_done, i - 1)
                nc.vector.tensor_scalar(h[:, q, :], ps_h[q], k.dinv_in[:, bass.ds(i, 1)], None, ALU.mult).then_inc(scaled, 1)
                dve.wait_ge(scaled, i + 1)
                dve.wait_ge(hi_done, i + 1)
                rows = k.rows[1][:, bass.ds(i, 1), :][:, 0, :]
                nc.vector.tensor_tensor(rows[:, D:2 * D], h[:, q, :], rows[:, 0:D], ALU.subtract).then_inc(lo_done, 1)

            def turn(i, q, uses, first):
                dve.wait_ge(summed, i + 1)
                if not first:
                    dve.wait_ge(z_ready, i - 1)
                d = k.dinv_out[:, bass.ds(i, 1)]
                nc.vector.scalar_tensor_tensor(pre[:, q, :], ps_o[q][:, 0:D], d, brow[:], ALU.mult, ALU.add).then_inc(half, 1)
                dve.wait_ge(half, i + 1)
                nc.vector.scalar_tensor_tensor(pre[:, q, :], ps_o[q][:, D:2 * D], d, pre[:, q, :], ALU.mult,
                                               ALU.add).then_inc(out_ready, 1)
                if not (isinstance(i, int) and i == 0):
                    finish(i - 1, 1 - q, isinstance(i, int) and i < 3)
            in_pairs(nc.vector, BLOCKS, turn)
            finish(BLOCKS - 1, 0, False)

        @block.scalar
        def _(act):
            def halves(i, q):
                act.wait_ge(scaled, i + 1)
                nc.scalar.activation(k.rows[1][:, bass.ds(i, 1), 0:D][:, 0, :], h[:, q, :], ACT.Copy).then_inc(hi_done, 1)

            def copies(i, q, first):
                act.wait_ge(t_done, i + 1)
                if not first:
                    act.wait_ge(h_done, i - 1)
                nc.scalar.activation(zt[:, q, :], ps_t[q], ACT.Copy).then_inc(t_copied, 1)

            def turn(i, q, uses, first):
                if not (isinstance(i, int) and i == 0):
                    copies(i - 1, 1 - q, isinstance(i, int) and i < 3)
                act.wait_ge(out_ready, i + 1)
                if not first:
                    act.wait_ge(t_done, i - 1)
                nc.scalar.activation(z[:, q, :], pre[:, q, :], ACT.Relu).then_inc(z_ready, 1)
                if not (isinstance(i, int) and i == 0):
                    halves(i - 1, 1 - q)
            in_pairs(nc.scalar, BLOCKS, turn)
            copies(BLOCKS - 1, 0, False)
            halves(BLOCKS - 1, 0)


def build_layer_two(k):
    nc = k.nc
    k.xn_rows = k.dr("xn_rows", [ROWS, D], fp32)
    with ExitStack() as st:
        sb, pb, sem = local(nc, st)
        wr = sb("r_wr", [P, KF, EXPERTS], fp32)
        br = sb("r_br", [P, EXPERTS], fp32)
        brow = sb("r_b2", [P, D], fp32)
        adj = sb("r_adj", [P, 2, BLOCKS * P], fp16)
        x = sb("r_x", [P, 2, D], fp32)
        pre = sb("r_pre", [P, 2, D], fp32)
        x2 = sb("r_x2", [P, 2, D], fp32)
        z = sb("r_z", [P, 2, D], fp32)
        xn = sb("r_xn", [P, 2, D], fp32)
        zt = sb("r_zt", [P, 2, D], fp32)
        stats = sb("r_stats", [P, 2, 6], fp32)
        mv = sb("r_mv", [P, 2, 2], fp32)
        ps_o = [pb(f"rp_o{i}", [P, 2 * D], fp32) for i in range(2)]
        ps_t = [pb(f"rp_t{i}", [P, D], fp32) for i in range(2)]
        ps_l = [pb(f"rp_l{i}", [P, EXPERTS], fp32) for i in range(2)]
        w_in, summed, half, out_ready, step, var_ready, root, x2_ready, xt_ready, xn_ready, t_done, t_copied, l_done, logit = (
            sem("r_" + s) for s in ("w_in", "summed", "half", "out", "step", "var", "root", "x2", "xt", "xn", "t_done",
                                    "t_copied", "l_done", "logit"))
        adj_in = [sem(f"r_adj_in{q}") for q in range(2)]
        x_in = [sem(f"r_x_in{q}") for q in range(2)]
        x2_out = [sem(f"r_x2_out{q}") for q in range(2)]
        xn_out = [sem(f"r_xn_out{q}") for q in range(2)]
        block = st.enter_context(nc.Block())
        STEPS = 4
        zero = sb("r_zero", [P, D], fp32)
        zero_set, zero_out = sem("r_zero_set"), sem("r_zero_out")

        @block.gpsimd
        def _(pool):
            nc.gpsimd.memset(zero[:], 0.0).then_inc(zero_set, 1)
            pool.wait_ge(zero_set, 1)
            for rows in (k.io["out"], k.xn_rows):
                pool.dma_start(rows[PAD_NODES:ROWS, :], zero[:]).then_inc(zero_out, 16)
            pool.wait_ge(zero_out, 32)

        @block.sync
        def _(sp):
            sp.dma_start(wr[:], k.io["L0_ffn_Wr"].rearrange("(c p) n -> p c n", p=P)).then_inc(w_in, 16)
            sp.dma_start(br[:], k.io["L0_ffn_br"][None, :].to_broadcast([P, EXPERTS])).then_inc(w_in, 16)
            sp.dma_start(brow[:], k.io["L0_gnn_b2"][None, :].to_broadcast([P, D])).then_inc(w_in, 16)

            def residual(i, q, uses, first):
                if not first:
                    sp.wait_ge(x2_ready, i - 1)
                sp.dma_start(x[:, q, :], k.io["x"][bass.ds(i * P, P), :]).then_inc(x_in[q], 16)
            load_adjacency(k, sp, adj, adj_in, summed, residual)

        @block.tensor
        def _(pe):
            pe.wait_ge(w_in, 48)

            def transposes(i, q, first):
                pe.wait_ge(xt_ready, i + 1)
                if not first:
                    pe.wait_ge(t_copied, i - 1)
                for c in range(KF):
                    mm = nc.tensor.transpose(ps_t[q][:, c * P:(c + 1) * P], z[:, q, c * P:(c + 1) * P], k.ident[:])
                mm.then_inc(t_done, 1)

            def products(i, q, first):
                pe.wait_ge(t_copied, i + 1)
                if not first:
                    pe.wait_ge(logit, i - 1)
                for c in range(KF):
                    mm = nc.tensor.matmul(ps_l[q], zt[:, q, c * P:(c + 1) * P], wr[:, c, :], start=c == 0, stop=c == KF - 1)
                mm.then_inc(l_done, 1)

            def turn(i, q, uses, first):
                if not first:
                    pe.wait_ge(out_ready, i - 1)
                aggregate(k, pe, i, q, uses, adj, adj_in, k.rows[1], ps_o[q], 0)
                if not (isinstance(i, int) and i == 0):
                    transposes(i - 1, 1 - q, isinstance(i, int) and i < 3)
                aggregate(k, pe, i, q, uses, adj, adj_in, k.rows[1], ps_o[q], 1).then_inc(summed, 1)
                if not (isinstance(i, int) and i == 0):
                    products(i - 1, 1 - q, isinstance(i, int) and i < 3)
            in_pairs(nc.tensor, BLOCKS, turn)
            transposes(BLOCKS - 1, 0, False)
            products(BLOCKS - 1, 0, False)

        @block.vector
        def _(dve):
            dve.wait_ge(w_in, 48)

            def finish(i, q):
                dve.wait_ge(l_done, i + 1)
                nc.vector.tensor_tensor(k.logits[:, bass.ds(i, 1), :][:, 0, :], ps_l[q], br[:], ALU.add).then_inc(logit, 1)

            def norm(i, q, src, out, s0, v, done):
                nc.vector.bn_stats(stats[:, q, :], src).then_inc(step, 1)
                dve.wait_ge(step, s0 + 1)
                hold_waits(k, nc.vector)
                nc.vector.bn_aggr(mv[:, q, :], stats[:, q, :]).then_inc(var_ready, 1)
                dve.wait_ge(root, v)
                nc.vector.reciprocal(mv[:, q, 1:2], mv[:, q, 1:2]).then_inc(step, 1)
                dve.wait_ge(step, s0 + 2)
                nc.vector.tensor_scalar(out, src, mv[:, q, 0:1], mv[:, q, 1:2], ALU.subtract, ALU.mult).then_inc(done, 1)

            def turn(i, q, uses, first):
                dve.wait_ge(summed, i + 1)
                d = k.dinv_out[:, bass.ds(i, 1)]
                nc.vector.scalar_tensor_tensor(pre[:, q, :], ps_o[q][:, 0:D], d, brow[:], ALU.mult, ALU.add).then_inc(half, 1)
                dve.wait_ge(half, i + 1)
                nc.vector.scalar_tensor_tensor(pre[:, q, :], ps_o[q][:, D:2 * D], d, pre[:, q, :], ALU.mult,
                                               ALU.add).then_inc(out_ready, 1)
                dve.wait_ge(out_ready, i + 1)
                dve.wait_ge(x_in[q], 16 * uses)
                if not first:
                    dve.wait_ge(x2_out[q], 16 * (uses - 1))
                    dve.wait_ge(xn_out[q], 16 * (uses - 1))
                    dve.wait_ge(t_done, i - 1)
                nc.vector.scalar_tensor_tensor(x2[:, q, :], pre[:, q, :], 0.0, x[:, q, :], ALU.max, ALU.add).then_inc(x2_ready, 1)
                dve.wait_ge(x2_ready, i + 1)
                hold_waits(k, nc.vector)
                norm(i, q, x2[:, q, :], z[:, q, :], i * STEPS, i * 2 + 1, xt_ready)
                dve.wait_ge(xt_ready, i + 1)
                hold_waits(k, nc.vector)
                norm(i, q, z[:, q, :], xn[:, q, :], i * STEPS + 2, i * 2 + 2, xn_ready)
                if not (isinstance(i, int) and i == 0):
                    finish(i - 1, 1 - q)
            in_pairs(nc.vector, BLOCKS, turn)
            finish(BLOCKS - 1, 0)

        @block.scalar
        def _(act):
            def copies(i, q, first):
                act.wait_ge(t_done, i + 1)
                if not first:
                    act.wait_ge(l_done, i - 1)
                nc.scalar.activation(zt[:, q, :], ps_t[q], ACT.Copy).then_inc(t_copied, 1)

            def turn(i, q, uses, first):
                if not (isinstance(i, int) and i == 0):
                    copies(i - 1, 1 - q, isinstance(i, int) and i < 3)
                for t in range(2):
                    act.wait_ge(var_ready, i * 2 + t + 1)
                    nc.scalar.activation(mv[:, q, 1:2], mv[:, q, 1:2], ACT.Sqrt, bias=k.eps[:]).then_inc(root, 1)
                act.wait_ge(x2_ready, i + 1)
                act.dma_start(k.io["out"][bass.ds(i * P, P), :], x2[:, q, :]).then_inc(x2_out[q], 16)
                act.wait_ge(xn_ready, i + 1)
                act.dma_start(k.xn_rows[bass.ds(i * P, P), :], xn[:, q, :]).then_inc(xn_out[q], 16)
            in_pairs(nc.scalar, BLOCKS, turn)
            copies(BLOCKS - 1, 0, False)
            for q in range(2):
                act.wait_ge(x2_out[q], 16 * ((BLOCKS + 1 - q) // 2))
                act.wait_ge(xn_out[q], 16 * ((BLOCKS + 1 - q) // 2))


class ExpertWeights:
    W = KF * HIDDEN
    LOADS = 2 * EXPERTS
    RAW = 3
    assert KF * HIDDEN == HB * D

    def __init__(self, k, sb, pb, sem):
        self.k = k
        self.raw = sb("w_raw", [P, self.RAW, self.W], fp32)
        self.scaled = sb("w_scaled", [P, self.W], fp32)
        self.gb_rows = sb("w_gb_rows", [2 * EXPERTS * KF, P], fp32)
        self.b1_rows = sb("w_b1_rows", [EXPERTS * HB, P], fp32)
        self.gb = sb("w_gb", [P, 2, EXPERTS, KF], fp32)
        self.ps_t = pb("wp_t", [P, (2 * KF + HB) * EXPERTS], fp32)
        self.ps_b = pb("wp_b", [P, EXPERTS * HB], fp32)
        self.small_in, self.small_t, self.gb_ready, self.offset_done, self.scaled_ready, self.hi, self.lo = (
            sem("w_" + x) for x in ("small_in", "small_t", "gb", "offset", "scaled", "hi", "lo"))
        self.raw_in = [sem(f"w_raw_in{r}") for r in range(self.RAW)]

    def sync(self, sp):
        k, n = self.k, EXPERTS * KF
        sp.dma_start(self.gb_rows[0:n, :], k.io["L0_ffn_ln_g"].rearrange("e (c p) -> (e c) p", p=P)).then_inc(self.small_in, 16)
        sp.dma_start(self.gb_rows[n:2 * n, :], k.io["L0_ffn_ln_b"].rearrange("e (c p) -> (e c) p", p=P)).then_inc(self.small_in, 16)
        sp.dma_start(self.b1_rows[:], k.io["L0_ffn_b1"].rearrange("e (c p) -> (e c) p", p=P)).then_inc(self.small_in, 16)
        sp.dma_start(k.b2[:], k.io["L0_ffn_b2"][None, :, :].to_broadcast([P, EXPERTS, D])).then_inc(self.small_in, 16)
        for i in range(self.LOADS):
            if i >= self.RAW:
                sp.wait_ge(self.scaled_ready, i - self.RAW + 1)
                sp.wait_ge(self.offset_done, (i - self.RAW) // 2 + 1)
            name, inner = ("L0_ffn_W1", HIDDEN) if i % 2 == 0 else ("L0_ffn_W2", D)
            sp.dma_start(self.raw[:, i % self.RAW].rearrange("p (c n) -> p c n", n=inner),
                         k.io[name][i // 2].rearrange("(c p) n -> p c n", p=P)).then_inc(self.raw_in[i % self.RAW], 16)

    def vector(self, dve):
        k, nc, raw, scaled = self.k, self.k.nc, self.raw, self.scaled
        dve.wait_ge(self.small_t, 1)
        gb = self.gb[:].rearrange("p t e c -> p t (e c)")
        ps = self.ps_t[:, 0:2 * KF * EXPERTS].rearrange("p (t n) -> p t n", t=2)
        nc.vector.tensor_scalar(gb[:, 0], ps[:, 0], SCALE, None, ALU.mult).then_inc(self.gb_ready, 1)
        nc.vector.tensor_copy(gb[:, 1], ps[:, 1]).then_inc(self.gb_ready, 1)
        nc.vector.tensor_copy(k.b1[:], self.ps_t[:, 2 * KF * EXPERTS:]).then_inc(self.gb_ready, 1)
        dve.wait_ge(self.gb_ready, 3)
        for i in range(self.LOADS):
            e, r = i // 2, i % self.RAW
            dve.wait_ge(self.raw_in[r], 16 * (i // self.RAW + 1))
            if i:
                dve.wait_ge(self.lo, i)
                dve.wait_ge(self.hi, i)
            if i % 2 == 0:
                for c in range(KF):
                    part = slice(c * HIDDEN, (c + 1) * HIDDEN)
                    mm = nc.vector.tensor_scalar(scaled[:, part], raw[:, r, part], self.gb[:, 0, e, c:c + 1], None, ALU.mult)
            else:
                mm = nc.vector.tensor_scalar(scaled[:], raw[:, r], SCALE, None, ALU.mult)
            mm.then_inc(self.scaled_ready, 1)
            dve.wait_ge(self.hi, i + 1)
            w = k.w1 if i % 2 == 0 else k.w2
            nc.vector.tensor_tensor(w[:, e, 1].rearrange("p c n -> p (c n)"), scaled[:],
                                    w[:, e, 0].rearrange("p c n -> p (c n)"), ALU.subtract).then_inc(self.lo, 1)
        dve.wait_ge(self.offset_done, EXPERTS)
        nc.vector.tensor_tensor(k.b1[:], self.ps_b[:], k.b1[:], ALU.add)

    def scalar(self, act):
        k, nc = self.k, self.k.nc
        for i in range(self.LOADS):
            act.wait_ge(self.scaled_ready, i + 1)
            w = k.w1 if i % 2 == 0 else k.w2
            nc.scalar.activation(w[:, i // 2, 0].rearrange("p c n -> p (c n)"), self.scaled[:], ACT.Copy).then_inc(self.hi, 1)

    def small_transposes(self, pe):
        k, nc, n = self.k, self.k.nc, 2 * KF * EXPERTS
        pe.wait_ge(self.small_in, 16 * 4)
        nc.tensor.transpose(self.ps_t[:, 0:n], self.gb_rows[:], k.ident[0:n, 0:n])
        nc.tensor.transpose(self.ps_t[:, n:], self.b1_rows[:], k.ident[0:HB * EXPERTS, 0:HB * EXPERTS]).then_inc(self.small_t, 1)

    def tensor(self, pe):
        nc, raw = self.k.nc, self.raw
        pe.wait_ge(self.gb_ready, 3)
        for e in range(EXPERTS):
            r = 2 * e % self.RAW
            pe.wait_ge(self.raw_in[r], 16 * (2 * e // self.RAW + 1))
            for h in range(HB):
                for c in range(KF):
                    mm = nc.tensor.matmul(self.ps_b[:, e * HB + h:e * HB + h + 1],
                                          raw[:, r, c * HIDDEN + h * P:c * HIDDEN + (h + 1) * P],
                                          self.gb[:, 1, e, c:c + 1], start=c == 0, stop=c == KF - 1)
            mm.then_inc(self.offset_done, 1)


def build_routing(k, kst):
    nc = k.nc
    slot_list = k.dr("slot_list", [SLOTS, 2], i32)
    NE = BLOCKS * EXPERTS
    own = lambda name, shape, dt: kst.enter_context(nc.sbuf_tensor(name, shape, dt))
    k.w1 = own("w1", [P, EXPERTS, 2, KF, HIDDEN], fp16)
    k.w2 = own("w2", [P, EXPERTS, 2, HB, D], fp16)
    k.b1 = own("b1", [P, EXPERTS * HB], fp32)
    k.b2 = own("b2", [P, EXPERTS, D], fp32)
    with ExitStack() as st:
        sb, pb, sem = local(nc, st)
        back = sb("o_back", [P, EXPERTS], fp32)
        best = sb("o_best", [P, 2, BLOCKS], fp32)
        rest = sb("o_rest", [P, BLOCKS, EXPERTS], fp32)
        pick = sb("o_pick", [P, BLOCKS], fp32)
        hot = sb("o_hot", [P, 2, BLOCKS, EXPERTS], fp32)
        both = sb("o_both", [P, BLOCKS, EXPERTS], fp32)
        inner = sb("o_inner", [P, BLOCKS, EXPERTS], fp32)
        tot = sb("o_tot", [P, EXPERTS, BLOCKS], fp32)
        cum = sb("o_cum", [P, EXPERTS, BLOCKS], fp32)
        ones = sb("o_ones", [P, BLOCKS], fp32)
        cnt = sb("o_cnt", [P, EXPERTS], fp32)
        cnt_i = sb("o_cnt_i", [P, EXPERTS], i32)
        tiles = sb("o_tiles", [P, EXPERTS], fp32)
        ends = sb("o_ends", [P, EXPERTS], fp32)
        begin = sb("o_begin", [P, EXPERTS], fp32)
        slot_f = sb("o_slot_f", [P, 2, BLOCKS], fp32)
        gap = sb("o_gap", [P, BLOCKS], fp32)
        ex = sb("o_ex", [P, BLOCKS], fp32)
        le = sb("o_le", [1, TOKEN_TILES, EXPERTS - 1], fp32)
        te = sb("o_te", [1, TOKEN_TILES], fp32)
        empty = sb("o_empty", [TOKEN_TILES, P, 2], i32)
        lst = sb("o_lst", [TOKEN_TILES, P, 2], i32)
        lst_f = sb("o_lst_f", [TOKEN_TILES, 2, P], fp32)
        stage = sb("o_stage", [P, 2, U], i32)
        stage_row = sb("o_stage_row", [P, 2, U, 2], i32)
        ps_in = pb("op_in", [P, NE], fp32)
        ps_tot = pb("op_tot", [P, NE], fp32)
        ps_l = pb("op_l", [P, 2 * TOKEN_TILES], fp32)
        s, hot_ready, pre_done, gap_ready, exp_done, slots_ready = (
            sem("o_" + x) for x in ("s", "hot", "pre", "gap", "exp", "slots"))
        zeroed, staged, list_in, lst_ready, lst_t = (
            sem("o_" + x) for x in ("zeroed", "staged", "list_in", "lst_ready", "lst_t"))
        put = [sem(f"o_put{i}") for i in range(2 * U)]
        empty_set = sem("o_empty_set")
        weights = ExpertWeights(k, sb, pb, sem)
        block = st.enter_context(nc.Block())

        @block.vector
        def _(dve):
            count = [0]

            def link(ins):
                count[0] += 1
                ins.then_inc(s, 1)
                dve.wait_ge(s, count[0])

            nc.vector.memset(empty[:, :, 1], 0)
            nc.vector.tensor_scalar(empty[:, :, 0], k.lane_f[0:TOKEN_TILES, :], float(PAD_NODES), None,
                                    ALU.add).then_inc(empty_set, 1)
            link(nc.vector.memset(ones[:], 1.0))

            link(nc.vector.tensor_scalar(back[:], k.lane_f[:, 0:EXPERTS], float(-EXPERTS), None, ALU.add))
            full = [P, BLOCKS, EXPERTS]
            for c in range(2):
                src = k.logits if c == 0 else rest
                link(nc.vector.tensor_reduce(best[:, c, :], src[:], AX.X, ALU.max))
                link(nc.vector.tensor_tensor(inner[:], src[:], bc(best[:, c, :, None], full), ALU.is_equal))
                link(nc.vector.tensor_tensor(inner[:], inner[:], bc(back[:, None, :], full), ALU.mult))
                link(nc.vector.tensor_reduce(pick[:], inner[:], AX.X, ALU.min))
                link(nc.vector.tensor_tensor(hot[:, c], bc(back[:, None, :], full), bc(pick[:, :, None], full),
                                             ALU.is_equal))
                if c == 0:
                    link(nc.vector.scalar_tensor_tensor(rest[:], hot[:, 0], -3e38, k.logits[:], ALU.mult, ALU.add))
            link(nc.vector.tensor_tensor(gap[:], best[:, 1, :], best[:, 0, :], ALU.subtract))
            nc.vector.tensor_tensor(both[:], hot[:, 0], hot[:, 1], ALU.add).then_inc(hot_ready, 1)
            dve.wait_ge(exp_done, 1)
            link(nc.vector.tensor_scalar(gap[:], ex[:], 1.0, None, ALU.add))
            link(nc.vector.reciprocal(k.gate[:, 0, :], gap[:]))
            link(nc.vector.tensor_tensor(k.gate[:, 1, :], ex[:], k.gate[:, 0, :], ALU.mult))
            dve.wait_ge(pre_done, 1)
            link(nc.vector.tensor_copy(inner[:], ps_in[:].rearrange("p (b e) -> p b e", e=EXPERTS)))
            link(nc.vector.tensor_copy(tot[:], ps_tot[:].rearrange("p (b e) -> p e b", e=EXPERTS)))
            for e in range(EXPERTS):
                link(nc.vector.tensor_tensor_scan(cum[:, e, :], ones[:], tot[:, e, :], 0.0, ALU.mult, ALU.add))
            link(nc.vector.tensor_scalar(cnt[:], cum[:, :, BLOCKS - 1], float(P - 1), None, ALU.add))
            link(nc.vector.tensor_copy(cnt_i[:], cnt[:]))
            link(nc.vector.tensor_single_scalar(cnt_i[:], cnt_i[:], 7, ALU.arith_shift_right))
            link(nc.vector.tensor_copy(tiles[:], cnt_i[:]))
            link(nc.vector.tensor_tensor_scan(ends[:], ones[:, 0:EXPERTS], tiles[:], 0.0, ALU.mult, ALU.add))
            link(nc.vector.tensor_tensor(begin[:], ends[:], tiles[:], ALU.subtract))
            link(nc.vector.tensor_scalar(begin[:], begin[:], float(P), None, ALU.mult))
            link(nc.vector.tensor_tensor(cum[:], cum[:], tot[:], ALU.subtract))
            link(nc.vector.tensor_tensor(inner[:], inner[:], cum[:].rearrange("p e b -> p b e"), ALU.add))
            link(nc.vector.tensor_tensor(inner[:], inner[:], bc(begin[:, None, :], [P, BLOCKS, EXPERTS]), ALU.add))
            for c in range(2):
                link(nc.vector.tensor_tensor(hot[:, c], hot[:, c], inner[:], ALU.mult))
                link(nc.vector.tensor_reduce(slot_f[:, c, :], hot[:, c], AX.X, ALU.add))
            nc.vector.tensor_copy(k.slot[:], slot_f[:]).then_inc(slots_ready, 1)
            link(nc.vector.tensor_tensor(le[:], bc(ends[0:1, None, 0:EXPERTS - 1], [1, TOKEN_TILES, EXPERTS - 1]),
                                         bc(k.lane_f[0:1, 0:TOKEN_TILES, None], [1, TOKEN_TILES, EXPERTS - 1]), ALU.is_le))
            link(nc.vector.tensor_reduce(te[:], le[:], AX.X, ALU.add))
            nc.vector.memset(k.tile_expert[:, 0:1], 0)
            nc.vector.tensor_copy(k.tile_expert[:, 1:], te[:])
            weights.vector(dve)
            dve.wait_ge(list_in, 16)
            nc.vector.tensor_copy(lst_f[:, 0], lst[:, :, 0]).then_inc(lst_ready, 1)
            nc.vector.tensor_copy(lst_f[:, 1], lst[:, :, 1].bitcast(fp32)).then_inc(lst_ready, 1)
            dve.wait_ge(lst_t, 1)
            nc.vector.tensor_copy(k.slot_token[:], ps_l[:, 0:TOKEN_TILES])
            nc.vector.tensor_copy(k.slot_gate[:], ps_l[:, TOKEN_TILES:])

        @block.scalar
        def _(act):
            act.wait_ge(hot_ready, 1)
            nc.scalar.activation(ex[:], gap[:], ACT.Exp).then_inc(exp_done, 1)
            weights.scalar(act)

        @block.tensor
        def _(pe):
            pe.wait_ge(hot_ready, 1)
            flat = both[:].rearrange("p b e -> p (b e)")
            nc.tensor.matmul(ps_in[:], k.tri[:], flat, start=True, stop=True)
            nc.tensor.matmul(ps_tot[:], k.ones[:], flat, start=True, stop=True).then_inc(pre_done, 1)
            weights.small_transposes(pe)
            weights.tensor(pe)
            pe.wait_ge(lst_ready, 2)
            for j in range(2):
                mm = nc.tensor.transpose(ps_l[:, j * TOKEN_TILES:(j + 1) * TOKEN_TILES], lst_f[:, j],
                                         k.ident[0:TOKEN_TILES, 0:TOKEN_TILES])
            mm.then_inc(lst_t, 1)

        @block.sync
        def _(sp):
            sp.wait_ge(empty_set, 1)
            sp.dma_start(slot_list.rearrange("(t p) o -> t (p o)", p=P), empty[:].rearrange("t p o -> t (p o)")).then_inc(zeroed, 16)
            sp.wait_ge(zeroed, 16)
            weights.sync(sp)
            for i in range(2 * U):
                sp.wait_ge(put[i], 16 * TURNS)
            sp.dma_start(lst[:].rearrange("t p o -> t (p o)"), slot_list.rearrange("(t p) o -> t (p o)", p=P)).then_inc(list_in, 16)
            sp.wait_ge(list_in, 16)

        @block.gpsimd
        def _(pool):
            pool.wait_ge(zeroed, 16)
            pool.wait_ge(slots_ready, 1)

            def turn(n, first=False):
                if not first:
                    for i in range(2 * U):
                        pool.wait_ge(put[i], 16 * n)
                nc.gpsimd.tensor_copy(stage[:], k.slot[:, :, bass.ds(n * U, U)]).then_inc(staged, 1)
                for c in range(2):
                    nc.gpsimd.tensor_copy(stage_row[:, c, :, 0], k.token_id[:, bass.ds(n * U, U)]).then_inc(staged, 1)
                nc.gpsimd.tensor_copy(stage_row[:, :, :, 1].bitcast(fp32), k.gate[:, :, bass.ds(n * U, U)]).then_inc(staged, 1)
                pool.wait_ge(staged, n * 4 + 4)
                hold_waits(k, nc.gpsimd)
                for c in range(2):
                    for u in range(U):
                        pool.indirect_dma_start(
                            out=slot_list, out_offset=bass.IndirectOffsetOnAxis(ap=stage[:, c, u:u + 1], axis=0),
                            in_=stage_row[:, c, u, :], in_offset=None).then_inc(put[c * U + u], 16)
            turn(0, first=True)
            with nc.gpsimd.Fori(1, TURNS) as n:
                turn(n)
            for i in range(2 * U):
                pool.wait_ge(put[i], 16 * TURNS)


def build_experts(k):
    nc = k.nc
    PAIRS = ((0, 0), (0, 1), (1, 0))
    HALVES = 2
    HBH = HB // HALVES
    HW = HIDDEN // HALVES
    with ExitStack() as st:
        sb, pb, sem = local(nc, st)
        stage = sb("f_stage", [P, 2, M], i32)
        xg = sb("f_xg", [P, 2, M, D], fp32)
        xt = sb("f_xt", [P, 2, 2, D], fp16)
        h32 = sb("f_h32", [P, 2, HIDDEN], fp32)
        hh = sb("f_hh", [P, 2, 2, HIDDEN], fp16)
        y = sb("f_y", [P, M, D], fp32)
        weighted = sb("f_weighted", [P, M, D], fp32)
        to = sb("f_to", [P, 2, M], i32)
        ps_x = [pb(f"fp_x{i}", [P, D], fp32) for i in range(2)]
        ps_h = [pb(f"fp_h{i}", [P, HIDDEN], fp32) for i in range(2)]
        ps_y = [pb(f"fp_y{i}", [P, D], fp32) for i in range(2)]
        got = [[sem(f"f_got{q}_{i}") for i in range(M)] for q in range(2)]
        to_staged, added, y_done = sem("f_to"), sem("f_added"), sem("f_y_done")
        staged, x_t, x_hi, x_lo, up, act_done, h_hi, h_lo, down, y_ready = (
            sem("f_" + x) for x in ("staged", "x_t", "x_hi", "x_lo", "up", "act", "h_hi", "h_lo", "down", "y_ready"))
        block = st.enter_context(nc.Block())

        def experts(eng, regs, n):
            eng.load(regs, k.tile_expert[0:1, bass.ds(n * M, M + 1)])
            return [eng.snap(r, min_val=0, max_val=EXPERTS - 1) for r in regs]

        assert TILE_TURNS % 2 == 1 and M % 2 == 1

        def every(eng, turn):
            turn(0, 0, 1, True, False)
            with eng.Fori(0, (TILE_TURNS - 3) // 2) as n:
                turn(2 * n + 1, 1, n + 1, False, False)
                turn(2 * n + 2, 0, n + 2, False, False)
            turn(TILE_TURNS - 2, 1, (TILE_TURNS - 1) // 2, False, False)
            turn(TILE_TURNS - 1, 0, (TILE_TURNS + 1) // 2, False, True)

        @block.gpsimd
        def _(pool):
            def gathers(n, par, uses, begun):
                if begun:
                    for m in range(M):
                        pool.wait_ge(got[par][m], 16 * (uses - 1))
                    pool.wait_ge(x_t, n * M - M)
                nc.gpsimd.tensor_copy(stage[:, par], k.slot_token[:, bass.ds(n * M, M)]).then_inc(staged, 1)
                pool.wait_ge(staged, n + 1)
                hold_waits(k, nc.gpsimd)
                for m in range(M):
                    pool.indirect_dma_start(
                        out=xg[:, par, m, :], out_offset=None, in_=k.xn_rows,
                        in_offset=bass.IndirectOffsetOnAxis(ap=stage[:, par, m:m + 1], axis=0)).then_inc(got[par][m], 16)

            def additions(n, par, uses, first, last):
                if not first:
                    pool.wait_ge(added, n * (16 * M))
                    hold_waits(k, nc.gpsimd, M + 1)
                nc.gpsimd.tensor_copy(to[:, par], k.slot_token[:, bass.ds(n * M, M)]).then_inc(to_staged, 1)
                for m in range(M):
                    if m == 0:
                        pool.wait_ge(to_staged, n + 1)
                    pool.wait_ge(y_ready, n * M + m + 1)
                    if not (first and m == 0):
                        pool.wait_ge(added, n * (16 * M) + 16 * m)
                    hold_waits(k, nc.gpsimd, 1 + m)
                    pool.indirect_dma_start(
                        out=k.io["out"], out_offset=bass.IndirectOffsetOnAxis(ap=to[:, par, m:m + 1], axis=0),
                        in_=weighted[:, m, :], in_offset=None, compute_op=ALU.add).then_inc(added, 16)

            def turn(n, par, uses, first, last):
                if not last:
                    gathers(n + 1, 1 - par, uses + par, not first)
                additions(n, par, uses, first, last)
            gathers(0, 0, 1, False)
            every(nc.gpsimd, turn)
            pool.wait_ge(added, 16 * TOKEN_TILES)

        @block.tensor
        def _(pe):
            regs = [nc.tensor.alloc_register(f"f_pe{m}") for m in range(M + 1)]

            def transposes(n, m, par, uses, begun):
                q = (par + m) % 2
                if m == M:
                    pe.wait_ge(got[1 - par][0], 16 * (uses + par))
                else:
                    pe.wait_ge(got[par][m], 16 * uses)
                if begun:
                    pe.wait_ge(x_hi, n * M + (m - 1))
                    pe.wait_ge(x_lo, n * M + (m - 1))
                for c in range(KF):
                    rows = xg[:, 1 - par, 0, :] if m == M else xg[:, par, m, :]
                    mm = nc.tensor.transpose(ps_x[q][:, c * P:(c + 1) * P], rows[:, c * P:(c + 1) * P], k.ident[:])
                mm.then_inc(x_t, 1)

            def first_product(n, m, par, ex, begun):
                q = (par + m) % 2
                pe.wait_ge(x_hi, n * M + m + 1)
                pe.wait_ge(x_lo, n * M + m + 1)
                for a in range(HALVES):
                    if begun:
                        pe.wait_ge(act_done, n * (HALVES * M) + (HALVES * (m - 2) + a + 1))
                    for h in range(a * HBH, (a + 1) * HBH):
                        i = 0
                        for wh, xh in PAIRS:
                            for c in range(KF):
                                w = k.w1[:, bass.ds(ex, 1), wh, c, h * P:(h + 1) * P][:, 0, :]
                                mm = nc.tensor.matmul(ps_h[q][:, h * P:(h + 1) * P], w,
                                                      xt[:, q, xh, c * P:(c + 1) * P], start=i == 0, stop=i == 5)
                                i += 1
                    mm.then_inc(up, 1)

            def second_product(n, m, par, ex, begun):
                q = (par + m) % 2
                if begun:
                    pe.wait_ge(y_done, n * M + (m - 1))
                i = 0
                for a in range(HALVES):
                    pe.wait_ge(h_hi, n * (HALVES * M) + (HALVES * m + a + 1))
                    pe.wait_ge(h_lo, n * (HALVES * M) + (HALVES * m + a + 1))
                    for h in range(a * HBH, (a + 1) * HBH):
                        for wh, xh in PAIRS:
                            w = k.w2[:, bass.ds(ex, 1), wh, h, :][:, 0, :]
                            mm = nc.tensor.matmul(ps_y[q][:], hh[:, q, xh, h * P:(h + 1) * P], w,
                                                  start=i == 0, stop=i == 3 * HB - 1)
                            i += 1
                mm.then_inc(down, 1)

            def turn(n, par, uses, first, last):
                ex = experts(nc.tensor, regs, n)
                if first:
                    transposes(0, 0, 0, 1, False)
                for m in range(M):
                    if not (last and m == M - 1):
                        transposes(n, m + 1, par, uses, not (first and m == 0))
                    first_product(n, m, par, ex[m + 1], not (first and m < 2))
                    if not (first and m == 0):
                        second_product(n, m - 1, par, ex[m], not (first and m < 3))
                if last:
                    second_product(n, M - 1, par, ex[M], True)
            every(nc.tensor, turn)

        @block.scalar
        def _(act):
            regs = [nc.scalar.alloc_register(f"f_act{m}") for m in range(M + 1)]

            def high_half(n, m, par, begun):
                q = (par + m) % 2
                act.wait_ge(x_t, n * M + m + 1)
                if begun:
                    act.wait_ge(up, n * (HALVES * M) + HALVES * (m - 1))
                nc.scalar.activation(xt[:, q, 0, :], ps_x[q][:], ACT.Copy).then_inc(x_hi, 1)

            def turn(n, par, uses, first, last):
                ex = experts(nc.scalar, regs, n)
                if first:
                    high_half(0, 0, 0, False)
                for m in range(M):
                    q = (par + m) % 2
                    if not (last and m == M - 1):
                        high_half(n, m + 1, par, not (first and m == 0))
                    for a in range(HALVES):
                        act.wait_ge(up, n * (HALVES * M) + (HALVES * m + a + 1))
                        if not (first and m < 2):
                            act.wait_ge(h_hi, n * (HALVES * M) + (HALVES * (m - 2) + a + 1))
                            act.wait_ge(h_lo, n * (HALVES * M) + (HALVES * (m - 2) + a + 1))
                        for h in range(a * HBH, (a + 1) * HBH):
                            g = nc.scalar.activation(h32[:, q, h * P:(h + 1) * P], ps_h[q][:, h * P:(h + 1) * P],
                                                     ACT.Gelu, bias=k.b1[:, bass.ds(ex[m + 1] * HB + h, 1)],
                                                     scale=1.0 / SCALE)
                        g.then_inc(act_done, 1)
            every(nc.scalar, turn)

        @block.vector
        def _(dve):
            regs = [nc.vector.alloc_register(f"f_dve{m}") for m in range(M + 1)]

            def low_half(n, m, par):
                q = (par + m) % 2
                dve.wait_ge(x_hi, n * M + m + 1)
                nc.vector.tensor_tensor(xt[:, q, 1, :], ps_x[q][:], xt[:, q, 0, :], ALU.subtract).then_inc(x_lo, 1)

            def result(n, m, par, ex, begun):
                q, slot = (par + m) % 2, m % M
                dve.wait_ge(down, n * M + m + 1)
                if begun:
                    dve.wait_ge(added, n * (16 * M) + 16 * (m + 2 - M))
                nc.vector.scalar_tensor_tensor(y[:, slot, :], ps_y[q][:], 1.0 / SCALE,
                                               k.b2[:, bass.ds(ex, 1), :][:, 0, :], ALU.mult,
                                               ALU.add).then_inc(y_done, 1)
                dve.wait_ge(y_done, n * M + m + 1)
                nc.vector.tensor_scalar(weighted[:, slot, :], y[:, slot, :], k.slot_gate[:, bass.ds(n * M + m, 1)],
                                        None, ALU.mult).then_inc(y_ready, 1)

            def turn(n, par, uses, first, last):
                ex = experts(nc.vector, regs, n)
                if first:
                    low_half(0, 0, 0)
                for m in range(M):
                    q = (par + m) % 2
                    if not (last and m == M - 1):
                        low_half(n, m + 1, par)
                    if not (first and m < 2):
                        dve.wait_ge(down, n * M + (m - 1))
                    for a in range(HALVES):
                        part = slice(a * HW, (a + 1) * HW)
                        dve.wait_ge(act_done, n * (HALVES * M) + (HALVES * m + a + 1))
                        nc.vector.tensor_copy(hh[:, q, 0, part], h32[:, q, part]).then_inc(h_hi, 1)
                        dve.wait_ge(h_hi, n * (HALVES * M) + (HALVES * m + a + 1))
                        nc.vector.tensor_tensor(hh[:, q, 1, part], h32[:, q, part], hh[:, q, 0, part],
                                                ALU.subtract).then_inc(h_lo, 1)
                    if not (first and m == 0):
                        result(n, m - 1, par, ex[m], not first)
                if last:
                    result(n, M - 1, par, ex[M], True)
            every(nc.vector, turn)


def build(nc, io):
    with ExitStack() as ctx:
        k = Kernel(nc, ctx, io)
        build_constants(k)
        with ExitStack() as rst:
            k.rows = [rst.enter_context(nc.sbuf_tensor("rows0", [P, BLOCKS, 2 * D], fp16))]
            with ExitStack() as gst:
                build_edge_tables(k, gst)
                build_input_rows(k)
                build_adjacency(k)
            k.rows.append(rst.enter_context(nc.sbuf_tensor("rows1", [P, BLOCKS, 2 * D], fp16)))
            build_layer_one(k)
            build_layer_two(k)
        with ExitStack() as kst:
            build_routing(k, kst)
            build_experts(k)


_INS = ["x", "src", "dst", "L0_gnn_W1", "L0_gnn_b1", "L0_gnn_W2", "L0_gnn_b2", "L0_ffn_Wr", "L0_ffn_br",
        "L0_ffn_ln_g", "L0_ffn_ln_b", "L0_ffn_W1", "L0_ffn_b1", "L0_ffn_W2", "L0_ffn_b2"]


def kernel(**inputs):
    import numpy as _np
    import concourse.bacc as _bacc
    from concourse import mybir as _mybir
    from concourse.bass_utils import run_bass_kernel_spmd as _run

    arrays = {n: _np.ascontiguousarray(inputs[n]) for n in _INS}
    arrays["x"] = _np.concatenate([arrays["x"], _np.zeros((PAD_NODES - NODES, D), arrays["x"].dtype)])
    pad = EDGE_TILES * P - EDGES
    arrays["src"] = _np.concatenate([arrays["src"], _np.zeros(pad, arrays["src"].dtype)])
    arrays["dst"] = _np.concatenate([arrays["dst"], _np.full(pad, PAD_NODES, arrays["dst"].dtype)])
    nc = _bacc.Bacc("TRN2", target_bir_lowering=False, num_devices=1)
    io, ins = {}, {}
    for n, a in arrays.items():
        ins[f"in_{n}_dram"] = a
        io[n] = nc.dram_tensor(f"in_{n}_dram", a.shape, _mybir.dt.from_np(a.dtype), kind="ExternalInput").ap()
    io["out"] = nc.dram_tensor("out_0_dram", (ROWS, D), _mybir.dt.float32, kind="ExternalOutput").ap()
    build(nc, io)
    r = _run(nc, [ins], core_ids=[0])
    return r.results[0]["out_0_dram"][:NODES]
```

```python
from contextlib import ExitStack

import concourse.bass as bass
from concourse import mybir

P = 128
D = 256
KF = D // P
NODES = 6250
BLOCKS = -(-NODES // P)
PAD_NODES = BLOCKS * P
ROWS = PAD_NODES + P
EDGES = 206250
EDGE_TILES = -(-EDGES // P)
WIN = 8
WINS = PAD_NODES // WIN
BLOCK_WINS = P // WIN
CELLS = WIN * BLOCKS
ITEMS = EDGES // P + WINS
ITEM_COLS = -(-ITEMS // P)
EXPERTS = 8
HIDDEN = 1024
HB = HIDDEN // P
PAIR = 2 * P
PAIRS = (2 * PAD_NODES + EXPERTS * (PAIR - 1)) // PAIR
TOKEN_TILES = 2 * PAIRS
SLOTS = TOKEN_TILES * P
EPS = 1e-5
SCALE = 64.0

fp32 = mybir.dt.float32
fp16 = mybir.dt.float16
bf16 = mybir.dt.bfloat16
i32 = mybir.dt.int32
u16 = mybir.dt.uint16
ALU = mybir.AluOpType
ACT = mybir.ActivationFunctionType
AX = mybir.AxisListType

GRP = 13
GROUPS = EDGE_TILES // GRP
DIFFS = 6
HRING = 4
HTURNS = GROUPS // HRING
BANK = 512
RING = 4
U = 7
TURNS = BLOCKS // U
R = BLOCKS
LANES = 7
SUM_FROM = 2 * LANES
G = 3
ADJ_TURNS = BLOCKS
ADJ_ITEMS = ADJ_TURNS * R
BANKS = 4
COUNT_SCALE = 0.25
M = 4
PAIR_TURNS = PAIRS // M
POOL_HOLDS = 3 * M + 3
LN_STEPS = 2 * U + 1
assert GROUPS * GRP == EDGE_TILES and HTURNS * HRING == GROUPS and TURNS * U == BLOCKS
assert R % LANES == 0 and G < BANKS and ITEMS <= ADJ_ITEMS and ADJ_ITEMS <= ITEM_COLS * P and PAIR_TURNS * M == PAIRS


PLAN_PARTS, PLAN = [], 0
for _places in (range(0, 17), range(17, 33), range(33, R)):
    _last = [min(_g + G, len(_places)) - 1 for _g in range(0, len(_places), G)]
    PLAN_PARTS.append((PLAN, _places, [_places[_j] for _j in _last]))
    PLAN += len(_places) + len(_last)


class Kernel:

    def __init__(self, nc, ctx, dram):
        self.nc, self.ctx, self.io = nc, ctx, dram

    def sb(self, name, shape, dt):
        return self.ctx.enter_context(self.nc.sbuf_tensor(name, shape, dt))

    def dr(self, name, shape, dt):
        return self.nc.dram_tensor(name, shape, dt, kind="Internal").ap()


def local(nc, st):
    def banks(name, shape, dt):
        n = -(-shape[1] // BANK) * BANK
        return st.enter_context(nc.psum_tensor(name, [P, n], dt))[0:shape[0], 0:shape[1]]

    sems = []

    def sem(name):
        sems.append(nc.alloc_semaphore(name))
        return sems[-1]

    def give_back():
        nc.clear_and_free_semaphores(sems)
        nc.all_engine_barrier()

    st.callback(give_back)
    return lambda name, shape, dt: st.enter_context(nc.sbuf_tensor(name, shape, dt)), banks, sem


def hold_waits(k, eng, place=0):
    if eng is k.nc.gpsimd:
        last = k.held_pool[:, POOL_HOLDS:]
        eng.tensor_tensor(k.held_pool[:, place:place + 1], last, last, ALU.add)
    else:
        eng.memset(k.held_dve[:], 0.0)


def since(u):
    return RING if u >= RING else U - max(v for v in range(U) if v % RING == u)


def bc(ap, shape):
    return ap.to_broadcast(shape)


def build_constants(k):
    nc = k.nc
    k.ident = k.sb("ident", [P, P], fp32)
    k.ones = k.sb("ones", [P, P], fp32)
    k.held_pool = k.sb("held_pool", [1, POOL_HOLDS + 1], fp32)
    k.held_act = k.sb("held_act", [P, 1], fp32)
    k.self_loop = k.sb("self_loop", [P, P], fp16)
    k.held_dve = k.sb("held_dve", [1, 1], fp32)
    k.eps = k.sb("eps", [P, 1], fp32)
    k.tri = k.sb("tri", [P, P], fp32)
    k.lane_b = k.sb("lane_b", [P, P], bf16)
    k.lane_f = k.sb("lane_f", [P, P], fp32)
    k.item_id = k.sb("item_id", [P, ITEM_COLS], fp32)
    k.token_id = k.sb("token_id", [P, BLOCKS], i32)
    k.dinv_in = k.sb("dinv_in", [P, BLOCKS], fp32)
    k.dinv_out = k.sb("dinv_out", [P, BLOCKS], fp32)
    k.logits = k.sb("logits", [P, BLOCKS, EXPERTS], fp32)
    k.gate = k.sb("gate", [P, 2, BLOCKS], fp32)
    k.slot_gate = k.sb("slot_gate", [P, TOKEN_TILES], fp32)
    k.slot = k.sb("slot", [P, 2, BLOCKS], i32)
    k.slot_token = k.sb("slot_token", [P, TOKEN_TILES], i32)
    k.pair_expert = k.sb("pair_expert", [1, 1 + PAIRS], i32)
    k.adj = k.dr("adj", [BLOCKS, P, BLOCKS * P], fp16)
    with ExitStack() as st:
        sb, pb, sem = local(nc, st)
        ints = sb("c_ints", [P, P], i32)
        item_i = sb("c_item_i", [P, ITEM_COLS], i32)
        io_done, ones_done = sem("c_iota"), sem("c_ones")
        block = st.enter_context(nc.Block())

        @block.gpsimd
        def _(pool):
            nc.gpsimd.iota(ints[:], pattern=[[1, P]], base=0, channel_multiplier=0).then_inc(io_done, 1)
            nc.gpsimd.iota(item_i[:], pattern=[[P, ITEM_COLS]], base=0, channel_multiplier=1).then_inc(io_done, 1)
            nc.gpsimd.iota(k.token_id[:], pattern=[[P, BLOCKS]], base=0, channel_multiplier=1).then_inc(io_done, 1)
            pool.wait_ge(ones_done, 1)
            nc.gpsimd.affine_select(out=k.ident[:], in_=k.ones[:], compare_op=ALU.is_equal, fill=0.0, base=0,
                                    pattern=[[-1, P]], channel_multiplier=1).then_inc(io_done, 1)
            nc.gpsimd.affine_select(out=k.tri[:], in_=k.ones[:], compare_op=ALU.is_gt, fill=0.0, base=0,
                                    pattern=[[1, P]], channel_multiplier=-1)

        @block.vector
        def _(dve):
            nc.vector.memset(k.ones[:], 1.0).then_inc(ones_done, 1)
            nc.vector.memset(k.eps[:], EPS)
            nc.vector.memset(k.held_pool[:], 0.0)
            dve.wait_ge(io_done, 4)
            nc.vector.tensor_scalar(k.self_loop[:], k.ident[:], COUNT_SCALE, None, ALU.mult)
            nc.vector.tensor_copy(k.lane_b[:], ints[:])
            nc.vector.tensor_copy(k.lane_f[:], ints[:])
            nc.vector.tensor_copy(k.item_id[:], item_i[:])


def in_pairs(eng, total, turn):
    peeled = 2 + total % 2
    for i in range(peeled):
        turn(i, i % 2, i // 2 + 1, i < 2)
    with eng.Fori(0, (total - peeled) // 2) as n:
        if peeled == 3:
            turn(2 * n + 3, 1, n + 2, False)
            turn(2 * n + 4, 0, n + 3, False)
        else:
            turn(2 * n + 2, 0, n + 2, False)
            turn(2 * n + 3, 1, n + 2, False)


def build_edge_tables(k, gst):
    nc = k.nc
    own = lambda name, shape, dt: gst.enter_context(nc.sbuf_tensor(name, shape, dt))
    k.edge_cell = own("edge_cell", [P, ITEM_COLS * P], fp32)
    k.edge_lane = own("edge_lane", [P, ITEM_COLS * P], bf16)
    k.plan = own("plan", [1, ADJ_TURNS * PLAN], u16)
    k.fits = own("fits", [1, 1], u16)
    k.win_end = own("win_end", [1, WINS], u16)
    win_first = k.dr("win_first", [1, WINS], i32)
    win_row_d = k.dr("win_row_d", [ITEM_COLS, P], i32)
    with ExitStack() as st:
        sb, pb, sem = local(nc, st)
        dst = sb("t_dst", [P, EDGE_TILES], i32)
        part = sb("t_part", [P, EDGE_TILES], i32)
        hi = sb("t_hi", [P, EDGE_TILES], bf16)
        lo = sb("t_lo", [P, EDGE_TILES], bf16)
        minus_lo = sb("t_minus_lo", [P, EDGE_TILES], fp32)
        diff = sb("t_diff", [P, HRING, DIFFS, P], bf16)
        oh_lo = sb("t_oh_lo", [P, HRING, GRP, P], bf16)
        oh_hi = sb("t_oh_hi", [P, HRING, GRP, BLOCKS], bf16)
        deg = sb("t_deg", [P, BLOCKS], fp32)
        tmp = sb("t_tmp", [P, BLOCKS], fp32)
        tot = sb("t_tot", [P, BLOCKS], fp32)
        cum = sb("t_cum", [P, BLOCKS], fp32)
        below = sb("t_below", [P, BLOCK_WINS], fp32)
        win_id = sb("t_win_id", [BLOCK_WINS, BLOCKS], i32)
        win_idf = sb("t_win_idf", [BLOCK_WINS, BLOCKS], fp32)
        first = sb("t_first", [BLOCK_WINS, BLOCKS], fp32)
        first_i = sb("t_first_i", [BLOCK_WINS, BLOCKS], i32)
        all_i = sb("t_all_i", [P, WINS], i32)
        all_f = sb("t_all_f", [P, WINS], fp32)
        le = sb("t_le", [P, WINS], fp32)
        win = sb("t_win", [P, ITEM_COLS], fp32)
        win8 = sb("t_win8", [P, ITEM_COLS], fp32)
        tile_f = sb("t_tile_f", [P, ITEM_COLS], fp32)
        tile_i = sb("t_tile_i", [P, ITEM_COLS], i32)
        win_t = sb("t_win_t", [ITEM_COLS, P], i32)
        win_row = sb("t_win_row", [1, ITEM_COLS * P], i32)
        bank_row = sb("t_bank_row", [1, ITEM_COLS * P], i32)
        turn_item = sb("t_turn_item", [1, BLOCKS - 1], fp32)
        late = sb("t_late", [1, BLOCKS - 1], fp32)
        early = sb("t_early", [1, BLOCKS - 1], fp32)
        both = sb("t_both", [1, 1], fp32)
        rows_s = sb("t_rows_s", [P, 4, P], i32)
        rows_d = sb("t_rows_d", [P, 4, P], i32)
        rows_p = sb("t_rows_p", [P, 2, P], i32)
        rows_l = sb("t_rows_l", [P, 4, P], fp32)
        rows_h = sb("t_rows_h", [P, 4, P], fp32)
        rows_c = sb("t_rows_c", [P, 4, P], fp32)
        ps_deg = pb("tp_deg", [P, BLOCKS], fp32)
        ps_tot = pb("tp_tot", [P, BLOCKS], fp32)
        ps_win = pb("tp_win", [ITEM_COLS, P], fp32)
        ps_t = [pb(f"tp_t{i}", [P, P], fp32) for i in range(4)]
        ps_in = pb("tp_in", [BLOCK_WINS, BLOCKS], fp32)
        (dst_in, lo_done, hi_done, groups_done, step, consts, deg_ready, tot_done, root_done, first_ready, first_out,
         all_in, tile_ready, win_ready, win_t_done, win_t_ready, row_out, row_in, lane_ready, cell_ready,
         t_done, t_copied, minus_ready, diff_ready) = (sem("t_" + x) for x in (
             "dst_in", "lo", "hi", "groups", "step", "consts", "deg", "tot", "root", "first", "first_out", "all_in",
             "tile", "win", "win_t", "win_tr", "row_out", "row_in", "lane", "cell", "t_done", "t_copied", "minus", "diff"))
        diff_used = sem("t_diff_used")
        got = [sem(f"t_got{i}") for i in range(4)]
        block = st.enter_context(nc.Block())

        @block.sync
        def _(sp):
            sp.dma_start(dst[:], k.io["dst"].rearrange("(p c) -> p c", p=P)).then_inc(dst_in, 16)
            sp.wait_ge(first_ready, 1)
            with nc.allow_non_contiguous_dma(reason="one number per window"):
                sp.dma_start(win_first[0].rearrange("(b m) -> m b", m=BLOCK_WINS), first_i[:]).then_inc(first_out, 16)
            sp.wait_ge(first_out, 16)
            sp.dma_start(all_i[:], win_first.to_broadcast([P, WINS])).then_inc(all_in, 16)
            sp.wait_ge(win_t_ready, 1)
            sp.dma_start(win_row_d, win_t[:]).then_inc(row_out, 16)
            sp.wait_ge(row_out, 16)
            sp.dma_start(win_row[:], win_row_d.rearrange("c p -> (c p)")[None, :]).then_inc(row_in, 16)
            sp.wait_ge(row_in, 16)

        @block.vector
        def _(dve):
            count = [0]

            def link(ins):
                count[0] += 1
                ins.then_inc(step, 1)
                dve.wait_ge(step, count[0])

            dve.wait_ge(dst_in, 16)
            link(nc.vector.tensor_single_scalar(part[:], dst[:], 7, ALU.arith_shift_right))
            link(nc.vector.tensor_copy(hi[:], part[:]))
            link(nc.vector.tensor_single_scalar(part[:], dst[:], P - 1, ALU.bitwise_and))
            nc.vector.tensor_scalar(minus_lo[:], part[:], -1.0, None, ALU.mult).then_inc(minus_ready, 1)
            link(nc.vector.tensor_copy(lo[:], part[:]))

            def one_hots(n):
                for r in range(HRING):
                    if not (isinstance(n, int) and n == 0):
                        dve.wait_ge(groups_done, n * HRING + (r + 1 - HRING))
                    nc.vector.tensor_tensor(
                        oh_lo[:, r, DIFFS:], bc(k.lane_b[:, None, :], [P, GRP - DIFFS, P]),
                        bc(lo[:, bass.ds(n * (HRING * GRP) + (r * GRP + DIFFS), GRP - DIFFS)][:, :, None],
                           [P, GRP - DIFFS, P]), ALU.is_equal).then_inc(lo_done, 1)
                    nc.vector.tensor_tensor(
                        oh_hi[:, r], bc(k.lane_b[:, None, 0:BLOCKS], [P, GRP, BLOCKS]),
                        bc(hi[:, bass.ds(n * (HRING * GRP) + r * GRP, GRP)][:, :, None], [P, GRP, BLOCKS]),
                        ALU.is_equal).then_inc(hi_done, 1)
                    dve.wait_ge(diff_ready, n * HRING + (r + 1))
                    nc.vector.tensor_scalar(oh_lo[:, r, 0:DIFFS], diff[:, r], 0.0, None, ALU.is_equal).then_inc(diff_used, 1)
            one_hots(0)
            with nc.vector.Fori(1, HTURNS) as n:
                one_hots(n)
            dve.wait_ge(groups_done, GROUPS)
            nc.vector.tensor_copy(deg[:], ps_deg[:]).then_inc(deg_ready, 1)
            dve.wait_ge(deg_ready, 1)
            nc.vector.tensor_scalar(tmp[:], deg[:], 1.0, None, ALU.add).then_inc(deg_ready, 1)
            dve.wait_ge(root_done, 1)
            link(nc.vector.reciprocal(cum[:], tot[:]))
            nc.vector.tensor_scalar(k.dinv_in[:], cum[:], SCALE, None, ALU.mult)
            link(nc.vector.tensor_scalar(k.dinv_out[:], cum[:], 1.0 / (SCALE * COUNT_SCALE), None, ALU.mult))
            dve.wait_ge(tot_done, 1)
            link(nc.vector.tensor_copy(tot[:], ps_tot[:]))
            link(nc.vector.memset(tmp[:], 1.0))
            link(nc.vector.tensor_tensor_scan(cum[:], tmp[:], tot[:], 0.0, ALU.mult, ALU.add))
            link(nc.vector.tensor_tensor(cum[:], cum[:], tot[:], ALU.subtract))
            link(nc.vector.tensor_tensor(first[:], cum[0:BLOCK_WINS, :], ps_in[:], ALU.add))
            link(nc.vector.tensor_copy(first_i[:], first[:]))
            link(nc.vector.tensor_single_scalar(first_i[:], first_i[:], 7, ALU.arith_shift_right))
            link(nc.vector.tensor_copy(first[:], first_i[:]))
            dve.wait_ge(consts, 3)
            link(nc.vector.tensor_copy(win_idf[:], win_id[:]))
            link(nc.vector.tensor_tensor(first[:], first[:], win_idf[:], ALU.add))
            nc.vector.tensor_copy(first_i[:], first[:]).then_inc(first_ready, 1)
            dve.wait_ge(all_in, 16)
            link(nc.vector.tensor_copy(all_f[:], all_i[:]))
            for c in range(ITEM_COLS):
                link(nc.vector.tensor_scalar(le[:], all_f[:], k.item_id[:, c:c + 1], None, ALU.is_le))
                link(nc.vector.tensor_reduce(win[:, c:c + 1], le[:], AX.X, ALU.add))
            link(nc.vector.tensor_scalar(win[:], win[:], -1.0, None, ALU.add))
            nc.vector.tensor_scalar(win8[:], win[:], float(WIN), None, ALU.mult).then_inc(win_ready, 1)
            link(nc.vector.tensor_tensor(tile_f[:], k.item_id[:], win[:], ALU.subtract))
            link(nc.vector.tensor_scalar(tile_f[:], tile_f[:], float(EDGE_TILES - 1), None, ALU.min))
            nc.vector.tensor_copy(tile_i[:], tile_f[:]).then_inc(tile_ready, 1)
            dve.wait_ge(win_t_done, 1)
            nc.vector.tensor_copy(win_t[:], ps_win[:]).then_inc(win_t_ready, 1)
            dve.wait_ge(win_ready, 1)
            for c in range(ITEM_COLS):
                s = c % 4
                dve.wait_ge(got[s], 32 * (c // 4 + 1))
                if c >= 4:
                    dve.wait_ge(t_done, 2 * (c - 3))
                link(nc.vector.tensor_single_scalar(rows_p[:, 0], rows_s[:, s], P - 1, ALU.bitwise_and))
                nc.vector.tensor_copy(rows_l[:, s], rows_p[:, 0]).then_inc(lane_ready, 1)
                link(nc.vector.tensor_single_scalar(rows_p[:, 1], rows_s[:, s], 7, ALU.arith_shift_right))
                link(nc.vector.tensor_copy(rows_h[:, s], rows_p[:, 1]))
                link(nc.vector.tensor_scalar(rows_c[:, s], rows_d[:, s], win8[:, c:c + 1], float(BLOCKS),
                                             ALU.subtract, ALU.mult))
                dve.wait_ge(lane_ready, c + 1)
                nc.vector.tensor_tensor(rows_c[:, s], rows_c[:, s], rows_h[:, s], ALU.add).then_inc(cell_ready, 1)
                dve.wait_ge(t_done, 2 * c + 2)
                dve.wait_ge(cell_ready, c + 1)
                nc.vector.tensor_copy(k.edge_lane[:, c * P:(c + 1) * P], ps_t[(2 * c) % 4][:]).then_inc(t_copied, 1)
                nc.vector.tensor_copy(k.edge_cell[:, c * P:(c + 1) * P], ps_t[(2 * c + 1) % 4][:]).then_inc(t_copied, 1)
            dve.wait_ge(row_in, 16)
            plan = k.plan[:].rearrange("o (n w) -> o n w", w=PLAN)
            items = lambda t: t[:, 0:ADJ_ITEMS].rearrange("o (n r) -> o n r", r=R)
            link(nc.vector.tensor_scalar(bank_row[:], win_row[:], BANKS - 1, 9, ALU.bitwise_and, ALU.logical_shift_left))
            for base, places, waits in PLAN_PARTS:
                n = len(places)
                nc.vector.tensor_copy(plan[:, :, base:base + n], items(bank_row)[:, :, places[0]:places[0] + n])
                for g, r in enumerate(waits):
                    nc.vector.tensor_scalar(plan[:, :, base + n + g], items(win_row)[:, :, r], 1.0, None, ALU.add)
            turns = k.lane_f[0:1, 1:BLOCKS]
            first_of = all_f[0:1, :].rearrange("o (b m) -> o b m", m=BLOCK_WINS)[:, 1:BLOCKS, :]
            link(nc.vector.tensor_scalar(turn_item[:], turns, float(R), None, ALU.mult))
            link(nc.vector.tensor_tensor(late[:], first_of[:, :, 0], turn_item[:], ALU.subtract))
            link(nc.vector.tensor_scalar(late[:], late[:], float(SUM_FROM), None, ALU.is_le))
            link(nc.vector.tensor_tensor(early[:], first_of[:, :, BANKS], turn_item[:], ALU.is_ge))
            link(nc.vector.tensor_tensor(late[:], late[:], early[:], ALU.mult))
            link(nc.vector.tensor_reduce(both[:], late[:], AX.X, ALU.min))
            nc.vector.tensor_copy(k.fits[:], both[:])
            nc.vector.tensor_copy(k.win_end[:, 0:WINS - 1], all_i[0:1, 1:WINS])
            nc.vector.memset(k.win_end[:, WINS - 1:WINS], ADJ_ITEMS)
            dve.wait_ge(t_copied, 2 * ITEM_COLS)
            nc.vector.memset(k.edge_cell[:, ITEMS:], -1.0)

        @block.scalar
        def _(act):
            act.wait_ge(minus_ready, 1)

            def differences(n):
                for r in range(HRING):
                    if not (isinstance(n, int) and n == 0):
                        act.wait_ge(diff_used, n * HRING + (r + 1 - HRING))
                    for g in range(DIFFS):
                        a = nc.scalar.activation(diff[:, r, g], k.lane_b[:], ACT.Identity,
                                                 bias=minus_lo[:, bass.ds(n * (HRING * GRP) + (r * GRP + g), 1)])
                    a.then_inc(diff_ready, 1)
            differences(0)
            with nc.scalar.Fori(1, HTURNS) as n:
                differences(n)
            act.wait_ge(deg_ready, 2)
            nc.scalar.activation(tot[:], tmp[:], ACT.Sqrt).then_inc(root_done, 1)

        @block.gpsimd
        def _(pool):
            nc.gpsimd.memset(below[:], 1.0).then_inc(consts, 1)
            pool.wait_ge(consts, 1)
            nc.gpsimd.affine_select(out=below[:], in_=below[:], compare_op=ALU.is_gt, fill=0.0, base=0,
                                    pattern=[[WIN, BLOCK_WINS]], channel_multiplier=-1).then_inc(consts, 1)
            nc.gpsimd.iota(win_id[:], pattern=[[BLOCK_WINS, BLOCKS]], base=0, channel_multiplier=1).then_inc(consts, 1)
            pool.wait_ge(tile_ready, 1)
            for c in range(ITEM_COLS):
                if c >= 4:
                    pool.wait_ge(cell_ready, c - 3)
                for rows, name in ((rows_s, "src"), (rows_d, "dst")):
                    pool.indirect_dma_start(
                        out=rows[:, c % 4, :], out_offset=None, in_=k.io[name].rearrange("(t e) -> t e", e=P),
                        in_offset=bass.IndirectOffsetOnAxis(ap=tile_i[:, c:c + 1], axis=0)).then_inc(got[c % 4], 16)

        @block.tensor
        def _(pe):
            def group(n, first=False, last=False):
                for r in range(HRING):
                    pe.wait_ge(lo_done, n * HRING + r + 1)
                    pe.wait_ge(hi_done, n * HRING + r + 1)
                    pe.wait_ge(diff_used, n * HRING + r + 1)
                    for g in range(GRP):
                        mm = nc.tensor.matmul(ps_deg[:], oh_lo[:, r, g, :], oh_hi[:, r, g, :],
                                              start=first and r == 0 and g == 0,
                                              stop=last and r == HRING - 1 and g == GRP - 1)
                    mm.then_inc(groups_done, 1)
            group(0, first=True)
            with nc.tensor.Fori(1, HTURNS - 1) as n:
                group(n)
            group(HTURNS - 1, last=True)
            pe.wait_ge(deg_ready, 1)
            pe.wait_ge(consts, 2)
            nc.tensor.matmul(ps_in[:], below[:], deg[:], start=True, stop=True)
            nc.tensor.matmul(ps_tot[:], k.ones[:], deg[:], start=True, stop=True).then_inc(tot_done, 1)
            pe.wait_ge(win_ready, 1)
            nc.tensor.transpose(ps_win[:], win[:], k.ident[:]).then_inc(win_t_done, 1)
            for c in range(ITEM_COLS):
                for j, rows, ready in ((0, rows_l, lane_ready), (1, rows_c, cell_ready)):
                    pe.wait_ge(ready, c + 1)
                    if c >= 2:
                        pe.wait_ge(t_copied, 2 * c + j - 3)
                    nc.tensor.transpose(ps_t[(2 * c + j) % 4][:], rows[:, c % 4, :], k.ident[:]).then_inc(t_done, 1)


def build_input_rows(k):
    nc = k.nc
    with ExitStack() as st:
        sb, pb, sem = local(nc, st)
        w = sb("p_w", [P, KF, D], fp32)
        x = sb("p_x", [P, 2, U, D], fp32)
        z = sb("p_z", [P, 2, U, D], fp32)
        zt = sb("p_zt", [P, U, D], fp32)
        h = sb("p_h", [P, U, D], fp32)
        stats = sb("p_stats", [P, 2, U, 6], fp32)
        mv = sb("p_mv", [P, 2, U, 2], fp32)
        ps_t = [pb(f"pp_t{i}", [P, D], fp32) for i in range(RING)]
        ps_h = [pb(f"pp_h{i}", [P, D], fp32) for i in range(RING)]
        w_in, root, ln, z_ready, t_done, t_copied, h_done, scaled, hi_done, lo_done = (
            sem("p_" + s) for s in ("w_in", "root", "ln", "z_ready", "t_done", "t_copied", "h_done", "scaled",
                                    "hi_done", "lo_done"))
        x_in = [[sem(f"p_x_in{q}_{u}") for u in range(U)] for q in range(2)]
        block = st.enter_context(nc.Block())

        def is_turn(i, n):
            return isinstance(i, int) and i == n

        @block.sync
        def _(sp):
            sp.dma_start(w[:], k.io["L0_gnn_W1"].rearrange("(c p) n -> p c n", p=P)).then_inc(w_in, 16)

            def turn(i, q, uses, first):
                if not first:
                    sp.wait_ge(z_ready, i * U - U)
                for u in range(U):
                    sp.dma_start(x[:, q, u, :], k.io["x"][bass.ds((i * U + u) * P, P), :]).then_inc(x_in[q][u], 16)
            in_pairs(nc.sync, TURNS, turn)

        @block.vector
        def _(dve):
            def norms(i, q, uses, first):
                if not first:
                    dve.wait_ge(t_done, i * U - U)
                for u in range(U):
                    dve.wait_ge(x_in[q][u], uses * 16)
                hold_waits(k, nc.vector)
                for u in range(U):
                    nc.vector.bn_stats(stats[:, q, u, :], x[:, q, u, :]).then_inc(ln, 1)
                dve.wait_ge(ln, i * LN_STEPS + U)
                hold_waits(k, nc.vector)
                for u in range(U):
                    nc.vector.bn_aggr(mv[:, q, u, :], stats[:, q, u, :]).then_inc(ln, 1)
                dve.wait_ge(root, i + 1)
                nc.vector.reciprocal(mv[:, q, :, 1], mv[:, q, :, 1]).then_inc(ln, 1)
                dve.wait_ge(ln, i * LN_STEPS + LN_STEPS)
                for u in range(U):
                    nc.vector.tensor_scalar(z[:, q, u, :], x[:, q, u, :], mv[:, q, u, 0:1], mv[:, q, u, 1:2],
                                            ALU.subtract, ALU.mult).then_inc(z_ready, 1)

            def finish(i):
                for u in range(U):
                    dve.wait_ge(h_done, i * U + u + 1)
                    if not is_turn(i, 0):
                        dve.wait_ge(hi_done, i * U + (u + 1 - U))
                        dve.wait_ge(lo_done, i * U + (u + 1 - U))
                    nc.vector.tensor_scalar(h[:, u, :], ps_h[u % RING], k.dinv_in[:, bass.ds(i * U + u, 1)], None,
                                            ALU.mult).then_inc(scaled, 1)
                for u in range(U):
                    dve.wait_ge(scaled, i * U + u + 1)
                    dve.wait_ge(hi_done, i * U + u + 1)
                    rows = k.rows[0][:, bass.ds(i * U + u, 1), :][:, 0, :]
                    nc.vector.tensor_tensor(rows[:, D:2 * D], h[:, u, :], rows[:, 0:D], ALU.subtract).then_inc(lo_done, 1)

            def turn(i, q, uses, first):
                norms(i, q, uses, first)
                if not is_turn(i, 0):
                    finish(i - 1)
            in_pairs(nc.vector, TURNS, turn)
            finish(TURNS - 1)

        @block.scalar
        def _(act):
            def copies(i):
                for u in range(U):
                    act.wait_ge(t_done, i * U + u + 1)
                    if not is_turn(i, 0):
                        act.wait_ge(h_done, i * U + (u + 1 - U))
                    nc.scalar.activation(zt[:, u, :], ps_t[u % RING], ACT.Copy).then_inc(t_copied, 1)

            def high_halves(i):
                for u in range(U):
                    act.wait_ge(scaled, i * U + u + 1)
                    nc.scalar.activation(k.rows[0][:, bass.ds(i * U + u, 1), 0:D][:, 0, :], h[:, u, :],
                                         ACT.Copy).then_inc(hi_done, 1)

            def turn(i, q, uses, first):
                if not is_turn(i, 0):
                    copies(i - 1)
                act.wait_ge(ln, i * LN_STEPS + 2 * U)
                nc.scalar.activation(mv[:, q, :, 1], mv[:, q, :, 1], ACT.Sqrt, bias=k.eps[:]).then_inc(root, 1)
                if not is_turn(i, 0):
                    high_halves(i - 1)
            in_pairs(nc.scalar, TURNS, turn)
            copies(TURNS - 1)
            high_halves(TURNS - 1)

        @block.tensor
        def _(pe):
            pe.wait_ge(w_in, 16)

            def turn(i, q, uses, first):
                for u in range(U):
                    pe.wait_ge(z_ready, i * U + u + 1)
                    if not (is_turn(i, 0) and u < RING):
                        pe.wait_ge(t_copied, i * U + (u + 1 - since(u)))
                    for c in range(KF):
                        mm = nc.tensor.transpose(ps_t[u % RING][:, c * P:(c + 1) * P], z[:, q, u, c * P:(c + 1) * P],
                                                 k.ident[:])
                    mm.then_inc(t_done, 1)
                for u in range(U):
                    pe.wait_ge(t_copied, i * U + u + 1)
                    if not (is_turn(i, 0) and u < RING):
                        pe.wait_ge(scaled, i * U + (u + 1 - since(u)))
                    for c in range(KF):
                        mm = nc.tensor.matmul(ps_h[u % RING], zt[:, u, c * P:(c + 1) * P], w[:, c, :], start=c == 0,
                                              stop=c == KF - 1)
                    mm.then_inc(h_done, 1)
            in_pairs(nc.tensor, TURNS, turn)


def build_adjacency_and_sums(k):
    nc = k.nc
    with ExitStack() as st:
        sb, pb, sem = local(nc, st)
        cells = sb("j_cells", [P, CELLS], fp16)
        cells_i = sb("j_cells_i", [P, CELLS], i32)
        oh_lane = sb("j_oh_lane", [P, R, P], fp16)
        oh_cell = sb("j_oh_cell", [P, R, CELLS], fp16)
        zeros = sb("j_zeros", [P, CELLS], fp16)
        counts = sb("j_counts", [P, 2, BLOCKS, P], fp16)
        brow = sb("j_b1", [P, D], fp32)
        ps = st.enter_context(nc.psum_tensor("jp", [P, BANKS * BANK], fp32))
        ps_o = [pb(f"jp_o{q}", [P, 2 * D], fp32) for q in range(2)]
        (iota_done, cells_ready, lane_ready, cell_ready, item_done, emptied, zeroed, block_ready, zeros_set, b_in, summed,
         half, out_ready) = (sem("j_" + x) for x in (
             "iota", "cells", "lane", "cell", "item", "emptied", "zeroed", "block", "zeros", "b_in", "summed", "half",
             "out"))
        stored = [sem(f"j_stored{q}") for q in range(2)]
        adj_in = [sem(f"j_adj_in{q}") for q in range(2)]
        block = st.enter_context(nc.Block())

        def bank(j):
            return ps[:, (j % BANKS) * BANK:(j % BANKS) * BANK + CELLS]

        def choose(eng, together, apart):
            flag = eng.alloc_register("j_fits")
            eng.load([flag], k.fits[0:1, 0:1])
            fits = eng.snap(flag, min_val=0, max_val=1)
            with eng.If(fits > 0):
                together()
            with eng.Else():
                apart()

        @block.gpsimd
        def _(pool):
            nc.gpsimd.iota(cells_i[:], pattern=[[1, CELLS]], base=0, channel_multiplier=0).then_inc(iota_done, 1)
            nc.gpsimd.memset(zeros[:], 0.0).then_inc(zeros_set, 1)

        @block.vector
        def _(dve):
            dve.wait_ge(iota_done, 1)
            nc.vector.tensor_copy(cells[:], cells_i[:]).then_inc(cells_ready, 1)
            dve.wait_ge(cells_ready, 1)
            dve.wait_ge(b_in, 16)

            def one_hots(i, q, uses, first):
                for r in range(R):
                    if r % LANES == 0:
                        if not (isinstance(i, int) and i == 0):
                            dve.wait_ge(item_done, i * R + (r + LANES - R))
                        nc.vector.tensor_tensor(oh_lane[:, r:r + LANES], bc(k.lane_b[:, None, :], [P, LANES, P]),
                                                bc(k.edge_lane[:, bass.ds(i * R + r, LANES)][:, :, None], [P, LANES, P]),
                                                ALU.is_equal).then_inc(lane_ready, 1)
                    nc.vector.tensor_scalar(oh_cell[:, r, :], cells[:], k.edge_cell[:, bass.ds(i * R + r, 1)], None,
                                            ALU.is_equal).then_inc(cell_ready, 1)

            def finish(b, q):
                dve.wait_ge(summed, b + 1)
                d = k.dinv_out[:, bass.ds(b, 1)]
                z = k.z[:, bass.ds(b, 1), :][:, 0, :]
                nc.vector.scalar_tensor_tensor(z, ps_o[q][:, 0:D], d, brow[:], ALU.mult, ALU.add).then_inc(half, 1)
                dve.wait_ge(half, b + 1)
                nc.vector.scalar_tensor_tensor(z, ps_o[q][:, D:2 * D], d, z, ALU.mult, ALU.add).then_inc(out_ready, 1)

            def together():
                def turn(i, q, uses, first):
                    one_hots(i, q, uses, first)
                    if not first:
                        finish(i - 2, q)
                in_pairs(nc.vector, BLOCKS, turn)
                finish(BLOCKS - 2, 1)
                finish(BLOCKS - 1, 0)

            def apart():
                in_pairs(nc.vector, BLOCKS, one_hots)
                in_pairs(nc.vector, BLOCKS, lambda i, q, uses, first: finish(i, q))
            choose(nc.vector, together, apart)

        @block.tensor
        def _(pe):
            regs = [nc.tensor.alloc_register(f"j_plan{m}") for m in range(max(len(b) + len(w) for _, b, w in PLAN_PARTS))]

            def items(i, q, uses, first, between=None):
                for base, places, waits in PLAN_PARTS:
                    n = len(places) + len(waits)
                    nc.tensor.load(regs[0:n], k.plan[0:1, bass.ds(i * PLAN + base, n)])
                    banks = [nc.tensor.snap(g, min_val=0, max_val=(BANKS - 1) * BANK) for g in regs[0:len(places)]]
                    begun = [nc.tensor.snap(g, min_val=1, max_val=WINS) for g in regs[len(places):n]]
                    for j, r in enumerate(places):
                        if r % LANES == 0:
                            pe.wait_ge(lane_ready, i * (R // LANES) + (r // LANES + 1))
                        if j % G == 0:
                            pe.wait_ge(zeroed, begun[j // G])
                        pe.wait_ge(cell_ready, i * R + r + 1)
                        nc.tensor.matmul(ps[:, bass.ds(banks[j], CELLS)], oh_lane[:, r, :], oh_cell[:, r, :],
                                         start=False, stop=True, skip_group_check=True).then_inc(item_done, 1)
                        if between and (r + 1) % LANES == 0 and r + 1 >= SUM_FROM:
                            between((r + 1 - SUM_FROM) // LANES)

            def sum_part(b, q, begun, part, parts=1):
                if part == 0:
                    if begun:
                        pe.wait_ge(out_ready, b - 1)
                    nc.tensor.matmul(ps_o[q], k.self_loop[:], k.rows[0][:, bass.ds(b, 1), :][:, 0, :], start=True,
                                     stop=False)
                for s in range(part * BLOCKS // parts, (part + 1) * BLOCKS // parts):
                    mm = nc.tensor.matmul(ps_o[q], counts[:, q, s, :], k.rows[0][:, s, :], start=False,
                                          stop=s == BLOCKS - 1)
                if part == parts - 1:
                    mm.then_inc(summed, 1)

            def together():
                def turn(i, q, uses, first):
                    def part(j):
                        if j == 0:
                            pe.wait_ge(block_ready, i)
                        sum_part(i - 1, 1 - q, not (isinstance(i, int) and i < 3), j, (R - SUM_FROM) // LANES + 1)
                    items(i, q, uses, first, None if isinstance(i, int) and i == 0 else part)
                in_pairs(nc.tensor, BLOCKS, turn)
                pe.wait_ge(block_ready, BLOCKS)
                sum_part(BLOCKS - 1, 0, True, 0)

            def apart():
                def turn(i, q, uses, first):
                    pe.wait_ge(adj_in[q], 16 * uses)
                    sum_part(i, q, not first, 0)
                in_pairs(nc.tensor, BLOCKS, items)
                in_pairs(nc.tensor, BLOCKS, turn)
            choose(nc.tensor, together, apart)

        @block.scalar
        def _(act):
            regs = [nc.scalar.alloc_register(f"j_end{m}") for m in range(BLOCK_WINS)]
            act.wait_ge(zeros_set, 1)
            for j in range(BANKS):
                nc.scalar.activation(bank(j), zeros[:], ACT.Copy).then_inc(zeroed, 1)

            def empty(i, q, uses, first, used):
                nc.scalar.load(regs, k.win_end[0:1, bass.ds(i * BLOCK_WINS, BLOCK_WINS)])
                ends = [nc.scalar.snap(r, min_val=1, max_val=ADJ_ITEMS) for r in regs]
                if not first:
                    act.wait_ge(stored[q], 16 * (uses - 1))
                    if used:
                        act.wait_ge(summed, i - 1)
                for j in range(BLOCK_WINS):
                    act.wait_ge(item_done, ends[j])
                    nc.scalar.activation(
                        counts[:, q, :, j * WIN:(j + 1) * WIN].rearrange("p h d -> p d h"),
                        bank(j).rearrange("p (d h) -> p d h", h=BLOCKS), ACT.Copy, scale=COUNT_SCALE).then_inc(emptied, 1)
                    act.wait_ge(emptied, i * BLOCK_WINS + (j + 1))
                    nc.scalar.activation(bank(j), zeros[:], ACT.Copy).then_inc(zeroed, 1)
                nc.scalar.activation(k.held_act[:], k.ones[:, 0:1], ACT.Copy).then_inc(block_ready, 1)
            choose(nc.scalar, lambda: in_pairs(nc.scalar, BLOCKS, lambda *a: empty(*a, True)),
                   lambda: in_pairs(nc.scalar, BLOCKS, lambda *a: empty(*a, False)))

        @block.sync
        def _(sp):
            sp.dma_start(brow[:], k.io["L0_gnn_b1"][None, :].to_broadcast([P, D])).then_inc(b_in, 16)

            def store(i, q, uses, first):
                sp.wait_ge(block_ready, i + 1)
                sp.dma_start(k.adj[bass.ds(i, 1)][0], counts[:, q].rearrange("p h d -> p (h d)")).then_inc(stored[q], 16)

            def all_stored():
                for q in range(2):
                    sp.wait_ge(stored[q], 16 * ((BLOCKS + 1 - q) // 2))

            def together():
                in_pairs(nc.sync, BLOCKS, store)
                all_stored()

            def apart():
                def load(i, q, uses, first):
                    if not first:
                        sp.wait_ge(summed, i - 1)
                    sp.dma_start(counts[:, q].rearrange("p h d -> p (h d)"), k.adj[bass.ds(i, 1)][0]).then_inc(adj_in[q], 16)
                in_pairs(nc.sync, BLOCKS, store)
                all_stored()
                in_pairs(nc.sync, BLOCKS, load)
            choose(nc.sync, together, apart)


def build_second_rows(k):
    nc = k.nc
    with ExitStack() as st:
        sb, pb, sem = local(nc, st)
        w = sb("l_w", [P, KF, D], fp32)
        zr = sb("l_zr", [P, 2, U, D], fp32)
        zt = sb("l_zt", [P, U, D], fp32)
        h = sb("l_h", [P, U, D], fp32)
        ps_t = [pb(f"lp_t{i}", [P, D], fp32) for i in range(RING)]
        ps_h = [pb(f"lp_h{i}", [P, D], fp32) for i in range(RING)]
        w_in, z_ready, t_done, t_copied, h_done, scaled, hi_done, lo_done = (
            sem("l_" + s) for s in ("w_in", "z_ready", "t_done", "t_copied", "h_done", "scaled", "hi_done", "lo_done"))
        block = st.enter_context(nc.Block())

        @block.sync
        def _(sp):
            sp.dma_start(w[:], k.io["L0_gnn_W2"].rearrange("(c p) n -> p c n", p=P)).then_inc(w_in, 16)

        @block.tensor
        def _(pe):
            pe.wait_ge(w_in, 16)

            def turn(i, q, uses, first):
                for u in range(U):
                    pe.wait_ge(z_ready, i * U + u + 1)
                    if not (isinstance(i, int) and i == 0 and u < RING):
                        pe.wait_ge(t_copied, i * U + (u + 1 - since(u)))
                    for c in range(KF):
                        mm = nc.tensor.transpose(ps_t[u % RING][:, c * P:(c + 1) * P], zr[:, q, u, c * P:(c + 1) * P],
                                                 k.ident[:])
                    mm.then_inc(t_done, 1)
                for u in range(U):
                    pe.wait_ge(t_copied, i * U + u + 1)
                    if not (isinstance(i, int) and i == 0 and u < RING):
                        pe.wait_ge(scaled, i * U + (u + 1 - since(u)))
                    for c in range(KF):
                        mm = nc.tensor.matmul(ps_h[u % RING], zt[:, u, c * P:(c + 1) * P], w[:, c, :], start=c == 0,
                                              stop=c == KF - 1)
                    mm.then_inc(h_done, 1)
            in_pairs(nc.tensor, TURNS, turn)

        @block.scalar
        def _(act):
            def turn(i, q, uses, first):
                for u in range(U):
                    act.wait_ge(t_done, i * U + u + 1)
                    if not (isinstance(i, int) and i == 0):
                        act.wait_ge(h_done, i * U + (u + 1 - U))
                    nc.scalar.activation(zt[:, u, :], ps_t[u % RING], ACT.Copy).then_inc(t_copied, 1)
                for u in range(U):
                    act.wait_ge(scaled, i * U + u + 1)
                    nc.scalar.activation(k.rows[1][:, bass.ds(i * U + u, 1), 0:D][:, 0, :], h[:, u, :],
                                         ACT.Copy).then_inc(hi_done, 1)
            in_pairs(nc.scalar, TURNS, turn)

        @block.vector
        def _(dve):
            def relu(i, q, first):
                for u in range(U):
                    if not first:
                        dve.wait_ge(t_done, i * U + (u + 1 - 2 * U))
                    nc.vector.tensor_scalar(zr[:, q, u, :], k.z[:, bass.ds(i * U + u, 1), :][:, 0, :], 0.0, None,
                                            ALU.max).then_inc(z_ready, 1)

            def finish(i):
                for u in range(U):
                    dve.wait_ge(h_done, i * U + u + 1)
                    if not (isinstance(i, int) and i == 0):
                        dve.wait_ge(hi_done, i * U + (u + 1 - U))
                        dve.wait_ge(lo_done, i * U + (u + 1 - U))
                    nc.vector.tensor_scalar(h[:, u, :], ps_h[u % RING], k.dinv_in[:, bass.ds(i * U + u, 1)], None,
                                            ALU.mult).then_inc(scaled, 1)
                for u in range(U):
                    dve.wait_ge(scaled, i * U + u + 1)
                    dve.wait_ge(hi_done, i * U + u + 1)
                    rows = k.rows[1][:, bass.ds(i * U + u, 1), :][:, 0, :]
                    nc.vector.tensor_tensor(rows[:, D:2 * D], h[:, u, :], rows[:, 0:D], ALU.subtract).then_inc(lo_done, 1)

            def turn(i, q, uses, first):
                relu(i, q, first)
                if not (isinstance(i, int) and i == 0):
                    finish(i - 1)
            in_pairs(nc.vector, TURNS, turn)
            finish(TURNS - 1)


AHEAD = BLOCKS // 2


def aggregate(k, pe, i, q, uses, adj, adj_in, rows, ps, part):
    nc = k.nc
    if part == 0:
        pe.wait_ge(adj_in[q], 16 * uses)
        nc.tensor.matmul(ps, k.self_loop[:], rows[:, bass.ds(i, 1), :][:, 0, :], start=True, stop=False)
    for s in (range(0, AHEAD) if part == 0 else range(AHEAD, BLOCKS)):
        mm = nc.tensor.matmul(ps, adj[:, q, s * P:(s + 1) * P], rows[:, s, :], start=False, stop=s == BLOCKS - 1)
    return mm


def load_adjacency(k, sp, adj, adj_in, summed, more=None):
    def turn(i, q, uses, first):
        if not first:
            sp.wait_ge(summed, i - 1)
        sp.dma_start(adj[:, q, :], k.adj[bass.ds(i, 1)][0]).then_inc(adj_in[q], 16)
        if more:
            more(i, q, uses, first)
    in_pairs(k.nc.sync, BLOCKS, turn)


def build_layer_two(k):
    nc = k.nc
    k.xn_rows = k.dr("xn_rows", [ROWS, D], fp32)
    with ExitStack() as st:
        sb, pb, sem = local(nc, st)
        wr = sb("r_wr", [P, KF, EXPERTS], fp32)
        br = sb("r_br", [P, EXPERTS], fp32)
        brow = sb("r_b2", [P, D], fp32)
        adj = sb("r_adj", [P, 2, BLOCKS * P], fp16)
        x = sb("r_x", [P, 2, D], fp32)
        pre = sb("r_pre", [P, 2, D], fp32)
        x2 = sb("r_x2", [P, 2, D], fp32)
        z = sb("r_z", [P, 2, D], fp32)
        xn = sb("r_xn", [P, 2, D], fp32)
        zt = sb("r_zt", [P, 2, D], fp32)
        stats = sb("r_stats", [P, 2, 6], fp32)
        mv = sb("r_mv", [P, 2, 2], fp32)
        ps_o = [pb(f"rp_o{i}", [P, 2 * D], fp32) for i in range(2)]
        ps_t = [pb(f"rp_t{i}", [P, D], fp32) for i in range(2)]
        ps_l = [pb(f"rp_l{i}", [P, EXPERTS], fp32) for i in range(2)]
        w_in, summed, half, out_ready, step, var_ready, root, x2_ready, xt_ready, xn_ready, t_done, t_copied, l_done, logit = (
            sem("r_" + s) for s in ("w_in", "summed", "half", "out", "step", "var", "root", "x2", "xt", "xn", "t_done",
                                    "t_copied", "l_done", "logit"))
        adj_in = [sem(f"r_adj_in{q}") for q in range(2)]
        x_in = [sem(f"r_x_in{q}") for q in range(2)]
        x2_out = [sem(f"r_x2_out{q}") for q in range(2)]
        xn_out = [sem(f"r_xn_out{q}") for q in range(2)]
        block = st.enter_context(nc.Block())
        STEPS = 4
        zero = sb("r_zero", [P, D], fp32)
        zero_set, zero_out = sem("r_zero_set"), sem("r_zero_out")

        @block.gpsimd
        def _(pool):
            nc.gpsimd.memset(zero[:], 0.0).then_inc(zero_set, 1)
            pool.wait_ge(zero_set, 1)
            for rows in (k.io["out"], k.xn_rows):
                pool.dma_start(rows[PAD_NODES:ROWS, :], zero[:]).then_inc(zero_out, 16)
            pool.wait_ge(zero_out, 32)

        @block.sync
        def _(sp):
            sp.dma_start(wr[:], k.io["L0_ffn_Wr"].rearrange("(c p) n -> p c n", p=P)).then_inc(w_in, 16)
            sp.dma_start(br[:], k.io["L0_ffn_br"][None, :].to_broadcast([P, EXPERTS])).then_inc(w_in, 16)
            sp.dma_start(brow[:], k.io["L0_gnn_b2"][None, :].to_broadcast([P, D])).then_inc(w_in, 16)

            def residual(i, q, uses, first):
                if not first:
                    sp.wait_ge(x2_ready, i - 1)
                sp.dma_start(x[:, q, :], k.io["x"][bass.ds(i * P, P), :]).then_inc(x_in[q], 16)
            load_adjacency(k, sp, adj, adj_in, summed, residual)

        @block.tensor
        def _(pe):
            pe.wait_ge(w_in, 48)

            def transposes(i, q, first):
                pe.wait_ge(xt_ready, i + 1)
                if not first:
                    pe.wait_ge(t_copied, i - 1)
                for c in range(KF):
                    mm = nc.tensor.transpose(ps_t[q][:, c * P:(c + 1) * P], z[:, q, c * P:(c + 1) * P], k.ident[:])
                mm.then_inc(t_done, 1)

            def products(i, q, first):
                pe.wait_ge(t_copied, i + 1)
                if not first:
                    pe.wait_ge(logit, i - 1)
                for c in range(KF):
                    mm = nc.tensor.matmul(ps_l[q], zt[:, q, c * P:(c + 1) * P], wr[:, c, :], start=c == 0, stop=c == KF - 1)
                mm.then_inc(l_done, 1)

            def turn(i, q, uses, first):
                if not first:
                    pe.wait_ge(out_ready, i - 1)
                aggregate(k, pe, i, q, uses, adj, adj_in, k.rows[1], ps_o[q], 0)
                if not (isinstance(i, int) and i == 0):
                    transposes(i - 1, 1 - q, isinstance(i, int) and i < 3)
                aggregate(k, pe, i, q, uses, adj, adj_in, k.rows[1], ps_o[q], 1).then_inc(summed, 1)
                if not (isinstance(i, int) and i == 0):
                    products(i - 1, 1 - q, isinstance(i, int) and i < 3)
            in_pairs(nc.tensor, BLOCKS, turn)
            transposes(BLOCKS - 1, 0, False)
            products(BLOCKS - 1, 0, False)

        @block.vector
        def _(dve):
            dve.wait_ge(w_in, 48)

            def finish(i, q):
                dve.wait_ge(l_done, i + 1)
                nc.vector.tensor_tensor(k.logits[:, bass.ds(i, 1), :][:, 0, :], ps_l[q], br[:], ALU.add).then_inc(logit, 1)

            def norm(i, q, src, out, s0, v, done):
                nc.vector.bn_stats(stats[:, q, :], src).then_inc(step, 1)
                dve.wait_ge(step, s0 + 1)
                hold_waits(k, nc.vector)
                nc.vector.bn_aggr(mv[:, q, :], stats[:, q, :]).then_inc(var_ready, 1)
                dve.wait_ge(root, v)
                nc.vector.reciprocal(mv[:, q, 1:2], mv[:, q, 1:2]).then_inc(step, 1)
                dve.wait_ge(step, s0 + 2)
                nc.vector.tensor_scalar(out, src, mv[:, q, 0:1], mv[:, q, 1:2], ALU.subtract, ALU.mult).then_inc(done, 1)

            def turn(i, q, uses, first):
                dve.wait_ge(summed, i + 1)
                d = k.dinv_out[:, bass.ds(i, 1)]
                nc.vector.scalar_tensor_tensor(pre[:, q, :], ps_o[q][:, 0:D], d, brow[:], ALU.mult, ALU.add).then_inc(half, 1)
                dve.wait_ge(half, i + 1)
                nc.vector.scalar_tensor_tensor(pre[:, q, :], ps_o[q][:, D:2 * D], d, pre[:, q, :], ALU.mult,
                                               ALU.add).then_inc(out_ready, 1)
                dve.wait_ge(out_ready, i + 1)
                dve.wait_ge(x_in[q], 16 * uses)
                if not first:
                    dve.wait_ge(x2_out[q], 16 * (uses - 1))
                    dve.wait_ge(xn_out[q], 16 * (uses - 1))
                    dve.wait_ge(t_done, i - 1)
                nc.vector.scalar_tensor_tensor(x2[:, q, :], pre[:, q, :], 0.0, x[:, q, :], ALU.max, ALU.add).then_inc(x2_ready, 1)
                dve.wait_ge(x2_ready, i + 1)
                hold_waits(k, nc.vector)
                norm(i, q, x2[:, q, :], z[:, q, :], i * STEPS, i * 2 + 1, xt_ready)
                dve.wait_ge(xt_ready, i + 1)
                hold_waits(k, nc.vector)
                norm(i, q, z[:, q, :], xn[:, q, :], i * STEPS + 2, i * 2 + 2, xn_ready)
                if not (isinstance(i, int) and i == 0):
                    finish(i - 1, 1 - q)
            in_pairs(nc.vector, BLOCKS, turn)
            finish(BLOCKS - 1, 0)

        @block.scalar
        def _(act):
            def copies(i, q, first):
                act.wait_ge(t_done, i + 1)
                if not first:
                    act.wait_ge(l_done, i - 1)
                nc.scalar.activation(zt[:, q, :], ps_t[q], ACT.Copy).then_inc(t_copied, 1)

            def turn(i, q, uses, first):
                if not (isinstance(i, int) and i == 0):
                    copies(i - 1, 1 - q, isinstance(i, int) and i < 3)
                for t in range(2):
                    act.wait_ge(var_ready, i * 2 + t + 1)
                    nc.scalar.activation(mv[:, q, 1:2], mv[:, q, 1:2], ACT.Sqrt, bias=k.eps[:]).then_inc(root, 1)
                act.wait_ge(x2_ready, i + 1)
                act.dma_start(k.io["out"][bass.ds(i * P, P), :], x2[:, q, :]).then_inc(x2_out[q], 16)
                act.wait_ge(xn_ready, i + 1)
                act.dma_start(k.xn_rows[bass.ds(i * P, P), :], xn[:, q, :]).then_inc(xn_out[q], 16)
            in_pairs(nc.scalar, BLOCKS, turn)
            copies(BLOCKS - 1, 0, False)
            for q in range(2):
                act.wait_ge(x2_out[q], 16 * ((BLOCKS + 1 - q) // 2))
                act.wait_ge(xn_out[q], 16 * ((BLOCKS + 1 - q) // 2))


class ExpertWeights:
    W = KF * HIDDEN
    LOADS = 2 * EXPERTS
    RAW = 3
    assert KF * HIDDEN == HB * D

    def __init__(self, k, sb, pb, sem):
        self.k = k
        self.raw = sb("w_raw", [P, self.RAW, self.W], fp32)
        self.scaled = sb("w_scaled", [P, self.W], fp32)
        self.gb_rows = sb("w_gb_rows", [2 * EXPERTS * KF, P], fp32)
        self.b1_rows = sb("w_b1_rows", [EXPERTS * HB, P], fp32)
        self.gb = sb("w_gb", [P, 2, EXPERTS, KF], fp32)
        self.ps_t = pb("wp_t", [P, (2 * KF + HB) * EXPERTS], fp32)
        self.ps_b = pb("wp_b", [P, EXPERTS * HB], fp32)
        self.small_in, self.small_t, self.gb_ready, self.offset_done, self.scaled_ready, self.hi, self.lo = (
            sem("w_" + x) for x in ("small_in", "small_t", "gb", "offset", "scaled", "hi", "lo"))
        self.raw_in = [sem(f"w_raw_in{r}") for r in range(self.RAW)]

    def sync(self, sp):
        k, n = self.k, EXPERTS * KF
        sp.dma_start(self.gb_rows[0:n, :], k.io["L0_ffn_ln_g"].rearrange("e (c p) -> (e c) p", p=P)).then_inc(self.small_in, 16)
        sp.dma_start(self.gb_rows[n:2 * n, :], k.io["L0_ffn_ln_b"].rearrange("e (c p) -> (e c) p", p=P)).then_inc(self.small_in, 16)
        sp.dma_start(self.b1_rows[:], k.io["L0_ffn_b1"].rearrange("e (c p) -> (e c) p", p=P)).then_inc(self.small_in, 16)
        sp.dma_start(k.b2[:], k.io["L0_ffn_b2"][None, :, :].to_broadcast([P, EXPERTS, D])).then_inc(self.small_in, 16)
        for i in range(self.LOADS):
            if i >= self.RAW:
                sp.wait_ge(self.scaled_ready, i - self.RAW + 1)
                sp.wait_ge(self.offset_done, (i - self.RAW) // 2 + 1)
            name, inner = ("L0_ffn_W1", HIDDEN) if i % 2 == 0 else ("L0_ffn_W2", D)
            sp.dma_start(self.raw[:, i % self.RAW].rearrange("p (c n) -> p c n", n=inner),
                         k.io[name][i // 2].rearrange("(c p) n -> p c n", p=P)).then_inc(self.raw_in[i % self.RAW], 16)

    def vector(self, dve):
        k, nc, raw, scaled = self.k, self.k.nc, self.raw, self.scaled
        dve.wait_ge(self.small_t, 1)
        gb = self.gb[:].rearrange("p t e c -> p t (e c)")
        ps = self.ps_t[:, 0:2 * KF * EXPERTS].rearrange("p (t n) -> p t n", t=2)
        nc.vector.tensor_scalar(gb[:, 0], ps[:, 0], SCALE, None, ALU.mult).then_inc(self.gb_ready, 1)
        nc.vector.tensor_copy(gb[:, 1], ps[:, 1]).then_inc(self.gb_ready, 1)
        nc.vector.tensor_copy(k.b1[:], self.ps_t[:, 2 * KF * EXPERTS:]).then_inc(self.gb_ready, 1)
        dve.wait_ge(self.gb_ready, 3)
        for i in range(self.LOADS):
            e, r = i // 2, i % self.RAW
            dve.wait_ge(self.raw_in[r], 16 * (i // self.RAW + 1))
            if i:
                dve.wait_ge(self.lo, i)
                dve.wait_ge(self.hi, i)
            if i % 2 == 0:
                for c in range(KF):
                    part = slice(c * HIDDEN, (c + 1) * HIDDEN)
                    mm = nc.vector.tensor_scalar(scaled[:, part], raw[:, r, part], self.gb[:, 0, e, c:c + 1], None, ALU.mult)
            else:
                mm = nc.vector.tensor_scalar(scaled[:], raw[:, r], SCALE, None, ALU.mult)
            mm.then_inc(self.scaled_ready, 1)
            dve.wait_ge(self.hi, i + 1)
            w = k.w1 if i % 2 == 0 else k.w2
            nc.vector.tensor_tensor(w[:, e, 1].rearrange("p c n -> p (c n)"), scaled[:],
                                    w[:, e, 0].rearrange("p c n -> p (c n)"), ALU.subtract).then_inc(self.lo, 1)
        dve.wait_ge(self.offset_done, EXPERTS)
        nc.vector.tensor_tensor(k.b1[:], self.ps_b[:], k.b1[:], ALU.add)

    def scalar(self, act):
        k, nc = self.k, self.k.nc
        for i in range(self.LOADS):
            act.wait_ge(self.scaled_ready, i + 1)
            w = k.w1 if i % 2 == 0 else k.w2
            nc.scalar.activation(w[:, i // 2, 0].rearrange("p c n -> p (c n)"), self.scaled[:], ACT.Copy).then_inc(self.hi, 1)

    def small_transposes(self, pe):
        k, nc, n = self.k, self.k.nc, 2 * KF * EXPERTS
        pe.wait_ge(self.small_in, 16 * 4)
        nc.tensor.transpose(self.ps_t[:, 0:n], self.gb_rows[:], k.ident[0:n, 0:n])
        nc.tensor.transpose(self.ps_t[:, n:], self.b1_rows[:], k.ident[0:HB * EXPERTS, 0:HB * EXPERTS]).then_inc(self.small_t, 1)

    def tensor(self, pe):
        nc, raw = self.k.nc, self.raw
        pe.wait_ge(self.gb_ready, 3)
        for e in range(EXPERTS):
            r = 2 * e % self.RAW
            pe.wait_ge(self.raw_in[r], 16 * (2 * e // self.RAW + 1))
            for h in range(HB):
                for c in range(KF):
                    mm = nc.tensor.matmul(self.ps_b[:, e * HB + h:e * HB + h + 1],
                                          raw[:, r, c * HIDDEN + h * P:c * HIDDEN + (h + 1) * P],
                                          self.gb[:, 1, e, c:c + 1], start=c == 0, stop=c == KF - 1)
            mm.then_inc(self.offset_done, 1)


def build_routing(k, kst):
    nc = k.nc
    slot_list = k.dr("slot_list", [SLOTS, 2], i32)
    NE = BLOCKS * EXPERTS
    own = lambda name, shape, dt: kst.enter_context(nc.sbuf_tensor(name, shape, dt))
    k.w1 = own("w1", [P, EXPERTS, 2, KF, HIDDEN], fp16)
    k.w2 = own("w2", [P, EXPERTS, 2, HB, D], fp16)
    k.b1 = own("b1", [P, EXPERTS * HB], fp32)
    k.b2 = own("b2", [P, EXPERTS, D], fp32)
    with ExitStack() as st:
        sb, pb, sem = local(nc, st)
        back = sb("o_back", [P, EXPERTS], fp32)
        best = sb("o_best", [P, 2, BLOCKS], fp32)
        rest = sb("o_rest", [P, BLOCKS, EXPERTS], fp32)
        pick = sb("o_pick", [P, BLOCKS], fp32)
        hot = sb("o_hot", [P, 2, BLOCKS, EXPERTS], fp32)
        both = sb("o_both", [P, BLOCKS, EXPERTS], fp32)
        inner = sb("o_inner", [P, BLOCKS, EXPERTS], fp32)
        tot = sb("o_tot", [P, EXPERTS, BLOCKS], fp32)
        cum = sb("o_cum", [P, EXPERTS, BLOCKS], fp32)
        ones = sb("o_ones", [P, BLOCKS], fp32)
        cnt = sb("o_cnt", [P, EXPERTS], fp32)
        cnt_i = sb("o_cnt_i", [P, EXPERTS], i32)
        tiles = sb("o_tiles", [P, EXPERTS], fp32)
        ends = sb("o_ends", [P, EXPERTS], fp32)
        begin = sb("o_begin", [P, EXPERTS], fp32)
        slot_f = sb("o_slot_f", [P, 2, BLOCKS], fp32)
        gap = sb("o_gap", [P, BLOCKS], fp32)
        ex = sb("o_ex", [P, BLOCKS], fp32)
        le = sb("o_le", [1, PAIRS, EXPERTS - 1], fp32)
        te = sb("o_te", [1, PAIRS], fp32)
        empty = sb("o_empty", [TOKEN_TILES, P, 2], i32)
        lst = sb("o_lst", [TOKEN_TILES, P, 2], i32)
        lst_f = sb("o_lst_f", [TOKEN_TILES, 2, P], fp32)
        stage = sb("o_stage", [P, 2, 2, U], i32)
        stage_row = sb("o_stage_row", [P, 2, 2, U, 2], i32)
        ps_in = pb("op_in", [P, NE], fp32)
        ps_tot = pb("op_tot", [P, NE], fp32)
        ps_l = pb("op_l", [P, 2 * TOKEN_TILES], fp32)
        s, hot_ready, pre_done, gap_ready, exp_done, slots_ready = (
            sem("o_" + x) for x in ("s", "hot", "pre", "gap", "exp", "slots"))
        zeroed, staged, list_in, lst_ready, lst_t = (
            sem("o_" + x) for x in ("zeroed", "staged", "list_in", "lst_ready", "lst_t"))
        put = [[sem(f"o_put{q}_{i}") for i in range(2 * U)] for q in range(2)]
        empty_set = sem("o_empty_set")
        weights = ExpertWeights(k, sb, pb, sem)
        block = st.enter_context(nc.Block())

        @block.vector
        def _(dve):
            count = [0]

            def link(ins):
                count[0] += 1
                ins.then_inc(s, 1)
                dve.wait_ge(s, count[0])

            nc.vector.memset(empty[:, :, 1], 0)
            nc.vector.tensor_scalar(empty[:, :, 0], k.lane_f[0:TOKEN_TILES, :], float(PAD_NODES), None,
                                    ALU.add).then_inc(empty_set, 1)
            link(nc.vector.memset(ones[:], 1.0))

            link(nc.vector.tensor_scalar(back[:], k.lane_f[:, 0:EXPERTS], float(-EXPERTS), None, ALU.add))
            full = [P, BLOCKS, EXPERTS]
            for c in range(2):
                src = k.logits if c == 0 else rest
                link(nc.vector.tensor_reduce(best[:, c, :], src[:], AX.X, ALU.max))
                link(nc.vector.tensor_tensor(inner[:], src[:], bc(best[:, c, :, None], full), ALU.is_equal))
                link(nc.vector.tensor_tensor(inner[:], inner[:], bc(back[:, None, :], full), ALU.mult))
                link(nc.vector.tensor_reduce(pick[:], inner[:], AX.X, ALU.min))
                link(nc.vector.tensor_tensor(hot[:, c], bc(back[:, None, :], full), bc(pick[:, :, None], full),
                                             ALU.is_equal))
                if c == 0:
                    link(nc.vector.scalar_tensor_tensor(rest[:], hot[:, 0], -3e38, k.logits[:], ALU.mult, ALU.add))
            link(nc.vector.tensor_tensor(gap[:], best[:, 1, :], best[:, 0, :], ALU.subtract))
            nc.vector.tensor_tensor(both[:], hot[:, 0], hot[:, 1], ALU.add).then_inc(hot_ready, 1)
            dve.wait_ge(exp_done, 1)
            link(nc.vector.tensor_scalar(gap[:], ex[:], 1.0, None, ALU.add))
            link(nc.vector.reciprocal(k.gate[:, 0, :], gap[:]))
            link(nc.vector.tensor_tensor(k.gate[:, 1, :], ex[:], k.gate[:, 0, :], ALU.mult))
            dve.wait_ge(pre_done, 1)
            link(nc.vector.tensor_copy(inner[:], ps_in[:].rearrange("p (b e) -> p b e", e=EXPERTS)))
            link(nc.vector.tensor_copy(tot[:], ps_tot[:].rearrange("p (b e) -> p e b", e=EXPERTS)))
            for e in range(EXPERTS):
                link(nc.vector.tensor_tensor_scan(cum[:, e, :], ones[:], tot[:, e, :], 0.0, ALU.mult, ALU.add))
            link(nc.vector.tensor_scalar(cnt[:], cum[:, :, BLOCKS - 1], float(PAIR - 1), None, ALU.add))
            link(nc.vector.tensor_copy(cnt_i[:], cnt[:]))
            link(nc.vector.tensor_single_scalar(cnt_i[:], cnt_i[:], 8, ALU.arith_shift_right))
            link(nc.vector.tensor_copy(tiles[:], cnt_i[:]))
            link(nc.vector.tensor_tensor_scan(ends[:], ones[:, 0:EXPERTS], tiles[:], 0.0, ALU.mult, ALU.add))
            link(nc.vector.tensor_tensor(begin[:], ends[:], tiles[:], ALU.subtract))
            link(nc.vector.tensor_scalar(begin[:], begin[:], float(PAIR), None, ALU.mult))
            link(nc.vector.tensor_tensor(cum[:], cum[:], tot[:], ALU.subtract))
            link(nc.vector.tensor_tensor(inner[:], inner[:], cum[:].rearrange("p e b -> p b e"), ALU.add))
            link(nc.vector.tensor_tensor(inner[:], inner[:], bc(begin[:, None, :], [P, BLOCKS, EXPERTS]), ALU.add))
            for c in range(2):
                link(nc.vector.tensor_tensor(hot[:, c], hot[:, c], inner[:], ALU.mult))
                link(nc.vector.tensor_reduce(slot_f[:, c, :], hot[:, c], AX.X, ALU.add))
            nc.vector.tensor_copy(k.slot[:], slot_f[:]).then_inc(slots_ready, 1)
            link(nc.vector.tensor_tensor(le[:], bc(ends[0:1, None, 0:EXPERTS - 1], [1, PAIRS, EXPERTS - 1]),
                                         bc(k.lane_f[0:1, 0:PAIRS, None], [1, PAIRS, EXPERTS - 1]), ALU.is_le))
            link(nc.vector.tensor_reduce(te[:], le[:], AX.X, ALU.add))
            nc.vector.memset(k.pair_expert[:, 0:1], 0)
            nc.vector.tensor_copy(k.pair_expert[:, 1:], te[:])
            weights.vector(dve)
            dve.wait_ge(list_in, 16)
            nc.vector.tensor_copy(lst_f[:, 0], lst[:, :, 0]).then_inc(lst_ready, 1)
            nc.vector.tensor_copy(lst_f[:, 1], lst[:, :, 1].bitcast(fp32)).then_inc(lst_ready, 1)
            dve.wait_ge(lst_t, 1)
            nc.vector.tensor_copy(k.slot_token[:], ps_l[:, 0:TOKEN_TILES])
            nc.vector.tensor_copy(k.slot_gate[:], ps_l[:, TOKEN_TILES:])

        @block.scalar
        def _(act):
            act.wait_ge(hot_ready, 1)
            nc.scalar.activation(ex[:], gap[:], ACT.Exp).then_inc(exp_done, 1)
            weights.scalar(act)

        @block.tensor
        def _(pe):
            pe.wait_ge(hot_ready, 1)
            flat = both[:].rearrange("p b e -> p (b e)")
            nc.tensor.matmul(ps_in[:], k.tri[:], flat, start=True, stop=True)
            nc.tensor.matmul(ps_tot[:], k.ones[:], flat, start=True, stop=True).then_inc(pre_done, 1)
            weights.small_transposes(pe)
            weights.tensor(pe)
            pe.wait_ge(lst_ready, 2)
            for j in range(2):
                mm = nc.tensor.transpose(ps_l[:, j * TOKEN_TILES:(j + 1) * TOKEN_TILES], lst_f[:, j],
                                         k.ident[0:TOKEN_TILES, 0:TOKEN_TILES])
            mm.then_inc(lst_t, 1)

        @block.sync
        def _(sp):
            sp.wait_ge(empty_set, 1)
            sp.dma_start(slot_list.rearrange("(t p) o -> t (p o)", p=P), empty[:].rearrange("t p o -> t (p o)")).then_inc(zeroed, 16)
            sp.wait_ge(zeroed, 16)
            weights.sync(sp)
            for q in range(2):
                for i in range(2 * U):
                    sp.wait_ge(put[q][i], 16 * ((TURNS + 1 - q) // 2))
            sp.dma_start(lst[:].rearrange("t p o -> t (p o)"), slot_list.rearrange("(t p) o -> t (p o)", p=P)).then_inc(list_in, 16)
            sp.wait_ge(list_in, 16)

        @block.gpsimd
        def _(pool):
            pool.wait_ge(zeroed, 16)
            pool.wait_ge(slots_ready, 1)

            def turn(n, q, uses, first):
                if not first:
                    for i in range(2 * U):
                        pool.wait_ge(put[q][i], 16 * (uses - 1))
                nc.gpsimd.tensor_copy(stage[:, q], k.slot[:, :, bass.ds(n * U, U)]).then_inc(staged, 1)
                for c in range(2):
                    nc.gpsimd.tensor_copy(stage_row[:, q, c, :, 0], k.token_id[:, bass.ds(n * U, U)]).then_inc(staged, 1)
                nc.gpsimd.tensor_copy(stage_row[:, q, :, :, 1].bitcast(fp32), k.gate[:, :, bass.ds(n * U, U)]).then_inc(staged, 1)
                pool.wait_ge(staged, n * 4 + 4)
                hold_waits(k, nc.gpsimd)
                for c in range(2):
                    for u in range(U):
                        pool.indirect_dma_start(
                            out=slot_list, out_offset=bass.IndirectOffsetOnAxis(ap=stage[:, q, c, u:u + 1], axis=0),
                            in_=stage_row[:, q, c, u, :], in_offset=None).then_inc(put[q][c * U + u], 16)
            in_pairs(nc.gpsimd, TURNS, turn)
            for q in range(2):
                for i in range(2 * U):
                    pool.wait_ge(put[q][i], 16 * ((TURNS + 1 - q) // 2))


def build_experts(k):
    nc = k.nc
    SPLITS = ((0, 0), (0, 1), (1, 0))
    HBANKS = HB * PAIR // BANK
    PER_BANK = HB // HBANKS
    YR = 4
    with ExitStack() as st:
        sb, pb, sem = local(nc, st)
        stage = sb("f_stage", [P, 2 * M], i32)
        to = sb("f_to", [P, 2 * M], i32)
        xg = sb("f_xg", [P, 2 * M, D], fp32)
        xt = sb("f_xt", [P, 2, 2, KF, PAIR], fp16)
        h32 = sb("f_h32", [P, HB, PAIR], fp32)
        hh = sb("f_hh", [P, 2, 2, HB, PAIR], fp16)
        y = sb("f_y", [P, YR, D], fp32)
        weighted = sb("f_weighted", [P, YR, D], fp32)
        ps_x = [pb(f"fp_x{s}", [P, D], fp32) for s in range(2)]
        ps_h = [pb(f"fp_h{b}", [P, BANK], fp32) for b in range(HBANKS)]
        ps_y = [pb(f"fp_y{s}", [P, D], fp32) for s in range(2)]
        got = [sem(f"f_got{i}") for i in range(2 * M)]
        staged, to_staged, x_t, x_hi, x_lo, up, act_done, h_hi, h_lo, down, y_done, y_ready, added = (
            sem("f_" + x) for x in ("staged", "to", "x_t", "x_hi", "x_lo", "up", "act", "h_hi", "h_lo", "down",
                                    "y_done", "y_ready", "added"))
        block = st.enter_context(nc.Block())

        def experts(eng, regs, n):
            eng.load(regs, k.pair_expert[0:1, bass.ds(n * M, M + 1)])
            return [eng.snap(r, min_val=0, max_val=EXPERTS - 1) for r in regs]

        def every(eng, turn):
            turn(0, True, False)
            with eng.Fori(1, PAIR_TURNS - 1) as n:
                turn(n, False, False)
            turn(PAIR_TURNS - 1, False, True)

        def tile(n, m, s):
            return n * (2 * M) + (2 * m + s)

        def done(n, m, s, ago=0):
            return n * (2 * M) + (2 * (m - ago) + s + 1)

        def bank_done(n, m, b, ago=0):
            return n * (HBANKS * M) + (HBANKS * (m - ago) + b + 1)

        @block.gpsimd
        def _(pool):
            def stage_tokens(n):
                nc.gpsimd.tensor_copy(stage[:], k.slot_token[:, bass.ds(n * (2 * M), 2 * M)]).then_inc(staged, 1)
                pool.wait_ge(staged, n + 1)

            def gathers(m):
                for i in (2 * m, 2 * m + 1):
                    pool.indirect_dma_start(
                        out=xg[:, i, :], out_offset=None, in_=k.xn_rows,
                        in_offset=bass.IndirectOffsetOnAxis(ap=stage[:, i:i + 1], axis=0)).then_inc(got[i], 16)

            def additions(n, m, begun):
                for s in range(2):
                    i = (2 * m + s) % (2 * M)
                    pool.wait_ge(y_ready, done(n, m, s))
                    if begun or s:
                        pool.wait_ge(added, n * (32 * M) + 16 * (2 * m + s))
                    hold_waits(k, nc.gpsimd, 1 + M + i)
                    pool.indirect_dma_start(
                        out=k.io["out"], out_offset=bass.IndirectOffsetOnAxis(ap=to[:, i:i + 1], axis=0),
                        in_=weighted[:, i % YR, :], in_offset=None, compute_op=ALU.add).then_inc(added, 16)

            def turn(n, first, last):
                if not last:
                    for i in range(2 * M):
                        pool.wait_ge(got[i], n * 16 + 16)
                    hold_waits(k, nc.gpsimd, 0)
                    stage_tokens(n + 1)
                for m in range(M):
                    if not last:
                        pool.wait_ge(x_t, done(n, m, 1))
                        hold_waits(k, nc.gpsimd, 1 + m)
                        gathers(m)
                    if not (first and m == 0):
                        additions(n, m - 1, not (first and m == 1))
                    if m == 0:
                        if not first:
                            pool.wait_ge(added, n * (32 * M))
                            hold_waits(k, nc.gpsimd, 1 + 3 * M)
                        nc.gpsimd.tensor_copy(to[:], k.slot_token[:, bass.ds(n * (2 * M), 2 * M)]).then_inc(to_staged, 1)
                        pool.wait_ge(to_staged, n + 1)
                        hold_waits(k, nc.gpsimd, 2 + 3 * M)
            stage_tokens(0)
            for m in range(M):
                gathers(m)
            every(nc.gpsimd, turn)
            additions(PAIR_TURNS - 1, M - 1, True)
            pool.wait_ge(added, 16 * TOKEN_TILES)

        @block.tensor
        def _(pe):
            regs = [nc.tensor.alloc_register(f"f_pe{m}") for m in range(M + 1)]

            def transposes(n, m, begun):
                for s in range(2):
                    i = (2 * m + s) % (2 * M)
                    pe.wait_ge(got[i], n * 16 + (32 if m == M else 16))
                    if begun:
                        pe.wait_ge(x_hi, done(n, m, s, 1))
                        pe.wait_ge(x_lo, done(n, m, s, 1))
                    for c in range(KF):
                        mm = nc.tensor.transpose(ps_x[s][:, c * P:(c + 1) * P], xg[:, i, c * P:(c + 1) * P], k.ident[:])
                    mm.then_inc(x_t, 1)

            def first_product(n, m, ex, begun):
                q = m % 2
                pe.wait_ge(x_hi, done(n, m, 1))
                pe.wait_ge(x_lo, done(n, m, 1))
                for b in range(HBANKS):
                    if begun:
                        pe.wait_ge(act_done, bank_done(n, m, b, 1))
                    for j in range(PER_BANK):
                        h, i = b * PER_BANK + j, 0
                        for wh, xh in SPLITS:
                            for c in range(KF):
                                w = k.w1[:, bass.ds(ex, 1), wh, c, h * P:(h + 1) * P][:, 0, :]
                                mm = nc.tensor.matmul(ps_h[b][:, j * PAIR:(j + 1) * PAIR], w, xt[:, q, xh, c, :],
                                                      start=i == 0, stop=i == 5)
                                i += 1
                    mm.then_inc(up, 1)

            def second_product(n, m, ex, begun):
                q = m % 2
                for s in range(2):
                    if begun:
                        pe.wait_ge(y_done, done(n, m, s, 1))
                    i = 0
                    for b in range(HBANKS):
                        if s == 0:
                            pe.wait_ge(h_hi, bank_done(n, m, b))
                            pe.wait_ge(h_lo, bank_done(n, m, b))
                        for h in range(b * PER_BANK, (b + 1) * PER_BANK):
                            for wh, xh in SPLITS:
                                w = k.w2[:, bass.ds(ex, 1), wh, h, :][:, 0, :]
                                mm = nc.tensor.matmul(ps_y[s][:], hh[:, q, xh, h, s * P:(s + 1) * P], w,
                                                      start=i == 0, stop=i == 3 * HB - 1)
                                i += 1
                    mm.then_inc(down, 1)

            def turn(n, first, last):
                ex = experts(nc.tensor, regs, n)
                if first:
                    transposes(0, 0, False)
                for m in range(M):
                    if not (last and m == M - 1):
                        transposes(n, m + 1, True)
                    first_product(n, m, ex[m + 1], not (first and m == 0))
                    if not (first and m == 0):
                        second_product(n, m - 1, ex[m], not (first and m == 1))
                if last:
                    second_product(n, M - 1, ex[M], True)
            every(nc.tensor, turn)

        @block.scalar
        def _(act):
            regs = [nc.scalar.alloc_register(f"f_act{m}") for m in range(M + 1)]

            def high_half(n, m, begun):
                q = m % 2
                for s in range(2):
                    act.wait_ge(x_t, done(n, m, s))
                    if begun:
                        act.wait_ge(up, bank_done(n, m, HBANKS - 1, 2))
                    nc.scalar.activation(xt[:, q, 0, :, s * P:(s + 1) * P], ps_x[s][:].rearrange("p (c n) -> p c n", c=KF),
                                         ACT.Copy).then_inc(x_hi, 1)

            def turn(n, first, last):
                ex = experts(nc.scalar, regs, n)
                if first:
                    high_half(0, 0, False)
                for m in range(M):
                    if not (last and m == M - 1):
                        high_half(n, m + 1, not (first and m == 0))
                    for b in range(HBANKS):
                        act.wait_ge(up, bank_done(n, m, b))
                        if not (first and m == 0):
                            act.wait_ge(h_hi, bank_done(n, m, b, 1))
                            act.wait_ge(h_lo, bank_done(n, m, b, 1))
                        for j in range(PER_BANK):
                            h = b * PER_BANK + j
                            g = nc.scalar.activation(h32[:, h, :], ps_h[b][:, j * PAIR:(j + 1) * PAIR], ACT.Gelu,
                                                     bias=k.b1[:, bass.ds(ex[m + 1] * HB + h, 1)], scale=1.0 / SCALE)
                        g.then_inc(act_done, 1)
            every(nc.scalar, turn)

        @block.vector
        def _(dve):
            regs = [nc.vector.alloc_register(f"f_dve{m}") for m in range(M + 1)]

            def low_half(n, m):
                q = m % 2
                for s in range(2):
                    dve.wait_ge(x_hi, done(n, m, s))
                    part = slice(s * P, (s + 1) * P)
                    nc.vector.tensor_tensor(xt[:, q, 1, :, part], ps_x[s][:].rearrange("p (c n) -> p c n", c=KF),
                                            xt[:, q, 0, :, part], ALU.subtract).then_inc(x_lo, 1)

            def result(n, m, ex, begun):
                for s in range(2):
                    r = (2 * m + s) % YR
                    dve.wait_ge(down, done(n, m, s))
                    if begun:
                        dve.wait_ge(added, n * (32 * M) + 16 * (2 * m + s + 1 - YR))
                    nc.vector.scalar_tensor_tensor(y[:, r, :], ps_y[s][:], 1.0 / SCALE,
                                                   k.b2[:, bass.ds(ex, 1), :][:, 0, :], ALU.mult,
                                                   ALU.add).then_inc(y_done, 1)
                    dve.wait_ge(y_done, done(n, m, s))
                    nc.vector.tensor_scalar(weighted[:, r, :], y[:, r, :], k.slot_gate[:, bass.ds(tile(n, m, s), 1)],
                                            None, ALU.mult).then_inc(y_ready, 1)

            def turn(n, first, last):
                ex = experts(nc.vector, regs, n)
                if first:
                    low_half(0, 0)
                for m in range(M):
                    q = m % 2
                    if not (last and m == M - 1):
                        low_half(n, m + 1)
                    if not (first and m < 2):
                        dve.wait_ge(down, done(n, m, 1, 2))
                    for b in range(HBANKS):
                        part = slice(b * PER_BANK, (b + 1) * PER_BANK)
                        dve.wait_ge(act_done, bank_done(n, m, b))
                        nc.vector.tensor_copy(hh[:, q, 0, part], h32[:, part]).then_inc(h_hi, 1)
                        dve.wait_ge(h_hi, bank_done(n, m, b))
                        nc.vector.tensor_tensor(hh[:, q, 1, part], h32[:, part], hh[:, q, 0, part],
                                                ALU.subtract).then_inc(h_lo, 1)
                    if not (first and m == 0):
                        result(n, m - 1, ex[m], not (first and m < 3))
                if last:
                    result(n, M - 1, ex[M], True)
            every(nc.vector, turn)


def build(nc, io):
    with ExitStack() as ctx:
        k = Kernel(nc, ctx, io)
        build_constants(k)
        with ExitStack() as gst:
            build_edge_tables(k, gst)
            k.rows = [gst.enter_context(nc.sbuf_tensor(f"rows{i}", [P, BLOCKS, 2 * D], fp16)) for i in range(2)]
            k.z = k.rows[1][:].bitcast(fp32)
            build_input_rows(k)
            build_adjacency_and_sums(k)
            build_second_rows(k)
            build_layer_two(k)
        with ExitStack() as kst:
            build_routing(k, kst)
            build_experts(k)


_INS = ["x", "src", "dst", "L0_gnn_W1", "L0_gnn_b1", "L0_gnn_W2", "L0_gnn_b2", "L0_ffn_Wr", "L0_ffn_br",
        "L0_ffn_ln_g", "L0_ffn_ln_b", "L0_ffn_W1", "L0_ffn_b1", "L0_ffn_W2", "L0_ffn_b2"]


def kernel(**inputs):
    import numpy as _np
    import concourse.bacc as _bacc
    from concourse import mybir as _mybir
    from concourse.bass_utils import run_bass_kernel_spmd as _run

    arrays = {n: _np.ascontiguousarray(inputs[n]) for n in _INS}
    arrays["x"] = _np.concatenate([arrays["x"], _np.zeros((PAD_NODES - NODES, D), arrays["x"].dtype)])
    pad = EDGE_TILES * P - EDGES
    arrays["src"] = _np.concatenate([arrays["src"], _np.zeros(pad, arrays["src"].dtype)])
    arrays["dst"] = _np.concatenate([arrays["dst"], _np.full(pad, PAD_NODES, arrays["dst"].dtype)])
    nc = _bacc.Bacc("TRN2", target_bir_lowering=False, num_devices=1)
    io, ins = {}, {}
    for n, a in arrays.items():
        ins[f"in_{n}_dram"] = a
        io[n] = nc.dram_tensor(f"in_{n}_dram", a.shape, _mybir.dt.from_np(a.dtype), kind="ExternalInput").ap()
    io["out"] = nc.dram_tensor("out_0_dram", (ROWS, D), _mybir.dt.float32, kind="ExternalOutput").ap()
    build(nc, io)
    r = _run(nc, [ins], core_ids=[0])
    return r.results[0]["out_0_dram"][:NODES]
```
